# Optimizing a Trainium2 kernel written in Bass

```python
import numpy as np
import jax
import jax.numpy as jnp

def _softmax(x, axis=-1):
    return jax.nn.softmax(x, axis=axis)
def _gelu(x):
    return jax.nn.gelu(x, approximate=True)
def _silu(x):
    return jax.nn.silu(x)
def _sigmoid(x):
    return jax.nn.sigmoid(x)
def _layernorm(x, axis=-1, eps=1e-5):
    m = jnp.mean(x, axis=axis, keepdims=True)
    v = jnp.var(x, axis=axis, keepdims=True)
    return (x - m) / jnp.sqrt(v + eps)
def _scatter_add(tgt, idx, src, axis=0):
    return tgt.at[idx].add(src)
def _segment_sum(src, seg, n):
    return jax.ops.segment_sum(src, seg, n)

kernel_name = 'mk_vit_tower_d1_tok_img256_03ee64'

def setup_inputs(seed: int = 0):
    np.random.seed(seed)
    _w = jnp.asarray
    def _rec_inputs():
        import jax
        import jax.numpy as jnp
        _rk = jax.random.key(seed)
        x = (-0.000209053 + 0.999977 * jax.random.normal(jax.random.fold_in(_rk, 1), (4, 256, 56, 56), jnp.float32))
        return x
    x = _rec_inputs()
    def _L0_tok_setup():
        import jax, jax.numpy as jnp
        import numpy as np
        B, EMB, HT, WD = (32, 256, 56, 56)
        NH, WS, SHIFTED = (8, 4, True)

        def _rel_indices(ws):
            coords = np.array([[i, j] for i in range(ws) for j in range(ws)])
            rel = coords[None, :, :] - coords[:, None, :] + ws - 1
            return jnp.asarray(rel)

        def _shift_masks(ws):
            m = np.zeros((ws * ws, ws * ws), np.float32)
            s = ws * (ws // 2)
            m[-s:, :-s] = -np.inf
            m[:-s, -s:] = -np.inf
            col = m.reshape(ws, ws, ws, ws).transpose(1, 0, 3, 2).reshape(ws * ws, ws * ws)
            return (jnp.asarray(m), jnp.asarray(col))
        key = jax.random.key(seed)
        ks = jax.random.split(key, 6)
        x = jax.random.normal(ks[0], (B, EMB, HT, WD), jnp.float32)
        s = 1.0 / np.sqrt(EMB)
        w1 = jax.random.uniform(ks[1], (3 * EMB, EMB), jnp.float32, -s, s)
        b1 = jax.random.uniform(ks[2], (3 * EMB,), jnp.float32, -s, s)
        w2 = jax.random.uniform(ks[3], (EMB, EMB), jnp.float32, -s, s)
        b2 = jax.random.uniform(ks[4], (EMB,), jnp.float32, -s, s)
        pos_emb = jax.random.normal(ks[5], (2 * WS - 1, 2 * WS - 1), jnp.float32)
        return {'x': x, 'w1': w1, 'b1': b1, 'w2': w2, 'b2': b2, 'pos_emb': pos_emb}
    _L0_tok_all = _L0_tok_setup()
    _L0_tok_in = {k: v for k, v in _L0_tok_all.items() if k in ('w1', 'b1', 'w2', 'b2', 'pos_emb', )}
    del _L0_tok_all

    def _L0_attn_setup():
        import jax, jax.numpy as jnp
        import numpy as np
        B, N, C, H = (4096, 64, 256, 8)
        key = jax.random.key(seed)
        ks = jax.random.split(key, 6)
        return {'x': jax.random.normal(ks[0], (B, N, C), dtype=jnp.float32), 'qkv_w': jax.random.normal(ks[1], (C, 3 * C), dtype=jnp.float32) * 0.02, 'qkv_b': jax.random.normal(ks[2], (3 * C,), dtype=jnp.float32) * 0.02, 'proj_w': jax.random.normal(ks[3], (C, C), dtype=jnp.float32) * 0.02, 'proj_b': jax.random.normal(ks[4], (C,), dtype=jnp.float32) * 0.02, 'rpb_table': jax.random.normal(ks[5], (2 * N - 1, H), dtype=jnp.float32) * 0.02}
    _L0_attn_all = _L0_attn_setup()
    _L0_attn_in = {k: v for k, v in _L0_attn_all.items() if k in ('qkv_w', 'qkv_b', 'proj_w', 'proj_b', 'rpb_table', )}
    del _L0_attn_all

    def _L0_ffn_setup():
        import jax, jax.numpy as jnp
        import numpy as np
        B, S, D = (8, 4096, 256)
        H = 4 * D
        CAPACITY = 0.5
        key = jax.random.key(seed)
        ks = jax.random.split(key, 6)
        x = jax.random.normal(ks[0], (B, S, D), dtype=jnp.float32)
        attention_mask = jnp.zeros((B, 1, 1, S), dtype=jnp.float32)
        wr = jax.random.normal(ks[1], (D, 1), dtype=jnp.float32) * 0.02
        br = jnp.zeros((1,), dtype=jnp.float32)
        w1 = jax.random.normal(ks[2], (D, H), dtype=jnp.float32) * 0.02
        b1 = jnp.zeros((H,), dtype=jnp.float32)
        w2 = jax.random.normal(ks[3], (H, D), dtype=jnp.float32) * 0.02
        b2 = jnp.zeros((D,), dtype=jnp.float32)
        return {'x': x, 'attention_mask': attention_mask, 'wr': wr, 'br': br, 'w1': w1, 'b1': b1, 'w2': w2, 'b2': b2}
    _L0_ffn_all = _L0_ffn_setup()
    _L0_ffn_in = {k: v for k, v in _L0_ffn_all.items() if k in ('attention_mask', 'wr', 'br', 'w1', 'b1', 'w2', 'b2', )}
    del _L0_ffn_all

    return {
        "x": x,
        "L0_tok_w1": _L0_tok_in["w1"],
        "L0_tok_b1": _L0_tok_in["b1"],
        "L0_tok_w2": _L0_tok_in["w2"],
        "L0_tok_b2": _L0_tok_in["b2"],
        "L0_tok_pos_emb": _L0_tok_in["pos_emb"],
        "L0_attn_qkv_w": _L0_attn_in["qkv_w"],
        "L0_attn_qkv_b": _L0_attn_in["qkv_b"],
        "L0_attn_proj_w": _L0_attn_in["proj_w"],
        "L0_attn_proj_b": _L0_attn_in["proj_b"],
        "L0_attn_rpb_table": _L0_attn_in["rpb_table"],
        "L0_ffn_attention_mask": _L0_ffn_in["attention_mask"],
        "L0_ffn_wr": _L0_ffn_in["wr"],
        "L0_ffn_br": _L0_ffn_in["br"],
        "L0_ffn_w1": _L0_ffn_in["w1"],
        "L0_ffn_b1": _L0_ffn_in["b1"],
        "L0_ffn_w2": _L0_ffn_in["w2"],
        "L0_ffn_b2": _L0_ffn_in["b2"],
    }

def reference(x, L0_tok_w1, L0_tok_b1, L0_tok_w2, L0_tok_b2, L0_tok_pos_emb, L0_attn_qkv_w, L0_attn_qkv_b, L0_attn_proj_w, L0_attn_proj_b, L0_attn_rpb_table, L0_ffn_attention_mask, L0_ffn_wr, L0_ffn_br, L0_ffn_w1, L0_ffn_b1, L0_ffn_w2, L0_ffn_b2):
    import jax
    import jax.numpy as jnp
    def _L0_tok_ref(x, w1, b1, w2, b2, pos_emb):
        import jax, jax.numpy as jnp
        import numpy as np
        B, EMB, HT, WD = (32, 256, 56, 56)
        NH, WS, SHIFTED = (8, 4, True)

        def _rel_indices(ws):
            coords = np.array([[i, j] for i in range(ws) for j in range(ws)])
            rel = coords[None, :, :] - coords[:, None, :] + ws - 1
            return jnp.asarray(rel)

        def _shift_masks(ws):
            m = np.zeros((ws * ws, ws * ws), np.float32)
            s = ws * (ws // 2)
            m[-s:, :-s] = -np.inf
            m[:-s, -s:] = -np.inf
            col = m.reshape(ws, ws, ws, ws).transpose(1, 0, 3, 2).reshape(ws * ws, ws * ws)
            return (jnp.asarray(m), jnp.asarray(col))
        b, c, ht, wd = x.shape
        ws, nh = (WS, NH)
        e = c // nh
        xt = x.reshape(b, c, ht * wd).transpose(0, 2, 1)
        qkv = xt @ w1.T + b1
        qkv = qkv.reshape(b, ht, wd, c, 3)
        if SHIFTED:
            qkv = jnp.roll(qkv, (-ws // 2, -ws // 2), axis=(1, 2))
        Wh, Ww = (ht // ws, wd // ws)
        qkv = qkv.reshape(b, Wh, ws, Ww, ws, e, nh, 3)
        qkv = qkv.transpose(0, 6, 1, 3, 2, 4, 5, 7).reshape(b, nh, Wh, Ww, ws * ws, e, 3)
        Q, K, V = (qkv[..., 0], qkv[..., 1], qkv[..., 2])
        scale = jnp.sqrt(jnp.float32(c / nh))
        wei = jnp.einsum('bhijpe,bhijqe->bhijpq', Q, K) / scale
        rel = _rel_indices(ws)
        wei = wei + pos_emb[rel[..., 0], rel[..., 1]]
        if SHIFTED:
            row_mask, col_mask = _shift_masks(ws)
            wei = wei.at[:, :, -1, :].add(row_mask)
            wei = wei.at[:, :, :, -1].add(col_mask)
        attn = jax.nn.softmax(wei, axis=-1)
        out = jnp.einsum('bhijpq,bhijqe->bhijpe', attn, V)
        out = out.reshape(b, nh, Wh, Ww, ws, ws, e)
        out = out.transpose(0, 2, 4, 3, 5, 1, 6).reshape(b, ht, wd, nh * e)
        out = out.reshape(b, ht * wd, c)
        return out @ w2.T + b2

    def _L0_attn_ref(x, qkv_w, qkv_b, proj_w, proj_b, rpb_table):
        import jax, jax.numpy as jnp
        import numpy as np
        B, N, C, H = (4096, 64, 256, 8)
        Bw, Nw, Cd = x.shape
        nh = rpb_table.shape[1]
        dh = Cd // nh
        scale = dh ** (-0.5)
        qkv = (x @ qkv_w + qkv_b).reshape(Bw, Nw, 3, nh, dh)
        q, k, v = (qkv[:, :, 0], qkv[:, :, 1], qkv[:, :, 2])
        attn = jnp.einsum('bnhd,bmhd->bhnm', q * scale, k)
        coords = jnp.arange(Nw)
        rel_idx = coords[:, None] - coords[None, :] + (Nw - 1)
        bias = jnp.transpose(rpb_table[rel_idx], (2, 0, 1))
        attn = jax.nn.softmax(attn + bias[None], axis=-1)
        out = jnp.einsum('bhnm,bmhd->bnhd', attn, v).reshape(Bw, Nw, Cd)
        return out @ proj_w + proj_b

    def _L0_ffn_ref(x, attention_mask, wr, br, w1, b1, w2, b2):
        import jax, jax.numpy as jnp
        import numpy as np
        B, S, D = (8, 4096, 256)
        H = 4 * D
        CAPACITY = 0.5
        b, s, d = x.shape
        weights = (jnp.einsum('bsd,do->bso', x, wr) + br)[..., 0]
        k = max(1, int(CAPACITY * s))
        kk = k - 1 if k > 1 else 1
        _, idx = jax.lax.top_k(weights, k)
        sel_idx = idx[:, :kk]
        sel = jnp.take_along_axis(x, sel_idx[:, :, None], axis=1)
        h = jax.nn.gelu(jnp.einsum('bkd,dh->bkh', sel, w1) + b1)
        y = jnp.einsum('bkh,hd->bkd', h, w2) + b2
        w_sel = jnp.take_along_axis(weights, sel_idx, axis=1)
        y = y * w_sel[..., None]
        batch_idx = jnp.arange(b)[:, None]
        processed = jnp.zeros_like(x).at[batch_idx, sel_idx].set(y)
        return processed + x

    h = _L0_tok_ref(x, L0_tok_w1, L0_tok_b1, L0_tok_w2, L0_tok_b2, L0_tok_pos_emb)
    h = h + _L0_attn_ref(_layernorm(h, axis=-1), L0_attn_qkv_w, L0_attn_qkv_b, L0_attn_proj_w, L0_attn_proj_b, L0_attn_rpb_table)
    h = h + _L0_ffn_ref(_layernorm(h, axis=-1), L0_ffn_attention_mask, L0_ffn_wr, L0_ffn_br, L0_ffn_w1, L0_ffn_b1, L0_ffn_w2, L0_ffn_b2)
    return h


_drawn_inputs = setup_inputs


def setup_inputs(seed=0):
    import zlib

    import numpy as np

    out = dict(_drawn_inputs(seed))
    spreads = {'L0_ffn_b1': (0.0, 0.8), 'L0_ffn_b2': (0.0, 0.341)}
    factors = {'L0_attn_rpb_table': 200.0}
    for name, (base, spread) in spreads.items():
        noise = np.random.default_rng([zlib.crc32(name.encode()), seed]).standard_normal(out[name].shape)
        drawn = base * np.exp(spread * noise) if base else spread * noise
        out[name] = jnp.asarray(drawn.astype(out[name].dtype))
    for name, factor in factors.items():
        out[name] = (out[name] * factor).astype(out[name].dtype)
    return out
```

```python
from contextlib import ExitStack

import concourse.bass as bass
from concourse import mybir

ALU = mybir.AluOpType
ACT = mybir.ActivationFunctionType
AX = mybir.AxisListType
F32 = mybir.dt.float32
F32R = mybir.dt.float32r

B = 4
C = 256
CT = C // 128
SIDE = 56
N = SIDE * SIDE
NH = 8
DH = C // NH
WS = 4
GROUP = SIDE // 2 * WS
UNIT = 2 * GROUP
UNITS = B * N // UNIT
HALFROW = SIDE // 2
CH = 448
CHUNKS = B * N // CH
PER_IMAGE = N // CH
QT = 112
NQ = CH // QT
G = 2
HG = NH // G
FIRST = 64
KT = 1 + (N - FIRST) // 128
SLOTS = 5
STACK = 3 * DH
HID = 4 * C
HT = HID // 128
KEEP = max(1, N // 2) - 1
REL = 127
NEG = -1.0e30
EPS = 1e-5


def view(dram, offset, dims):
    return bass.AP(dram.tensor, offset, dims)


def setup_tables(nc, d):
    with ExitStack() as ctx:
        sb = lambda n, s, t=F32: ctx.enter_context(nc.sbuf_tensor(n, s, t))
        sem = lambda n: ctx.enter_context(nc.semaphore(n))
        neg = sb("neg", [GROUP, 4, GROUP])
        rel = sb("rel", [NH, REL])
        edge = sb("edge", [NH, 255])
        corner = sb("corner", [128, NH, 128])
        corner_hi = sb("corner_hi", [128, NH, 128], F32R)
        corner_lo = sb("corner_lo", [128, NH, 128], F32R)
        zero = sb("zero", [128, 2, HG, 128])
        zero_set, zero_out = sem("zero_set"), sem("zero_out")
        neg_set, filled, placed, masked = sem("neg_set"), sem("filled"), sem("placed"), sem("masked")
        rel_in, edge_zero, edge_set, skewed, corner_in = (
            sem("rel_in"), sem("edge_zero"), sem("edge_set"), sem("skewed"), sem("corner_in"))
        hi_set, lo_set, corner_out = sem("hi_set"), sem("lo_set"), sem("corner_out")
        block = ctx.enter_context(nc.Block())

        def table(v, offset, dims):
            return view(d.win_bias, v * GROUP * GROUP + offset, dims)

        @block.sync
        def _(sp):
            sp.wait_ge(neg_set, 1)
            sp.dma_start(d.win_bias.rearrange("v p k -> p v k"), neg[:, :, :]).then_inc(filled, 16)
            sp.dma_start(d.negs, neg[0:28, 0, 0:28]).then_inc(filled, 16)
            sp.wait_ge(filled, 32)
            n = 0
            for v in range(4):
                for r in range(WS):
                    for p in range(WS):
                        src = view(d.pos_emb, (WS - 1 - r) * 7 + WS - 1 - p, [[0, 7], [7, WS], [1, WS]])
                        dst = table(v, (r * HALFROW + p) * GROUP,
                                    [[WS * GROUP + WS, 7], [HALFROW, WS], [1, WS]])
                        sp.dma_start(dst, src).then_inc(placed, 16)
                        n += 16
            sp.wait_ge(placed, n)
            half, m = GROUP // 2, 0
            for v in (1, 3):
                for off in (half * GROUP, half):
                    for part in (0, 28):
                        sp.dma_start(table(v, off + part * GROUP, [[GROUP, 28], [1, 28]]), d.negs).then_inc(masked, 16)
                        sp.dma_start(table(v, off + part * GROUP + 28, [[GROUP, 28], [1, 28]]),
                                     d.negs).then_inc(masked, 16)
                        m += 32
            sp.wait_ge(masked, m)
            for v in (2, 3):
                for r in range(WS):
                    for a, b in ((26, 24), (24, 26)):
                        dst = table(v, (r * HALFROW + a) * GROUP + b, [[GROUP, 2], [HALFROW, WS], [1, 2]])
                        sp.dma_start(dst, view(d.negs, 0, [[28, 2], [2, WS], [1, 2]])).then_inc(masked, 16)
                        m += 16
            sp.wait_ge(masked, m)

        @block.scalar
        def _(act):
            act.dma_start(rel[:, :], d.rpb).then_inc(rel_in, 16)
            act.wait_ge(edge_set, 1)
            act.dma_start(view(d.skew, 0, [[128 * 257, NH], [257, 128], [1, 255]]),
                          edge[:, :].unsqueeze(1).broadcast_to([NH, 128, 255])).then_inc(skewed, 16)
            act.wait_ge(skewed, 16)
            act.dma_start(corner[:, :, :], view(d.skew, 127, [[256, 128], [128 * 257, NH], [1, 128]])
                          ).then_inc(corner_in, 16)
            act.wait_ge(zero_set, 1)
            for g in range(G):
                act.dma_start(d.no_corner[g], zero[:, :, :, :]).then_inc(zero_out, 16)
            act.wait_ge(hi_set, 1)
            act.wait_ge(lo_set, 1)
            for g in range(G):
                act.dma_start(d.corner[g, :, 0], corner_hi[:, g * HG:(g + 1) * HG, :].bitcast(F32)).then_inc(corner_out, 16)
                act.dma_start(d.corner[g, :, 1], corner_lo[:, g * HG:(g + 1) * HG, :].bitcast(F32)).then_inc(corner_out, 16)
            act.wait_ge(corner_out, 16 * 2 * G)
            act.wait_ge(zero_out, 16 * G)

        @block.vector
        def _(dve):
            nc.vector.memset(neg[:, :, :], NEG).then_inc(neg_set, 1)
            nc.vector.memset(edge[:, :], 0.0).then_inc(edge_zero, 1)
            nc.vector.memset(zero[:, :, :, :], 0.0).then_inc(zero_set, 1)
            dve.wait_ge(rel_in, 16)
            dve.wait_ge(edge_zero, 1)
            nc.vector.tensor_scalar(edge[:, 0:REL], rel[:, :], rel[:, REL - 1:REL], None,
                                    ALU.subtract).then_inc(edge_set, 1)
            dve.wait_ge(corner_in, 16)
            nc.vector.tensor_copy(corner_hi[:, :, :], corner[:, :, :]).then_inc(hi_set, 1)
            dve.wait_ge(hi_set, 1)
            nc.vector.tensor_tensor(corner_lo[:, :, :], corner[:, :, :], corner_hi[:, :, :].bitcast(F32),
                                    ALU.subtract).then_inc(lo_set, 1)


def window_attention(nc, d):
    with ExitStack() as ctx:
        sb = lambda n, s, t=F32: ctx.enter_context(nc.sbuf_tensor(n, s, t))
        ps = lambda n, s: ctx.enter_context(nc.psum_tensor(n, s, F32))
        sem = lambda n: ctx.enter_context(nc.semaphore(n))
        w = sb("w_qkv", [128, CT, 3 * C])
        bias_col = sb("bias_col", [128, 2 * CT])
        bias_v = sb("bias_v", [GROUP, C])
        ident = sb("ident", [128, 128])
        ones = sb("ones", [GROUP, DH])
        tab = sb("tab", [GROUP, 2, CT, GROUP])
        tab_odd = sb("tab_odd", [GROUP, 2, CT, GROUP])
        xT = [sb(f"xT{i}", [128, CT, UNIT]) for i in range(2)]
        qk = [sb(f"qk{i}", [128, 2 * CT, UNIT]) for i in range(2)]
        v = [sb(f"v{i}", [GROUP, 2, C]) for i in range(2)]
        logit = [sb(f"logit{i}", [GROUP, NH, GROUP]) for i in range(2)]
        prob = [sb(f"prob{i}", [GROUP, NH, GROUP]) for i in range(2)]
        probT = [sb(f"probT{i}", [GROUP, NH, GROUP]) for i in range(2)]
        top = [sb(f"top{i}", [GROUP, NH]) for i in range(2)]
        rden = sb("rden", [128, CT, GROUP])
        oT = [sb(f"oT{i}", [128, CT, UNIT]) for i in range(2)]
        ps_s = ps("ps_s", [GROUP, 4, 512])
        ps_t = ps("ps_t", [128, 2, 512])
        ps_q = ps("ps_q", [128, 2, 512])

        consts_in, id_zero, id_set, ones_set, odd_in = (
            sem("consts_in"), sem("id_zero"), sem("id_set"), sem("ones_set"), sem("odd_in"))
        x_in, qkv_ready = [sem(f"x_in{u}") for u in range(2)], sem("qkv_ready")
        qk_kept, v_kept = sem("qk_kept"), sem("v_kept")
        s_ready, logit_ready, top_ready, shifted, prob_ready = (
            sem("s_ready"), sem("logit_ready"), sem("top_ready"), sem("shifted"), sem("prob_ready"))
        t_ready, t_kept, o_ready, recip_ready, o_kept, o_out = (
            sem("t_ready"), sem("t_kept"), sem("o_ready"), sem("recip_ready"), sem("o_kept"),
            [sem(f"o_out{u}") for u in range(2)])
        block = ctx.enter_context(nc.Block())
        JOBS = 2 * CT + 2
        SCALE = 1.0 / float(DH) ** 0.5

        @block.sync
        def _(sp):
            sp.dma_start(w[:, :, :], d.w_tok.rearrange("(t p) n -> p t n", p=128)).then_inc(consts_in, 16)
            sp.dma_start(bias_col[:, :], d.b_tok[0:2 * C].rearrange("(t p) -> p t", p=128),
                         allow_slow_non_contiguous=True).then_inc(consts_in, 16)
            sp.dma_start(bias_v[:, :], view(d.b_tok, 2 * C, [[0, GROUP], [1, C]])).then_inc(consts_in, 16)
            for half in range(2):
                for c in range(CT):
                    sp.dma_start(tab[:, half, c, :], d.win_bias[2 * half]).then_inc(consts_in, 16)
            for u in range(2):
                sp.dma_start(xT[u][:, :, :], d.x[u]).then_inc(x_in[u], 16)

            def pair(m, last_row):
                sp.wait_ge(logit_ready, 4 * m)
                for half in range(2):
                    for c in range(CT):
                        sp.dma_start(tab_odd[:, half, c, :], d.win_bias[2 * half + last_row]).then_inc(odd_in, 16)

            def store(m, u):
                sp.wait_ge(o_kept, 4 * m + 2 * u + 2)
                sp.dma_start(d.a1[2 * m + u], oT[u][:, :, :]).then_inc(o_out[u], 16)

            def load(m, u):
                sp.wait_ge(qkv_ready, JOBS * (2 * m + u + 1))
                sp.dma_start(xT[u][:, :, :], d.x[2 * m + u + 2]).then_inc(x_in[u], 16)

            def body(m, last_row, more):
                pair(m, last_row)
                if more:
                    load(m, 0)
                    load(m, 1)
                store(m, 0)
                store(m, 1)

            rows = UNITS // B // 2
            with sp.Fori(0, B - 1) as b:
                with sp.Fori(0, rows - 1) as r:
                    body(b * rows + r, 0, True)
                body(b * rows + rows - 1, 1, True)
            with sp.Fori(0, rows - 1) as r:
                body((B - 1) * rows + r, 0, True)
            body(B * rows - 1, 1, False)
            for u in range(2):
                sp.wait_ge(o_out[u], 8 * UNITS)

        @block.gpsimd
        def _(pool):
            nc.gpsimd.memset(ident[:, :], 0.0).then_inc(id_zero, 1)
            pool.wait_ge(id_zero, 1)
            nc.gpsimd.affine_select(out=ident[:, :], in_=ident[:, :], compare_op=ALU.not_equal, fill=1.0, base=0,
                                    pattern=[[-1, 128]], channel_multiplier=1).then_inc(id_set, 1)
            nc.gpsimd.memset(ones[:, :], 1.0).then_inc(ones_set, 1)

            def shift(k, p):
                pool.wait_ge(top_ready, k + 1)
                nc.gpsimd.tensor_tensor(logit[p][:, :, :], logit[p][:, :, :],
                                        top[p][:, :].unsqueeze(2).broadcast_to([GROUP, NH, GROUP]),
                                        ALU.subtract).then_inc(shifted, 1)

            with pool.Fori(0, UNITS // 2) as m:
                for k in range(4):
                    shift(4 * m + k, k % 2)

        @block.tensor
        def _(pe):
            pe.wait_ge(consts_in, 16 * (3 + 2 * CT))
            pe.wait_ge(id_set, 1)
            pe.wait_ge(ones_set, 1)

            def project(n, u):
                pe.wait_ge(x_in[u], 8 * (n - u) + 16)
                for job in range(2 * CT):
                    if job < 2:
                        pe.wait_ge(v_kept, 2 * n)
                    else:
                        pe.wait_ge(qk_kept, 2 * CT * n + job - 1)
                    for c in range(CT):
                        mm = nc.tensor.matmul(ps_q[:, job % 2, 0:UNIT], w[:, c, job * 128:(job + 1) * 128],
                                              xT[u][:, c, :], start=(c == 0), stop=(c == CT - 1))
                    mm.then_inc(qkv_ready, 1)
                for half in range(2):
                    pe.wait_ge(qk_kept, 2 * CT * n + 2 * CT - 1 + half)
                    for c in range(CT):
                        x = xT[u][:, c, half * GROUP:(half + 1) * GROUP]
                        mm = nc.tensor.matmul(ps_q[0:GROUP, half, 0:C], x, w[:, c, 2 * C:3 * C],
                                              start=(c == 0), stop=(c == CT - 1))
                    mm.then_inc(qkv_ready, 1)

            def scores(n, u, half):
                k = 2 * n + half
                pe.wait_ge(logit_ready, k)
                pe.wait_ge(qk_kept, 2 * CT * (n + 1))
                for c in range(CT):
                    for j in range(4):
                        rows = slice(32 * j, 32 * j + 32)
                        q = qk[u][rows, c, half * GROUP:(half + 1) * GROUP]
                        kk = qk[u][rows, CT + c, half * GROUP:(half + 1) * GROUP]
                        mm = nc.tensor.matmul(ps_s[:, j, c * GROUP:(c + 1) * GROUP], q, kk, start=True, stop=True)
                mm.then_inc(s_ready, 1)

            def weighted(n, u, half):
                k = 2 * n + half
                pe.wait_ge(prob_ready, k + 1)
                pe.wait_ge(o_kept, k)
                for h in range(NH):
                    mm = nc.tensor.transpose(ps_t[0:GROUP, h // 4, (h % 4) * GROUP:(h % 4 + 1) * GROUP],
                                             prob[half][:, h, :], ident[0:GROUP, 0:GROUP])
                mm.then_inc(t_ready, 1)
                pe.wait_ge(t_kept, k + 1)
                pe.wait_ge(v_kept, 2 * (n + 1))
                for c in range(CT):
                    for j in range(4):
                        nc.tensor.matmul(ps_t[32 * j:32 * j + 32, 0, c * GROUP:(c + 1) * GROUP],
                                         v[u][:, half, (4 * c + j) * DH:(4 * c + j + 1) * DH],
                                         probT[half][:, 2 * j + c, :], start=True, stop=True)
                for c in range(CT):
                    for j in range(4):
                        mm = nc.tensor.matmul(ps_t[32 * j:32 * j + 32, 0, (CT + c) * GROUP:(CT + c + 1) * GROUP],
                                              ones[:, :], probT[half][:, 2 * j + c, :], start=True, stop=True)
                mm.then_inc(o_ready, 1)

            def unit(n, u, more):
                scores(n, u, 1)
                if more:
                    project(n + 1, 1 - u)
                weighted(n, u, 0)
                if more:
                    scores(n + 1, 1 - u, 0)
                weighted(n, u, 1)

            project(0, 0)
            scores(0, 0, 0)
            with pe.Fori(0, UNITS // 2 - 1) as m:
                unit(2 * m, 0, True)
                unit(2 * m + 1, 1, True)
            unit(UNITS - 2, 0, True)
            unit(UNITS - 1, 1, False)

        @block.vector
        def _(dve):
            dve.wait_ge(consts_in, 16 * (3 + 2 * CT))

            def logits(n, u, half):
                k = 2 * n + half
                dve.wait_ge(s_ready, k + 1)
                if u:
                    dve.wait_ge(odd_in, 16 * CT * (n + 1))
                table = (tab_odd if u else tab)[:, half, :, :].rearrange("p c k -> p (c k)")
                table = table.unsqueeze(1).broadcast_to([GROUP, 4, CT * GROUP])
                nc.vector.scalar_tensor_tensor(
                    out=logit[half][:, :, :].rearrange("p (j c) k -> p j (c k)", j=4),
                    in0=ps_s[:, :, 0:2 * GROUP], scalar=SCALE,
                    in1=table, op0=ALU.mult, op1=ALU.add).then_inc(logit_ready, 1)
                dve.wait_ge(logit_ready, k + 1)
                nc.vector.tensor_reduce(top[half][:, :], logit[half][:, :, :], AX.X, ALU.max).then_inc(top_ready, 1)

            def keep_v(n, u):
                for half in range(2):
                    dve.wait_ge(qkv_ready, JOBS * n + 2 * CT + 1 + half)
                    nc.vector.tensor_tensor(v[u][:, half, :], ps_q[0:GROUP, half, 0:C], bias_v[:, :],
                                            ALU.add).then_inc(v_kept, 1)

            def outputs(n, u, half):
                k = 2 * n + half
                dve.wait_ge(o_ready, k + 1)
                nc.vector.reciprocal(rden[:, :, :].rearrange("p c k -> p (c k)"),
                                     ps_t[:, 0, CT * GROUP:2 * CT * GROUP]).then_inc(recip_ready, 1)
                dve.wait_ge(recip_ready, k + 1)
                if half == 0:
                    dve.wait_ge(o_out[u], 8 * (n - u))
                dst = oT[u][:, :, :].rearrange("p c (r h k) -> p c h r k", r=WS, h=2)[:, :, half]
                for c in range(CT):
                    ins = nc.vector.tensor_tensor(
                        dst[:, c], ps_t[:, 0, c * GROUP:(c + 1) * GROUP].rearrange("p (r k) -> p r k", r=WS),
                        rden[:, c, :].rearrange("p (r k) -> p r k", r=WS), ALU.mult)
                ins.then_inc(o_kept, 1)

            def unit(n, u, more):
                logits(n, u, 1)
                if more:
                    keep_v(n + 1, 1 - u)
                outputs(n, u, 0)
                if more:
                    logits(n + 1, 1 - u, 0)
                outputs(n, u, 1)

            keep_v(0, 0)
            logits(0, 0, 0)
            with dve.Fori(0, UNITS // 2 - 1) as m:
                unit(2 * m, 0, True)
                unit(2 * m + 1, 1, True)
            unit(UNITS - 2, 0, True)
            unit(UNITS - 1, 1, False)

        @block.scalar
        def _(act):
            act.wait_ge(consts_in, 16 * (3 + 2 * CT))

            def keep_qk(n, u):
                act.wait_ge(s_ready, 2 * (n - u))
                for job in range(2 * CT):
                    act.wait_ge(qkv_ready, JOBS * n + job + 1)
                    nc.scalar.activation(qk[u][:, job, :], ps_q[:, job % 2, 0:UNIT], ACT.Identity,
                                         bias=bias_col[:, job:job + 1]).then_inc(qk_kept, 1)

            def exps(n, half):
                k = 2 * n + half
                act.wait_ge(shifted, k + 1)
                nc.scalar.activation(prob[half][:, :, :], logit[half][:, :, :], ACT.Exp).then_inc(prob_ready, 1)

            def keep_t(n, half):
                k = 2 * n + half
                act.wait_ge(t_ready, k + 1)
                nc.scalar.activation(probT[half][:, :, :].rearrange("p (a h) k -> p a (h k)", a=2),
                                     ps_t[0:GROUP, :, 0:4 * GROUP], ACT.Copy).then_inc(t_kept, 1)

            def unit(n, u, more):
                if more:
                    keep_qk(n + 1, 1 - u)
                keep_t(n, 0)
                exps(n, 1)
                keep_t(n, 1)
                if more:
                    exps(n + 1, 0)

            keep_qk(0, 0)
            exps(0, 0)
            with act.Fori(0, UNITS // 2 - 1) as m:
                unit(2 * m, 0, True)
                unit(2 * m + 1, 1, True)
            unit(UNITS - 2, 0, True)
            unit(UNITS - 1, 1, False)


def project_qkv(nc, d):
    with ExitStack() as ctx:
        sb = lambda n, s, t=F32: ctx.enter_context(nc.sbuf_tensor(n, s, t))
        ps = lambda n, s: ctx.enter_context(nc.psum_tensor(n, s, F32))
        sem = lambda n: ctx.enter_context(nc.semaphore(n))
        w_out = sb("w_out", [128, CT, C])
        w = sb("w_qkv2", [128, CT, 3 * C])
        bias_out = sb("bias_out", [QT, NQ, C])
        bias_v = sb("bias_v2", [QT, NQ, C])
        bias_col = sb("bias_col2", [128, 2 * CT])
        ident = sb("ident2", [128, 128])
        minus_half = sb("minus_half", [QT, NQ])
        aT = [sb(f"aT{i}", [128, 2, CT, UNIT]) for i in range(2)]
        h1 = sb("h1", [QT, NQ, C])
        stats = sb("stats", [QT, NQ, 6])
        both = sb("both", [QT, NQ, 2])
        apart, mean, within, between = (sb(n, [QT, NQ]) for n in ("apart", "mean", "within", "between"))
        veps = sb("veps", [QT, NQ])
        rstd = sb("rstd", [QT, NQ])
        xn = sb("xn", [QT, NQ, C])
        xnT = sb("xnT", [128, CT, CH])
        full = [sb(f"full{i}", [128, CH]) for i in range(2)]
        hi = [sb(f"hi{i}", [128, CH], F32R) for i in range(2)]
        lo = [sb(f"lo{i}", [128, CH], F32R) for i in range(2)]
        v = sb("v_rows", [QT, NQ, C])
        ps_h = ps("ps_h", [128, 2, 512])
        ps_x = ps("ps_x", [128, 2, 512])
        ps_q = ps("ps_q2", [128, 2, 512])
        ps_v = ps("ps_v", [128, 2, 512])
        consts_in, id_zero, id_set, half_set = sem("consts_in2"), sem("id_zero2"), sem("id_set2"), sem("half_set")
        a_in = [sem(f"a_in{i}") for i in range(2)]
        h_ready, h_kept, h_out = sem("h_ready"), sem("h_kept"), sem("h_out")
        stats_ready, mv_ready, veps_ready, rstd_ready, xn_ready = (
            sem("stats_ready"), sem("mv_ready"), sem("veps_ready"), sem("rstd_ready"), sem("xn_ready"))
        xT_ready, xT_kept, q_ready, full_ready, hi_ready, lo_ready, parts_out = (
            sem("xT_ready"), sem("xT_kept"), sem("q_ready"), sem("full_ready"), sem("hi_ready"), sem("lo_ready"),
            [sem(f"parts_out{i}") for i in range(2)])
        v_ready, v_kept, v_out = sem("v_ready"), sem("v_kept2"), sem("v_out")
        block = ctx.enter_context(nc.Block())
        QK = 2 * CT
        SCALE = float(DH) ** -0.5

        @block.sync
        def _(sp):
            sp.dma_start(w_out[:, :, :], d.w_tok_out.rearrange("(t p) n -> p t n", p=128)).then_inc(consts_in, 16)
            sp.dma_start(w[:, :, :], d.w_qkv.rearrange("(t p) n -> p t n", p=128)).then_inc(consts_in, 16)
            sp.dma_start(bias_col[:, :], d.b_qkv[0:2 * C].rearrange("(t p) -> p t", p=128),
                         allow_slow_non_contiguous=True).then_inc(consts_in, 16)
            sp.dma_start(bias_out[:, :, :], view(d.b_tok_out, 0, [[0, QT], [0, NQ], [1, C]])).then_inc(consts_in, 16)
            sp.dma_start(bias_v[:, :, :], view(d.b_qkv, 2 * C, [[0, QT], [0, NQ], [1, C]])).then_inc(consts_in, 16)

            def load(m, i):
                for u in range(2):
                    sp.dma_start(aT[i][:, u, :, :], d.a1[2 * m + u]).then_inc(a_in[i], 16)

            def stores(m):
                sp.wait_ge(h_kept, 2 * m + 2)
                sp.dma_start(d.h1[m], h1[:, :, :]).then_inc(h_out, 16)
                for job in range(QK):
                    sp.wait_ge(hi_ready, QK * m + job + 1)
                    sp.dma_start((d.q, d.k)[job // CT][m, job % CT, 0], hi[job % 2][:, :].bitcast(F32)).then_inc(parts_out[job % 2], 16)
                    sp.wait_ge(lo_ready, QK * m + job + 1)
                    sp.dma_start((d.q, d.k)[job // CT][m, job % CT, 1], lo[job % 2][:, :].bitcast(F32)).then_inc(parts_out[job % 2], 16)
                sp.wait_ge(v_kept, 2 * m + 2)
                sp.dma_start(d.v[m].rearrange("(i p) c -> p i c", p=QT), v[:, :, :]).then_inc(v_out, 16)

            load(0, 0)
            load(1, 1)
            with sp.Fori(0, CHUNKS // 2 - 1) as m2:
                for i in range(2):
                    m = 2 * m2 + i
                    sp.wait_ge(h_ready, 2 * m + 2)
                    load(m + 2, i)
                    stores(m)
            stores(CHUNKS - 2)
            stores(CHUNKS - 1)
            sp.wait_ge(h_out, 16 * CHUNKS)
            for i in range(2):
                sp.wait_ge(parts_out[i], 16 * QK * CHUNKS)
            sp.wait_ge(v_out, 16 * CHUNKS)

        @block.gpsimd
        def _(pool):
            nc.gpsimd.memset(ident[:, :], 0.0).then_inc(id_zero, 1)
            pool.wait_ge(id_zero, 1)
            nc.gpsimd.affine_select(out=ident[:, :], in_=ident[:, :], compare_op=ALU.not_equal, fill=1.0, base=0,
                                    pattern=[[-1, 128]], channel_multiplier=1).then_inc(id_set, 1)
            nc.gpsimd.memset(minus_half[:, :], -0.5).then_inc(half_set, 1)
            pool.wait_ge(half_set, 1)

            def root(m):
                pool.wait_ge(veps_ready, m + 1)
                nc.gpsimd.tensor_tensor(rstd[:, :], veps[:, :], minus_half[:, :], ALU.pow).then_inc(rstd_ready, 1)

            def low(m, job):
                pool.wait_ge(hi_ready, QK * m + job + 1)
                pool.wait_ge(parts_out[job % 2], 32 * (QK // 2 * m + job // 2))
                nc.gpsimd.tensor_tensor(lo[job % 2][:, :], full[job % 2][:, :], hi[job % 2][:, :].bitcast(F32),
                                        ALU.subtract).then_inc(lo_ready, 1)

            root(0)
            with pool.Fori(0, CHUNKS - 1) as m:
                root(m + 1)
                for job in range(QK):
                    low(m, job)
            for job in range(QK):
                low(CHUNKS - 1, job)

        @block.tensor
        def _(pe):
            pe.wait_ge(consts_in, 16 * 5)
            pe.wait_ge(id_set, 1)

            def hidden(m, i):
                pe.wait_ge(a_in[i], 16 * (m - i) + 32)
                pe.wait_ge(h_kept, 2 * m)
                for r in range(NQ):
                    for c in range(CT):
                        mm = nc.tensor.matmul(ps_h[0:QT, r // 2, (r % 2) * C:(r % 2 + 1) * C],
                                              aT[i][:, r // 2, c, (r % 2) * QT:(r % 2 + 1) * QT], w_out[:, c, :],
                                              start=(c == 0), stop=(c == CT - 1))
                    if r % 2:
                        mm.then_inc(h_ready, 1)

            def turn(m):
                pe.wait_ge(xn_ready, NQ * (m + 1))
                pe.wait_ge(xT_kept, CT * m)
                for c in range(CT):
                    for r in range(NQ):
                        mm = nc.tensor.transpose(ps_x[:, c, r * QT:(r + 1) * QT], xn[:, r, c * 128:(c + 1) * 128],
                                                 ident[0:QT, 0:QT])
                    mm.then_inc(xT_ready, 1)

            def project(m):
                pe.wait_ge(xT_kept, CT * (m + 1))
                for job in range(QK):
                    pe.wait_ge(full_ready, QK * m + job - job % 2)
                    for c in range(CT):
                        mm = nc.tensor.matmul(ps_q[:, job % 2, 0:CH], w[:, c, job * 128:(job + 1) * 128],
                                              xnT[:, c, :], start=(c == 0), stop=(c == CT - 1))
                    mm.then_inc(q_ready, 1)
                pe.wait_ge(v_kept, 2 * m)
                for r in range(NQ):
                    for c in range(CT):
                        mm = nc.tensor.matmul(ps_v[0:QT, r // 2, (r % 2) * C:(r % 2 + 1) * C],
                                              xnT[:, c, r * QT:(r + 1) * QT], w[:, c, 2 * C:3 * C],
                                              start=(c == 0), stop=(c == CT - 1))
                    if r % 2:
                        mm.then_inc(v_ready, 1)

            hidden(0, 0)
            turn(0)
            hidden(1, 1)
            project(0)
            turn(1)
            with pe.Fori(0, CHUNKS // 2 - 1) as m2:
                for i in range(2):
                    hidden(2 * m2 + i + 2, i)
                    project(2 * m2 + i + 1)
                    turn(2 * m2 + i + 2)
            project(CHUNKS - 1)

        @block.vector
        def _(dve):
            dve.wait_ge(consts_in, 16 * 5)

            def norm(m):
                dve.wait_ge(h_out, 16 * m)
                for a in range(2):
                    dve.wait_ge(h_ready, 2 * m + a + 1)
                    nc.vector.tensor_tensor(h1[:, 2 * a:2 * a + 2, :].rearrange("p r c -> p (r c)"), ps_h[0:QT, a, :],
                                            bias_out[:, 0:2, :].rearrange("p r c -> p (r c)"),
                                            ALU.add).then_inc(h_kept, 1)
                dve.wait_ge(h_kept, 2 * m + 2)
                for r in range(NQ):
                    nc.vector.bn_stats(stats[:, r, :], h1[:, r, :]).then_inc(stats_ready, 1)
                dve.wait_ge(stats_ready, NQ * (m + 1))
                nc.vector.tensor_tensor(both[:, :, :], stats[:, :, 1:3], stats[:, :, 4:6], ALU.add).then_inc(mv_ready, 1)
                nc.vector.tensor_tensor(apart[:, :], stats[:, :, 1], stats[:, :, 4], ALU.subtract).then_inc(mv_ready, 1)
                dve.wait_ge(mv_ready, 5 * m + 2)
                nc.vector.tensor_scalar(mean[:, :], both[:, :, 0], 0.5, None, ALU.mult).then_inc(mv_ready, 1)
                nc.vector.tensor_scalar(within[:, :], both[:, :, 1], 1.0 / C, EPS, ALU.mult,
                                        ALU.add).then_inc(mv_ready, 1)
                nc.vector.scalar_tensor_tensor(out=between[:, :], in0=apart[:, :], scalar=0.25, in1=apart[:, :],
                                               op0=ALU.mult, op1=ALU.mult).then_inc(mv_ready, 1)
                dve.wait_ge(mv_ready, 5 * (m + 1))
                nc.vector.tensor_tensor(veps[:, :], within[:, :], between[:, :], ALU.add).then_inc(veps_ready, 1)
                dve.wait_ge(rstd_ready, m + 1)
                dve.wait_ge(xT_ready, CT * m)
                for r in range(NQ):
                    nc.vector.tensor_scalar(xn[:, r, :], h1[:, r, :], mean[:, r:r + 1], rstd[:, r:r + 1],
                                            ALU.subtract, ALU.mult).then_inc(xn_ready, 1)

            def keep(m):
                for job in range(QK):
                    dve.wait_ge(q_ready, QK * m + job + 1)
                    dve.wait_ge(lo_ready, QK * m + job - job % 2)
                    if job < CT:
                        nc.vector.tensor_scalar(full[job % 2][:, :], ps_q[:, job % 2, 0:CH], bias_col[:, job:job + 1],
                                                SCALE, ALU.add, ALU.mult).then_inc(full_ready, 1)
                    else:
                        nc.vector.tensor_scalar(full[job % 2][:, :], ps_q[:, job % 2, 0:CH], bias_col[:, job:job + 1],
                                                None, ALU.add).then_inc(full_ready, 1)
                dve.wait_ge(v_out, 16 * m)
                for a in range(2):
                    dve.wait_ge(v_ready, 2 * m + a + 1)
                    nc.vector.tensor_tensor(v[:, 2 * a:2 * a + 2, :].rearrange("p r c -> p (r c)"), ps_v[0:QT, a, :],
                                            bias_v[:, 0:2, :].rearrange("p r c -> p (r c)"),
                                            ALU.add).then_inc(v_kept, 1)

            norm(0)
            with dve.Fori(0, CHUNKS - 1) as m:
                norm(m + 1)
                keep(m)
            keep(CHUNKS - 1)

        @block.scalar
        def _(act):
            def keep_xT(m):
                act.wait_ge(v_ready, 2 * m)
                for c in range(CT):
                    act.wait_ge(xT_ready, CT * m + c + 1)
                    nc.scalar.activation(xnT[:, c, :], ps_x[:, c, 0:CH], ACT.Copy).then_inc(xT_kept, 1)

            def high(m):
                for job in range(QK):
                    act.wait_ge(full_ready, QK * m + job + 1)
                    act.wait_ge(lo_ready, QK * m + job - job % 2)
                    act.wait_ge(parts_out[job % 2], 32 * (QK // 2 * m + job // 2))
                    nc.scalar.activation(hi[job % 2][:, :], full[job % 2][:, :], ACT.Copy).then_inc(hi_ready, 1)

            keep_xT(0)
            with act.Fori(0, CHUNKS - 1) as m:
                high(m)
                keep_xT(m + 1)
            high(CHUNKS - 1)


def full_attention(nc, d):
    with ExitStack() as ctx:
        sb = lambda n, s, t=F32: ctx.enter_context(nc.sbuf_tensor(n, s, t))
        ps = lambda n, s: ctx.enter_context(nc.psum_tensor(n, s, F32))
        sem = lambda n: ctx.enter_context(nc.semaphore(n))
        keys = [sb(f"keys{g}", [STACK + 1, HG, N], F32R) for g in range(G)]
        queries = [sb(f"queries{g}", [STACK + 1, HG, CH], F32R) for g in range(G)]
        values = [sb(f"values{g}", [128, KT, HG * DH]) for g in range(G)]
        corner = [sb(f"corner{g}", [128, 2, HG, 2 * QT], F32R) for g in range(G)]
        prob = sb("prob", [128, SLOTS, HG, CH])
        ident = sb("ident3", [128, 128])
        ident_r = sb("ident_r", [128, 128], F32R)
        ones = sb("ones3", [128, 2, DH])
        tops = sb("tops", [QT, HG * NQ, PER_IMAGE])
        shift = sb("shift", [QT, HG * NQ])
        shift_rows = sb("shift_rows", [HG * NQ, QT], F32R)
        rden = sb("rden3", [128, CH])
        out = [sb(f"out{i}", [128, CH]) for i in range(G)]
        ps_s = ps("ps_s3", [128, 2, 2, 512])
        ps_m = ps("ps_m", [128, 2, 512])
        ps_o = ps("ps_o", [128, 512])
        ps_d = ps("ps_d", [128, 512])
        s_ready, exp_done, tile_used = sem("s_ready3"), sem("exp_done"), sem("tile_used")
        m_ready, m_used = sem("m_ready"), sem("m_used")
        id_zero, id_set, idr_set, ones_set, row_set = (
            sem("id_zero3"), sem("id_set3"), sem("idr_set"), sem("ones_set3"), sem("row_set"))
        k_in, q_in = [sem(f"k_in{g}") for g in range(G)], [sem(f"q_in{g}") for g in range(G)]
        shift_ready, rows_ready, rows_kept, shift_in = (
            sem("shift_ready"), sem("rows_ready"), sem("rows_kept"), sem("shift_in"))
        tops_ready, den_ready, out_ready, out_out = sem("tops_ready"), sem("den_ready"), sem("out_ready"), [sem(f"out_out{g}") for g in range(G)]
        credits = sem("credits")
        HALVES = G * CHUNKS
        PAIRS = 2 * KT
        MAXES = HG * NQ * PER_IMAGE
        AHEAD = 2
        TILE_CREDIT = SLOTS - 1

        with nc.Block() as first:
            @first.vector
            def _(dve):
                cell = 0
                for s, k in ((exp_done, AHEAD), (m_used, AHEAD), (tile_used, TILE_CREDIT)):
                    for _ in range(k):
                        nc.vector.memset(tops[:, cell, :], 0.0).then_inc(s, 1)
                        cell += 1
                for g in range(G):
                    nc.vector.memset(keys[g][STACK:STACK + 1, :, :].bitcast(F32), 1.0).then_inc(credits, 1)
                dve.wait_ge(credits, G)

        block = ctx.enter_context(nc.Block())

        def keys_of(t):
            return (0, FIRST) if t == 0 else (FIRST + 128 * (t - 1), 128)

        @block.sync
        def _(sp):
            def scored(n, g):
                sp.wait_ge(s_ready, PAIRS * (2 * n + g - 1))

            def load_keys(b, g):
                if b is not FIRST_IMAGE:
                    scored(b * PER_IMAGE, g)
                for c in range(PER_IMAGE):
                    for row, part in ((0, 0), (DH, 1), (2 * DH, 0)):
                        src = d.k[b * PER_IMAGE + c, g, part].rearrange("(j d) n -> d j n", j=HG)
                        sp.dma_start(keys[g][row:row + DH, :, c * CH:(c + 1) * CH].bitcast(F32), src
                                     ).then_inc(k_in[g], 16)

            def load_values(b, g):
                if b is not FIRST_IMAGE:
                    sp.wait_ge(tile_used, TILE_CREDIT + KT * (2 * PER_IMAGE * b - 1 + g))
                cols = slice(g * HG * DH, (g + 1) * HG * DH)
                sp.dma_start(values[g][0:FIRST, 0, :], d.v_rows[b, 0:FIRST, cols]).then_inc(k_in[g], 16)
                sp.dma_start(values[g][:, 1:KT, :],
                             d.v_rows[b, FIRST:N, cols].rearrange("(t p) c -> p t c", p=128)).then_inc(k_in[g], 16)
                sp.wait_ge(k_in[g], 16 * (3 * PER_IMAGE + 2) * (b + 1))

            def load_queries(n, g, corner_or_zero):
                if n is not FIRST_IMAGE:
                    scored(n, g)
                for row, part in ((0, 0), (DH, 0), (2 * DH, 1)):
                    sp.dma_start(queries[g][row:row + DH, :, :].bitcast(F32),
                                 d.q[n, g, part].rearrange("(j d) n -> d j n", j=HG)).then_inc(q_in[g], 16)
                sp.dma_start(corner[g][:, :, :, 0:128].bitcast(F32), corner_or_zero[g]).then_inc(q_in[g], 16)

            def shifts(h, g):
                sp.wait_ge(rows_kept, h + 1)
                sp.dma_start(queries[g][STACK:STACK + 1, :, :].rearrange("p j n -> p (j n)").bitcast(F32),
                             shift_rows[:, :].bitcast(F32)).then_inc(shift_in, 16)

            def store(h, g):
                sp.wait_ge(out_ready, h + 1)
                sp.dma_start(d.a2[h], out[g][:, :]).then_inc(out_out[g], 16)

            def chunk(b, n, first_of_image, corner_or_zero):
                for g in range(G):
                    if first_of_image:
                        load_keys(b, g)
                        load_values(b, g)
                    load_queries(n, g, corner_or_zero)
                    if n is not FIRST_IMAGE:
                        store(2 * n - 2 + g, g)
                    shifts(2 * n + g, g)

            FIRST_IMAGE = 0
            chunk(FIRST_IMAGE, FIRST_IMAGE, True, d.corner)
            with sp.Fori(1, PER_IMAGE) as c:
                chunk(FIRST_IMAGE, c, False, d.no_corner)
            with sp.Fori(1, B) as b:
                chunk(b, b * PER_IMAGE, True, d.corner)
                with sp.Fori(1, PER_IMAGE) as c:
                    chunk(b, b * PER_IMAGE + c, False, d.no_corner)
            for g in range(G):
                store(HALVES - G + g, g)
            for g in range(G):
                sp.wait_ge(out_out[g], 16 * CHUNKS)

        @block.gpsimd
        def _(pool):
            nc.gpsimd.memset(ident[:, :], 0.0).then_inc(id_zero, 1)
            pool.wait_ge(id_zero, 1)
            nc.gpsimd.affine_select(out=ident[:, :], in_=ident[:, :], compare_op=ALU.not_equal, fill=1.0, base=0,
                                    pattern=[[-1, 128]], channel_multiplier=1).then_inc(id_set, 1)
            pool.wait_ge(id_set, 1)
            nc.gpsimd.tensor_copy(ident_r[:, :], ident[:, :]).then_inc(idr_set, 1)
            nc.gpsimd.memset(ones[:, 1, :], 1.0).then_inc(ones_set, 1)
            for g in range(G):
                nc.gpsimd.memset(corner[g][:, :, :, 128:2 * QT].bitcast(F32), 0.0).then_inc(ones_set, 1)

        @block.tensor
        def _(pe):
            pe.wait_ge(idr_set, 1)
            pe.wait_ge(ones_set, 4 + 2 * G)

            def scores(h, g, t, spread):
                at, k = keys_of(t)
                for pair in range(2):
                    spread()
                    if pair:
                        spread()
                    i = 2 * t + pair
                    pe.wait_ge(exp_done, h * PAIRS + i + 1)
                    for jj in range(2):
                        j = 2 * pair + jj
                        o = ps_s[0:k, pair, jj, :]
                        last = t == KT - 1
                        mm = nc.tensor.matmul(o[:, 0:CH], keys[g][:, j, at:at + k], queries[g][:, j, :],
                                              start=True, stop=not last, skip_group_check=last)
                        if last:
                            for part in range(2):
                                mm = nc.tensor.matmul(o[:, 0:2 * QT], ident_r[:, :], corner[g][:, part, j, :],
                                                      start=False, stop=part == 1, skip_group_check=True)
                    mm.then_inc(s_ready, 1)

            def weigh(h, g, t, spread=None):
                pe.wait_ge(exp_done, AHEAD + h * PAIRS + 2 * t + 2)
                if t == 0:
                    pe.wait_ge(out_ready, h)
                for j in range(HG):
                    mm = nc.tensor.matmul(ps_o[j * DH:(j + 1) * DH, 0:CH], values[g][:, t, j * DH:(j + 1) * DH],
                                          prob[:, t % SLOTS, j, :], start=(t == 0), stop=(t == KT - 1))
                if spread:
                    spread()
                for j in range(HG):
                    mm = nc.tensor.matmul(ps_d[j * DH:(j + 1) * DH, 0:CH], ones[:, int(t > 0), :],
                                          prob[:, t % SLOTS, j, :], start=(t == 0), stop=(t == KT - 1))
                mm.then_inc(tile_used, 1)

            def turn(h):
                pe.wait_ge(shift_ready, h + 1)
                nc.tensor.transpose(ps_m[0:HG * NQ, 0, 0:QT], shift[:, :], ident[0:QT, 0:QT]).then_inc(rows_ready, 1)

            def half(h, g, chunk_next, has_next, has_before):
                pe.wait_ge(shift_in, 16 * (h + 1))
                done = [0]

                def spread(n=1):
                    if has_next and done[0] < min(MAXES, STEP * (t + 1 - LEAD)):
                        maxima(h + 1, 1 - g, chunk_next, done[0], done[0] + n)
                        done[0] += n

                for t in range(KT):
                    scores(h, g, t, spread)
                    if t > 0:
                        weigh(h, g, t - 1, spread)
                    elif has_before:
                        weigh(h - 1, 1 - g, KT - 1, spread)
                    spread()
                    spread()
                    if has_next and t == TURN_AT:
                        turn(h + 1)

            def maxima(h, g, chunk, a, b):
                for i in range(a, b):
                    if i == 0:
                        pe.wait_ge(q_in[g], 64 * (chunk + 1))
                        pe.wait_ge(rows_kept, h)
                    c, j, r = i // (HG * NQ), i // NQ % HG, i % NQ
                    pe.wait_ge(m_used, h * MAXES + i + 1)
                    o = ps_m[0:QT, i % 2, :]
                    q = queries[g][0:STACK, j, r * QT:(r + 1) * QT]
                    last = c == PER_IMAGE - 1 and r < 2
                    mm = nc.tensor.matmul(o[:, 0:CH], q, keys[g][0:STACK, j, c * CH:(c + 1) * CH],
                                          start=True, stop=not last, skip_group_check=last)
                    if last:
                        mm = nc.tensor.matmul(o[:, CH - 128:CH], corner[g][:, 0, j, r * QT:(r + 1) * QT],
                                              ident_r[:, :], start=False, stop=True, skip_group_check=True)
                    mm.then_inc(m_ready, 1)

            LEAD, STEP = 2, 6
            TURN_AT = LEAD + -(-MAXES // STEP)

            maxima(0, 0, 0, 0, MAXES)
            turn(0)
            half(0, 0, 0, True, False)
            with pe.Fori(0, CHUNKS - 1) as n:
                half(2 * n + 1, 1, n + 1, True, True)
                half(2 * n + 2, 0, n + 1, True, True)
            half(HALVES - 1, 1, 0, False, True)
            weigh(HALVES - 1, 1, KT - 1)

        @block.scalar
        def _(act):
            def half(h, g):
                for t in range(KT):
                    at, k = keys_of(t)
                    act.wait_ge(tile_used, h * KT + t)
                    for pair in range(2):
                        act.wait_ge(s_ready, h * PAIRS + 2 * t + pair + 1)
                        nc.scalar.activation(prob[0:k, t % SLOTS, 2 * pair:2 * pair + 2, :],
                                             ps_s[0:k, pair, :, 0:CH], ACT.Exp).then_inc(exp_done, 1)

            with act.Fori(0, CHUNKS) as n:
                half(2 * n, 0)
                half(2 * n + 1, 1)

        @block.vector
        def _(dve):
            def maxima(h):
                for i in range(MAXES):
                    dve.wait_ge(m_ready, h * MAXES + i + 1)
                    nc.vector.tensor_reduce(tops[:, i % (HG * NQ), i // (HG * NQ):i // (HG * NQ) + 1],
                                            ps_m[0:QT, i % 2, 0:CH], AX.X, ALU.max).then_inc(m_used, 1)
                dve.wait_ge(m_used, AHEAD + (h + 1) * MAXES)
                nc.vector.tensor_reduce(shift[:, :], tops[:, :, :], AX.X, ALU.max, negate=True).then_inc(shift_ready, 1)
                dve.wait_ge(rows_ready, h + 1)
                dve.wait_ge(shift_in, 16 * h)
                nc.vector.tensor_copy(shift_rows[:, :], ps_m[0:HG * NQ, 0, 0:QT]).then_inc(rows_kept, 1)

            def outputs(h, g):
                dve.wait_ge(tile_used, TILE_CREDIT + KT * (h + 1))
                nc.vector.reciprocal(rden[:, :], ps_d[:, 0:CH]).then_inc(den_ready, 1)
                dve.wait_ge(den_ready, h + 1)
                dve.wait_ge(out_out[g], 8 * (h - g))
                nc.vector.tensor_tensor(out[g][:, :], ps_o[:, 0:CH], rden[:, :], ALU.mult).then_inc(out_ready, 1)

            nc.vector.memset(ones[0:FIRST, 0, :], 1.0).then_inc(ones_set, 1)
            nc.vector.memset(ones[FIRST:128, 0, :], 0.0).then_inc(ones_set, 1)
            nc.vector.memset(prob[FIRST:128, 0, :, :], 0.0).then_inc(ones_set, 1)
            for g in range(G):
                nc.vector.memset(values[g][FIRST:128, 0, :], 0.0).then_inc(ones_set, 1)
            maxima(0)
            maxima(1)
            with dve.Fori(0, CHUNKS - 1) as n:
                outputs(2 * n, 0)
                maxima(2 * n + 2)
                outputs(2 * n + 1, 1)
                maxima(2 * n + 3)
            outputs(HALVES - 2, 0)
            outputs(HALVES - 1, 1)


def gated_ffn(nc, d):
    with ExitStack() as outer:
        osb = lambda n, s, t=F32: outer.enter_context(nc.sbuf_tensor(n, s, t))
        xnT = osb("xnT4", [128, CHUNKS, CT, CH])
        gate = osb("gate", [QT, B, PER_IMAGE * NQ])
        coef = osb("coef", [QT, B, PER_IMAGE * NQ])
        project_out(nc, d, xnT, gate)
        rank_gates(nc, d, gate, coef)
        ffn(nc, d, xnT, coef)


def project_out(nc, d, xnT, gate):
    with ExitStack() as ctx:
        sb = lambda n, s, t=F32: ctx.enter_context(nc.sbuf_tensor(n, s, t))
        ps = lambda n, s: ctx.enter_context(nc.psum_tensor(n, s, F32))
        sem = lambda n: ctx.enter_context(nc.semaphore(n))
        w = sb("w_proj", [128, CT, C])
        bias = sb("bias_proj", [QT, NQ, C])
        w_gate = sb("w_gate", [QT, C])
        b_gate = sb("b_gate", [QT, 1])
        ident = sb("ident4", [128, 128])
        minus_half = sb("minus_half4", [QT, NQ])
        aT = [sb(f"aT4{i}", [128, G, CH]) for i in range(2)]
        h1 = [sb(f"h1b{i}", [QT, NQ, C]) for i in range(2)]
        h1b = sb("h1_biased", [QT, NQ, C])
        h2 = sb("h2", [QT, NQ, C])
        stats = sb("stats4", [QT, NQ, 6])
        both = sb("both4", [QT, NQ, 2])
        apart, mean, within, between = (sb(n, [QT, NQ]) for n in ("apart4", "mean4", "within4", "between4"))
        veps = sb("veps4", [QT, NQ])
        rstd = sb("rstd4", [QT, NQ])
        xn = sb("xn4", [QT, NQ, C])
        base = sb("base", [QT, NQ, C])
        product = sb("product", [QT, NQ, C])
        dots = sb("dots", [QT, NQ])
        ps_h = ps("ps_h4", [128, 2, 512])
        ps_x = ps("ps_x4", [128, 2, 512])
        consts_in, id_zero, id_set, half_set = sem("consts_in4"), sem("id_zero4"), sem("id_set4"), sem("half_set4")
        a_in = [sem(f"a_in4{i}") for i in range(2)]
        biased, h_ready, h_kept = sem("biased"), sem("h_ready4"), sem("h_kept4")
        stats_ready, mv_ready, veps_ready, rstd_ready, xn_ready = (
            sem("stats_ready4"), sem("mv_ready4"), sem("veps_ready4"), sem("rstd_ready4"), sem("xn_ready4"))
        xT_ready, xT_kept, base_ready, base_out = (
            sem("xT_ready4"), sem("xT_kept4"), sem("base_ready"), sem("base_out"))
        dots_ready, gate_ready, gate_out = sem("dots_ready"), sem("gate_ready"), sem("gate_out")
        block = ctx.enter_context(nc.Block())

        @block.sync
        def _(sp):
            sp.dma_start(w[:, :, :], d.w_proj.rearrange("(t p) n -> p t n", p=128)).then_inc(consts_in, 16)
            sp.dma_start(bias[:, :, :], view(d.b_proj, 0, [[0, QT], [0, NQ], [1, C]])).then_inc(consts_in, 16)
            sp.dma_start(w_gate[:, :], view(d.w_gate, 0, [[0, QT], [1, C]])).then_inc(consts_in, 16)
            sp.dma_start(b_gate[:, :], view(d.b_gate, 0, [[0, QT], [1, 1]])).then_inc(consts_in, 16)

            def load(m, i):
                for g in range(G):
                    sp.dma_start(aT[i][:, g, :], d.a2[2 * m + g]).then_inc(a_in[i], 16)
                sp.dma_start(h1[i][:, :, :], d.h1[m]).then_inc(a_in[i], 16)

            def store(m):
                sp.wait_ge(base_ready, m + 1)
                sp.dma_start(d.base[m], base[:, :, :]).then_inc(base_out, 16)

            load(0, 0)
            load(1, 1)
            with sp.Fori(0, CHUNKS // 2 - 1) as m2:
                for i in range(2):
                    m = 2 * m2 + i
                    sp.wait_ge(biased, m + 1)
                    sp.wait_ge(h_ready, 2 * m + 2)
                    load(m + 2, i)
                    store(m)
            store(CHUNKS - 2)
            store(CHUNKS - 1)
            sp.wait_ge(base_out, 16 * CHUNKS)
            sp.wait_ge(gate_ready, CHUNKS)
            for b in range(B):
                sp.dma_start(d.gate[b].rearrange("(i p) -> p i", p=QT), gate[:, b, :],
                             allow_slow_non_contiguous=True).then_inc(gate_out, 16)
            sp.wait_ge(gate_out, 16 * B)

        @block.gpsimd
        def _(pool):
            nc.gpsimd.memset(ident[:, :], 0.0).then_inc(id_zero, 1)
            pool.wait_ge(id_zero, 1)
            nc.gpsimd.affine_select(out=ident[:, :], in_=ident[:, :], compare_op=ALU.not_equal, fill=1.0, base=0,
                                    pattern=[[-1, 128]], channel_multiplier=1).then_inc(id_set, 1)
            nc.gpsimd.memset(minus_half[:, :], -0.5).then_inc(half_set, 1)
            pool.wait_ge(half_set, 1)
            pool.wait_ge(consts_in, 64)

            def add_bias(m, i):
                pool.wait_ge(a_in[i], 24 * (m - i) + 48)
                pool.wait_ge(h_kept, 2 * m)
                nc.gpsimd.tensor_tensor(h1b[:, :, :], h1[i][:, :, :], bias[:, :, :], ALU.add).then_inc(biased, 1)

            def root(m):
                pool.wait_ge(veps_ready, m + 1)
                nc.gpsimd.tensor_tensor(rstd[:, :], veps[:, :], minus_half[:, :], ALU.pow).then_inc(rstd_ready, 1)

            def add_base(m):
                pool.wait_ge(xn_ready, NQ * (m + 1))
                pool.wait_ge(base_out, 16 * m)
                nc.gpsimd.tensor_tensor(base[:, :, :], h2[:, :, :], xn[:, :, :], ALU.add).then_inc(base_ready, 1)

            add_bias(0, 0)
            with pool.Fori(0, CHUNKS // 2 - 1) as m2:
                for i in range(2):
                    m = 2 * m2 + i
                    root(m)
                    add_bias(m + 1, 1 - i)
                    add_base(m)
            root(CHUNKS - 2)
            add_bias(CHUNKS - 1, 1)
            add_base(CHUNKS - 2)
            root(CHUNKS - 1)
            add_base(CHUNKS - 1)

        @block.tensor
        def _(pe):
            pe.wait_ge(consts_in, 64)
            pe.wait_ge(id_set, 1)

            def hidden(m, i):
                pe.wait_ge(a_in[i], 24 * (m - i) + 48)
                pe.wait_ge(h_kept, 2 * m)
                for r in range(NQ):
                    for c in range(CT):
                        mm = nc.tensor.matmul(ps_h[0:QT, r // 2, (r % 2) * C:(r % 2 + 1) * C],
                                              aT[i][:, c, r * QT:(r + 1) * QT], w[:, c, :],
                                              start=(c == 0), stop=(c == CT - 1))
                    if r % 2:
                        mm.then_inc(h_ready, 1)

            def turn(m):
                pe.wait_ge(xn_ready, NQ * (m + 1))
                pe.wait_ge(xT_kept, CT * m)
                for c in range(CT):
                    for r in range(NQ):
                        mm = nc.tensor.transpose(ps_x[:, c, r * QT:(r + 1) * QT], xn[:, r, c * 128:(c + 1) * 128],
                                                 ident[0:QT, 0:QT])
                    mm.then_inc(xT_ready, 1)

            hidden(0, 0)
            with pe.Fori(0, CHUNKS // 2 - 1) as m2:
                hidden(2 * m2 + 1, 1)
                turn(2 * m2)
                hidden(2 * m2 + 2, 0)
                turn(2 * m2 + 1)
            hidden(CHUNKS - 1, 1)
            turn(CHUNKS - 2)
            turn(CHUNKS - 1)

        @block.scalar
        def _(act):
            with act.Fori(0, CHUNKS) as m:
                for c in range(CT):
                    act.wait_ge(xT_ready, CT * m + c + 1)
                    nc.scalar.activation(xnT[:, m, c, :], ps_x[:, c, 0:CH], ACT.Copy).then_inc(xT_kept, 1)

        @block.vector
        def _(dve):
            dve.wait_ge(consts_in, 64)

            def norm(m, gates):
                dve.wait_ge(biased, m + 1)
                dve.wait_ge(base_ready, m)
                for a in range(2):
                    dve.wait_ge(h_ready, 2 * m + a + 1)
                    nc.vector.tensor_tensor(h2[:, 2 * a:2 * a + 2, :].rearrange("p r c -> p (r c)"), ps_h[0:QT, a, :],
                                            h1b[:, 2 * a:2 * a + 2, :].rearrange("p r c -> p (r c)"),
                                            ALU.add).then_inc(h_kept, 1)
                dve.wait_ge(h_kept, 2 * m + 2)
                for r in range(NQ):
                    nc.vector.bn_stats(stats[:, r, :], h2[:, r, :]).then_inc(stats_ready, 1)
                dve.wait_ge(stats_ready, NQ * (m + 1))
                nc.vector.tensor_tensor(both[:, :, :], stats[:, :, 1:3], stats[:, :, 4:6], ALU.add).then_inc(mv_ready, 1)
                nc.vector.tensor_tensor(apart[:, :], stats[:, :, 1], stats[:, :, 4], ALU.subtract).then_inc(mv_ready, 1)
                dve.wait_ge(mv_ready, 5 * m + 2)
                nc.vector.tensor_scalar(mean[:, :], both[:, :, 0], 0.5, None, ALU.mult).then_inc(mv_ready, 1)
                nc.vector.tensor_scalar(within[:, :], both[:, :, 1], 1.0 / C, EPS, ALU.mult,
                                        ALU.add).then_inc(mv_ready, 1)
                nc.vector.scalar_tensor_tensor(out=between[:, :], in0=apart[:, :], scalar=0.25, in1=apart[:, :],
                                               op0=ALU.mult, op1=ALU.mult).then_inc(mv_ready, 1)
                dve.wait_ge(mv_ready, 5 * (m + 1))
                nc.vector.tensor_tensor(veps[:, :], within[:, :], between[:, :], ALU.add).then_inc(veps_ready, 1)
                dve.wait_ge(rstd_ready, m + 1)
                dve.wait_ge(xT_ready, CT * m)
                for r in range(NQ):
                    nc.vector.tensor_scalar(xn[:, r, :], h2[:, r, :], mean[:, r:r + 1], rstd[:, r:r + 1],
                                            ALU.subtract, ALU.mult).then_inc(xn_ready, 1)
                for r in range(NQ):
                    dve.wait_ge(xn_ready, NQ * m + r + 1)
                    nc.vector.tensor_tensor_reduce(product[:, r, :], xn[:, r, :], w_gate[:, :], 1.0, 0.0, ALU.mult,
                                                   ALU.add, dots[:, r:r + 1]).then_inc(dots_ready, 1)
                dve.wait_ge(dots_ready, NQ * (m + 1))
                nc.vector.tensor_scalar(gates, dots[:, :], b_gate[:, 0:1], None, ALU.add).then_inc(gate_ready, 1)

            flat = gate[:, :, :].rearrange("p b i -> p (b i)")
            with dve.Fori(0, CHUNKS) as m:
                norm(m, flat[:, bass.ds(m * NQ, NQ)])


def rank_gates(nc, d, gate, coef):
    with ExitStack() as ctx:
        sb = lambda n, s, t=F32: ctx.enter_context(nc.sbuf_tensor(n, s, t))
        sem = lambda n: ctx.enter_context(nc.semaphore(n))
        TILES = N // QT
        row = [sb(f"gate_row{i}", [QT, N]) for i in range(B)]
        own = sb("own", [QT, TILES])
        hits = sb("hits", [QT, 4, N], mybir.dt.bfloat16)
        count = sb("count", [QT, TILES, 4])
        rank = sb("rank", [QT, TILES])
        kept = sb("kept", [QT, TILES])
        earlier = sb("earlier", [QT, QT])
        row_in = [sem(f"row_in{b}") for b in range(B)]
        tri_one, tri_set, zero_set = sem("tri_one"), sem("tri_set"), sem("zero_set5")
        own_ready, counted, ranked, kept_ready, coef_ready = (
            sem("own_ready"), sem("counted"), sem("ranked"), sem("kept_ready"), sem("coef_ready"))
        block = ctx.enter_context(nc.Block())
        OPS = 4 * TILES - 2

        @block.sync
        def _(sp):
            for b in range(B):
                sp.dma_start(row[b][:, :], view(d.gate, b * N, [[0, QT], [1, N]])).then_inc(row_in[b], 16)

        @block.gpsimd
        def _(pool):
            nc.gpsimd.memset(earlier[:, :], 1.0).then_inc(tri_one, 1)
            pool.wait_ge(tri_one, 1)
            nc.gpsimd.affine_select(out=earlier[:, :], in_=earlier[:, :], compare_op=ALU.is_gt, fill=0.0, base=0,
                                    pattern=[[-1, QT]], channel_multiplier=1).then_inc(tri_set, 1)

        @block.vector
        def _(dve):
            nc.vector.memset(count[:, :, :], 0.0).then_inc(zero_set, 1)
            dve.wait_ge(zero_set, 1)
            dve.wait_ge(tri_set, 1)
            for b in range(B):
                nc.vector.tensor_copy(own[:, :], gate[:, b, :]).then_inc(own_ready, 1)
                dve.wait_ge(own_ready, b + 1)
                dve.wait_ge(row_in[b], 16)
                dve.wait_ge(ranked, b)
                for i in range(TILES):
                    a, z = i * QT, (i + 1) * QT
                    mine = own[:, i:i + 1]

                    def tally(lo, hi, op, slot):
                        nc.vector.tensor_scalar(hits[:, slot, lo:hi], row[b][:, lo:hi], mine, 0.0, op, ALU.add,
                                                accum_out=count[:, i, slot:slot + 1]).then_inc(counted, 1)

                    if i > 0:
                        dve.wait_ge(counted, OPS * b + 4 * i - 1)
                        tally(0, a, ALU.is_ge, 0)
                    elif b > 0:
                        dve.wait_ge(counted, OPS * b)
                    if i < TILES - 1:
                        tally(z, N, ALU.is_gt, 1)
                    tally(a, z, ALU.is_gt, 2)
                    nc.vector.scalar_tensor_tensor(out=hits[:, 3, a:z], in0=row[b][:, a:z], scalar=mine,
                                                   in1=earlier[:, :], op0=ALU.is_equal, op1=ALU.mult,
                                                   accum_out=count[:, i, 3:4]).then_inc(counted, 1)
                dve.wait_ge(counted, OPS * (b + 1))
                nc.vector.tensor_reduce(rank[:, :], count[:, :, :], AX.X, ALU.add).then_inc(ranked, 1)
                dve.wait_ge(ranked, b + 1)
                nc.vector.tensor_scalar(kept[:, :], rank[:, :], float(KEEP), None, ALU.is_lt).then_inc(kept_ready, 1)
                dve.wait_ge(kept_ready, b + 1)
                nc.vector.tensor_tensor(coef[:, b, :], own[:, :], kept[:, :], ALU.mult).then_inc(coef_ready, 1)
                dve.wait_ge(coef_ready, b + 1)


def ffn(nc, d, xnT, coef):
    with ExitStack() as ctx:
        sb = lambda n, s, t=F32: ctx.enter_context(nc.sbuf_tensor(n, s, t))
        ps = lambda n, s: ctx.enter_context(nc.psum_tensor(n, s, F32))
        sem = lambda n: ctx.enter_context(nc.semaphore(n))
        w_up = sb("w_up", [128, CT, HID])
        w_down = sb("w_down", [128, HT, C])
        b_up = sb("b_up", [128, HT])
        b_down = sb("b_down", [QT, 2, C])
        base = [sb(f"base5{i}", [QT, NQ, C]) for i in range(2)]
        coefs = sb("coefs", [QT, NQ])
        hT = sb("hT", [128, HT, CH])
        y = sb("y", [QT, NQ, C])
        out = sb("out5", [QT, NQ, C])
        ps_h = ps("ps_h5", [128, 4, 512])
        ps_y = ps("ps_y", [128, 4, 512])
        base_in = [sem(f"base_in{i}") for i in range(2)]
        consts_in, h_ready, h_kept = sem("consts_in5"), sem("h_ready5"), sem("h_kept5")
        y_ready, y_kept, coefs_set, out_ready, out_out = (
            sem("y_ready"), sem("y_kept"), sem("coefs_set"), sem("out_ready5"), sem("out_out5"))
        block = ctx.enter_context(nc.Block())

        @block.sync
        def _(sp):
            sp.dma_start(w_up[:, :, :], d.w_up.rearrange("(t p) n -> p t n", p=128)).then_inc(consts_in, 16)
            sp.dma_start(w_down[:, :, :], d.w_down.rearrange("(t p) n -> p t n", p=128)).then_inc(consts_in, 16)
            sp.dma_start(b_up[:, :], d.b_up.rearrange("(t p) -> p t", p=128),
                         allow_slow_non_contiguous=True).then_inc(consts_in, 16)
            sp.dma_start(b_down[:, :, :], view(d.b_down, 0, [[0, QT], [0, 2], [1, C]])).then_inc(consts_in, 16)

            def load(m, i):
                sp.dma_start(base[i][:, :, :], d.base[m]).then_inc(base_in[i], 16)

            def store(m):
                sp.wait_ge(out_ready, NQ * (m + 1))
                sp.dma_start(d.out[m].rearrange("(i p) c -> p i c", p=QT), out[:, :, :]).then_inc(out_out, 16)

            load(0, 0)
            load(1, 1)
            with sp.Fori(0, CHUNKS // 2 - 1) as m2:
                for i in range(2):
                    store(2 * m2 + i)
                    load(2 * m2 + i + 2, i)
            store(CHUNKS - 2)
            store(CHUNKS - 1)
            sp.wait_ge(out_out, 16 * CHUNKS)

        @block.tensor
        def _(pe):
            pe.wait_ge(consts_in, 64)

            def up(m, t):
                if t < 4:
                    pe.wait_ge(h_kept, HT * m)
                else:
                    pe.wait_ge(h_kept, HT * m + t - 3)
                for c in range(CT):
                    mm = nc.tensor.matmul(ps_h[:, t % 4, 0:CH], w_up[:, c, t * 128:(t + 1) * 128], xnT[:, m, c, :],
                                          start=(c == 0), stop=(c == CT - 1))
                mm.then_inc(h_ready, 1)

            def down(m, r):
                pe.wait_ge(h_kept, HT * (m + 1))
                pe.wait_ge(y_kept, NQ * m)
                for t in range(HT):
                    mm = nc.tensor.matmul(ps_y[0:QT, r, 0:C], hT[:, t, r * QT:(r + 1) * QT], w_down[:, t, :],
                                          start=(t == 0), stop=(t == HT - 1))
                mm.then_inc(y_ready, 1)

            with pe.Fori(0, CHUNKS) as m:
                for t in range(HT):
                    up(m, t)
                for r in range(NQ):
                    down(m, r)

        @block.scalar
        def _(act):
            act.wait_ge(consts_in, 64)
            with act.Fori(0, CHUNKS) as m:
                act.wait_ge(y_ready, NQ * m)
                for t in range(HT):
                    act.wait_ge(h_ready, HT * m + t + 1)
                    nc.scalar.activation(hT[:, t, :], ps_h[:, t % 4, 0:CH], ACT.Gelu_apprx_tanh,
                                         bias=b_up[:, t:t + 1]).then_inc(h_kept, 1)

        @block.vector
        def _(dve):
            dve.wait_ge(consts_in, 64)
            flat = coef[:, :, :].rearrange("p b i -> p (b i)")

            def chunk(m, i):
                dve.wait_ge(out_ready, NQ * m)
                nc.vector.tensor_copy(coefs[:, :], flat[:, bass.ds(m * NQ, NQ)]).then_inc(coefs_set, 1)
                dve.wait_ge(coefs_set, m + 1)
                dve.wait_ge(base_in[i], 8 * (m - i) + 16)
                dve.wait_ge(out_out, 16 * m)
                for r in range(NQ):
                    dve.wait_ge(y_ready, NQ * m + r + 1)
                    nc.vector.tensor_tensor(y[:, r, :], ps_y[0:QT, r, 0:C], b_down[:, 0, :], ALU.add).then_inc(y_kept, 1)
                for r in range(NQ):
                    dve.wait_ge(y_kept, NQ * m + r + 1)
                    nc.vector.scalar_tensor_tensor(out=out[:, r, :], in0=y[:, r, :], scalar=coefs[:, r:r + 1],
                                                   in1=base[i][:, r, :], op0=ALU.mult, op1=ALU.add
                                                   ).then_inc(out_ready, 1)

            with dve.Fori(0, CHUNKS // 2) as m2:
                chunk(2 * m2, 0)
                chunk(2 * m2 + 1, 1)


class Dram:
    pass


def vit_tower(nc, d):
    def scratch(name, shape, dt=F32):
        return nc.dram_tensor(name, shape, dt, kind="Internal").ap()

    d.win_bias = scratch("win_bias", [4, GROUP, GROUP])
    d.negs = scratch("negs", [28, 28])
    d.skew = scratch("skew", [NH * 128 * 257])
    d.corner = scratch("corner_parts", [G, 128, 2, HG, 128])
    d.no_corner = scratch("no_corner", [G, 128, 2, HG, 128])
    d.a1 = scratch("window_out", [UNITS, 128, CT, UNIT])
    d.h1 = scratch("hidden1", [CHUNKS, QT, NQ, C])
    d.q = scratch("q_parts", [CHUNKS, G, 2, 128, CH])
    d.k = scratch("k_parts", [CHUNKS, G, 2, 128, CH])
    d.v = scratch("v_rows_dram", [CHUNKS, CH, C])
    d.v_rows = d.v.rearrange("(b k) n c -> b (k n) c", b=B)
    d.a2 = scratch("attention_out", [G * CHUNKS, 128, CH])
    d.base = scratch("base_rows", [CHUNKS, QT, NQ, C])
    d.gate = scratch("gate_rows", [B, N])
    setup_tables(nc, d)
    window_attention(nc, d)
    project_qkv(nc, d)
    full_attention(nc, d)
    gated_ffn(nc, d)


def kernel(**inputs):
    import numpy as np
    import concourse.bacc as bacc
    from concourse import mybir as mb
    from concourse.bass_utils import run_bass_kernel_spmd as run

    def rolled(x, axis):
        k = WS // 2
        head, tail = np.split(x, [k], axis=axis)
        return np.concatenate([tail, head], axis=axis)

    x = rolled(rolled(np.asarray(inputs["x"]), 2), 3)
    w1 = np.asarray(inputs["L0_tok_w1"]).reshape(DH, NH, 3, C)
    arrays = {
        "x": x.reshape(B, CT, 128, SIDE // WS, WS, 2, HALFROW).transpose(0, 3, 2, 1, 5, 4, 6).reshape(
            UNITS, 128, CT, UNIT),
        "w_tok": w1.transpose(3, 2, 1, 0).reshape(C, 3 * C),
        "b_tok": np.asarray(inputs["L0_tok_b1"]).reshape(DH, NH, 3).transpose(2, 1, 0).reshape(3 * C),
        "w_tok_out": np.asarray(inputs["L0_tok_w2"]).T,
        "b_tok_out": inputs["L0_tok_b2"],
        "pos_emb": inputs["L0_tok_pos_emb"],
        "w_qkv": inputs["L0_attn_qkv_w"],
        "b_qkv": inputs["L0_attn_qkv_b"],
        "w_proj": inputs["L0_attn_proj_w"],
        "b_proj": inputs["L0_attn_proj_b"],
        "rpb": np.asarray(inputs["L0_attn_rpb_table"]).T,
        "w_gate": np.asarray(inputs["L0_ffn_wr"]).reshape(C),
        "b_gate": inputs["L0_ffn_br"],
        "w_up": inputs["L0_ffn_w1"],
        "b_up": inputs["L0_ffn_b1"],
        "w_down": inputs["L0_ffn_w2"],
        "b_down": inputs["L0_ffn_b2"],
    }
    nc = bacc.Bacc("TRN2", target_bir_lowering=False, num_devices=1)
    d = Dram()
    launch = {}
    for name, a in arrays.items():
        a = np.ascontiguousarray(a)
        launch[f"in_{name}"] = a
        ap = nc.dram_tensor(f"in_{name}", a.shape, mb.dt.from_np(a.dtype), kind="ExternalInput").ap()
        d.__dict__[name] = ap
    d.out = nc.dram_tensor("out", (CHUNKS, CH, C), F32, kind="ExternalOutput").ap()
    vit_tower(nc, d)
    r = run(nc, [launch], core_ids=[0])
    return r.results[0]["out"].reshape(B, N, C)
```

```python
from contextlib import ExitStack

import concourse.bass as bass
from concourse import mybir

ALU = mybir.AluOpType
ACT = mybir.ActivationFunctionType
AX = mybir.AxisListType
F32 = mybir.dt.float32
F32R = mybir.dt.float32r

B = 4
C = 256
CT = C // 128
SIDE = 56
N = SIDE * SIDE
NH = 8
DH = C // NH
WS = 4
GROUP = SIDE // 2 * WS
UNIT = 2 * GROUP
UNITS = B * N // UNIT
HALFROW = SIDE // 2
CH = 448
CHUNKS = B * N // CH
PER_IMAGE = N // CH
QT = 112
NQ = CH // QT
G = 2
HG = NH // G
FIRST = 64
KT = 1 + (N - FIRST) // 128
SLOTS = 5
STACK = 3 * DH
HID = 4 * C
HT = HID // 128
KEEP = max(1, N // 2) - 1
REL = 127
NEG = -1.0e30
EPS = 1e-5


def view(dram, offset, dims):
    return bass.AP(dram.tensor, offset, dims)


ONE = 1


def start_counts(nc, sems, more=None):
    with nc.Block() as block:
        @block.vector
        def _(dve):
            for s in sems:
                dve.sem_inc(s, ONE)
            for s, uses in (more or {}).items():
                dve.sem_inc(s, uses)


def setup_tables(nc, d):
    with ExitStack() as ctx:
        sb = lambda n, s, t=F32: ctx.enter_context(nc.sbuf_tensor(n, s, t))
        sem = lambda n: ctx.enter_context(nc.semaphore(n))
        neg = sb("neg", [GROUP, 4, GROUP])
        rel = sb("rel", [NH, REL])
        edge = sb("edge", [NH, 255])
        corner = sb("corner", [128, NH, 128])
        corner_hi = sb("corner_hi", [128, NH, 128], F32R)
        corner_lo = sb("corner_lo", [128, NH, 128], F32R)
        zero = sb("zero", [128, 2, HG, 128])
        zero_set, zero_out = sem("zero_set"), sem("zero_out")
        neg_set, filled, placed, masked = sem("neg_set"), sem("filled"), sem("placed"), sem("masked")
        rel_in, edge_zero, edge_set, skewed, corner_in = (
            sem("rel_in"), sem("edge_zero"), sem("edge_set"), sem("skewed"), sem("corner_in"))
        hi_set, lo_set, corner_out = sem("hi_set"), sem("lo_set"), sem("corner_out")
        block = ctx.enter_context(nc.Block())

        def table(v, offset, dims):
            return view(d.win_bias, v * GROUP * GROUP + offset, dims)

        @block.sync
        def _(sp):
            sp.wait_ge(neg_set, 1)
            sp.dma_start(d.win_bias.rearrange("v p k -> p v k"), neg[:, :, :]).then_inc(filled, 16)
            sp.dma_start(d.negs, neg[0:28, 0, 0:28]).then_inc(filled, 16)
            sp.wait_ge(filled, 32)
            n = 0
            for v in range(4):
                for r in range(WS):
                    for p in range(WS):
                        src = view(d.pos_emb, (WS - 1 - r) * 7 + WS - 1 - p, [[0, 7], [7, WS], [1, WS]])
                        dst = table(v, (r * HALFROW + p) * GROUP,
                                    [[WS * GROUP + WS, 7], [HALFROW, WS], [1, WS]])
                        sp.dma_start(dst, src).then_inc(placed, 16)
                        n += 16
            sp.wait_ge(placed, n)
            half, m = GROUP // 2, 0
            for v in (1, 3):
                for off in (half * GROUP, half):
                    for part in (0, 28):
                        sp.dma_start(table(v, off + part * GROUP, [[GROUP, 28], [1, 28]]), d.negs).then_inc(masked, 16)
                        sp.dma_start(table(v, off + part * GROUP + 28, [[GROUP, 28], [1, 28]]),
                                     d.negs).then_inc(masked, 16)
                        m += 32
            sp.wait_ge(masked, m)
            for v in (2, 3):
                for r in range(WS):
                    for a, b in ((26, 24), (24, 26)):
                        dst = table(v, (r * HALFROW + a) * GROUP + b, [[GROUP, 2], [HALFROW, WS], [1, 2]])
                        sp.dma_start(dst, view(d.negs, 0, [[28, 2], [2, WS], [1, 2]])).then_inc(masked, 16)
                        m += 16
            sp.wait_ge(masked, m)

        @block.scalar
        def _(act):
            act.dma_start(rel[:, :], d.rpb).then_inc(rel_in, 16)
            act.wait_ge(edge_set, 1)
            act.dma_start(view(d.skew, 0, [[128 * 257, NH], [257, 128], [1, 255]]),
                          edge[:, :].unsqueeze(1).broadcast_to([NH, 128, 255])).then_inc(skewed, 16)
            act.wait_ge(skewed, 16)
            act.dma_start(corner[:, :, :], view(d.skew, 127, [[256, 128], [128 * 257, NH], [1, 128]])
                          ).then_inc(corner_in, 16)
            act.wait_ge(zero_set, 1)
            for g in range(G):
                act.dma_start(d.no_corner[g], zero[:, :, :, :]).then_inc(zero_out, 16)
            act.wait_ge(hi_set, 1)
            act.wait_ge(lo_set, 1)
            for g in range(G):
                act.dma_start(d.corner[g, :, 0], corner_hi[:, g * HG:(g + 1) * HG, :].bitcast(F32)).then_inc(corner_out, 16)
                act.dma_start(d.corner[g, :, 1], corner_lo[:, g * HG:(g + 1) * HG, :].bitcast(F32)).then_inc(corner_out, 16)
            act.wait_ge(corner_out, 16 * 2 * G)
            act.wait_ge(zero_out, 16 * G)

        @block.vector
        def _(dve):
            nc.vector.memset(neg[:, :, :], NEG).then_inc(neg_set, 1)
            nc.vector.memset(edge[:, :], 0.0).then_inc(edge_zero, 1)
            nc.vector.memset(zero[:, :, :, :], 0.0).then_inc(zero_set, 1)
            dve.wait_ge(rel_in, 16)
            dve.wait_ge(edge_zero, 1)
            nc.vector.tensor_scalar(edge[:, 0:REL], rel[:, :], rel[:, REL - 1:REL], None,
                                    ALU.subtract).then_inc(edge_set, 1)
            dve.wait_ge(corner_in, 16)
            nc.vector.tensor_copy(corner_hi[:, :, :], corner[:, :, :]).then_inc(hi_set, 1)
            dve.wait_ge(hi_set, 1)
            nc.vector.tensor_tensor(corner_lo[:, :, :], corner[:, :, :], corner_hi[:, :, :].bitcast(F32),
                                    ALU.subtract).then_inc(lo_set, 1)


def window_attention(nc, d):
    with ExitStack() as ctx:
        sb = lambda n, s, t=F32: ctx.enter_context(nc.sbuf_tensor(n, s, t))
        ps = lambda n, s: ctx.enter_context(nc.psum_tensor(n, s, F32))
        sems = []

        def sem(name):
            sems.append(ctx.enter_context(nc.semaphore(name)))
            return sems[-1]

        w = sb("w_qkv", [128, CT, 3 * C])
        bias_col = sb("bias_col", [128, 2 * CT])
        bias_v = sb("bias_v", [GROUP, C])
        ident = sb("ident", [128, 128])
        ones = sb("ones", [GROUP, DH])
        tab = sb("tab", [GROUP, 2, CT, GROUP])
        tab_odd = sb("tab_odd", [GROUP, 2, CT, GROUP])
        xT = [sb(f"xT{i}", [128, CT, UNIT]) for i in range(2)]
        qk = [sb(f"qk{i}", [128, 2 * CT, UNIT]) for i in range(2)]
        v = [sb(f"v{i}", [GROUP, 2, C]) for i in range(2)]
        logit = [sb(f"logit{i}", [GROUP, NH, GROUP]) for i in range(2)]
        prob = [sb(f"prob{i}", [GROUP, NH, GROUP]) for i in range(2)]
        probT = [sb(f"probT{i}", [GROUP, NH, GROUP]) for i in range(2)]
        top = [sb(f"top{i}", [GROUP, NH]) for i in range(2)]
        sums = [sb(f"sums{i}", [128, 2 * CT * GROUP]) for i in range(2)]
        rden = [sb(f"rden{i}", [128, CT, GROUP]) for i in range(2)]
        oT = [sb(f"oT{i}", [128, CT, UNIT]) for i in range(2)]
        ps_s = ps("ps_s", [GROUP, 4, 512])
        ps_t = ps("ps_t", [128, 2, 512])
        ps_q = ps("ps_q", [128, 2, 512])

        consts_in, id_zero, id_set, ones_set, odd_in = (
            sem("consts_in"), sem("id_zero"), sem("id_set"), sem("ones_set"), sem("odd_in"))
        x_in, qkv_ready = [sem(f"x_in{u}") for u in range(2)], sem("qkv_ready")
        qk_kept, v_kept = sem("qk_kept"), sem("v_kept")
        s_ready, logit_ready, top_ready, shifted, prob_ready = (
            sem("s_ready"), sem("logit_ready"), sem("top_ready"), sem("shifted"), sem("prob_ready"))
        t_ready, t_kept, o_ready, recip_ready, o_kept, o_out = (
            sem("t_ready"), sem("t_kept"), sem("o_ready"), sem("recip_ready"), sem("o_kept"),
            [sem(f"o_out{u}") for u in range(2)])
        normalized = sem("normalized")
        start_counts(nc, sems)
        block = ctx.enter_context(nc.Block())
        JOBS = 2 * CT + 2
        SCALE = 1.0 / float(DH) ** 0.5

        @block.sync
        def _(sp):
            sp.dma_start(w[:, :, :], d.w_tok.rearrange("(t p) n -> p t n", p=128)).then_inc(consts_in, 16)
            sp.dma_start(bias_col[:, :], d.b_tok[0:2 * C].rearrange("(t p) -> p t", p=128),
                         allow_slow_non_contiguous=True).then_inc(consts_in, 16)
            sp.dma_start(bias_v[:, :], view(d.b_tok, 2 * C, [[0, GROUP], [1, C]])).then_inc(consts_in, 16)
            for half in range(2):
                for c in range(CT):
                    sp.dma_start(tab[:, half, c, :], d.win_bias[2 * half]).then_inc(consts_in, 16)
            for u in range(2):
                sp.dma_start(xT[u][:, :, :], d.x[u]).then_inc(x_in[u], 16)

            def pair(m, last_row):
                sp.wait_ge(logit_ready, ONE + 4 * m)
                for half in range(2):
                    for c in range(CT):
                        sp.dma_start(tab_odd[:, half, c, :], d.win_bias[2 * half + last_row]).then_inc(odd_in, 16)

            def store(m, u):
                sp.wait_ge(normalized, ONE + 4 * m + 2 * u + 2)
                sp.dma_start(d.a1[2 * m + u], oT[u][:, :, :]).then_inc(o_out[u], 16)

            def load(m, u):
                sp.wait_ge(qkv_ready, ONE + JOBS * (2 * m + u + 1))
                sp.dma_start(xT[u][:, :, :], d.x[2 * m + u + 2]).then_inc(x_in[u], 16)

            def body(m, last_row, more):
                pair(m, last_row)
                if more:
                    load(m, 0)
                    load(m, 1)
                store(m, 0)
                store(m, 1)

            rows = UNITS // B // 2
            with sp.Fori(0, B - 1) as b:
                with sp.Fori(0, rows - 1) as r:
                    body(b * rows + r, 0, True)
                body(b * rows + rows - 1, 1, True)
            with sp.Fori(0, rows - 1) as r:
                body((B - 1) * rows + r, 0, True)
            body(B * rows - 1, 1, False)
            for u in range(2):
                sp.wait_ge(o_out[u], ONE + 8 * UNITS)

        @block.gpsimd
        def _(pool):
            nc.gpsimd.memset(ident[:, :], 0.0).then_inc(id_zero, 1)
            pool.wait_ge(id_zero, ONE + 1)
            nc.gpsimd.affine_select(out=ident[:, :], in_=ident[:, :], compare_op=ALU.not_equal, fill=1.0, base=0,
                                    pattern=[[-1, 128]], channel_multiplier=1).then_inc(id_set, 1)
            nc.gpsimd.memset(ones[:, :], 1.0).then_inc(ones_set, 1)

            def shift(k, p):
                pool.wait_ge(top_ready, ONE + k + 1)
                nc.gpsimd.tensor_tensor(logit[p][:, :, :], logit[p][:, :, :],
                                        top[p][:, :].unsqueeze(2).broadcast_to([GROUP, NH, GROUP]),
                                        ALU.subtract).then_inc(shifted, 1)

            with pool.Fori(0, UNITS // 2) as m:
                for k in range(4):
                    shift(4 * m + k, k % 2)

        @block.tensor
        def _(pe):
            pe.wait_ge(consts_in, ONE + 16 * (3 + 2 * CT))
            pe.wait_ge(id_set, ONE + 1)
            pe.wait_ge(ones_set, ONE + 1)

            def project_qk(n, u, jobs):
                pe.wait_ge(x_in[u], ONE + 8 * (n - u) + 16)
                for job in jobs:
                    if job < 2:
                        pe.wait_ge(v_kept, ONE + 2 * n)
                    else:
                        pe.wait_ge(qk_kept, ONE + 2 * CT * n + job - 1)
                    for c in range(CT):
                        mm = nc.tensor.matmul(ps_q[:, job % 2, 0:UNIT], w[:, c, job * 128:(job + 1) * 128],
                                              xT[u][:, c, :], start=(c == 0), stop=(c == CT - 1))
                    mm.then_inc(qkv_ready, 1)

            def project_v(n, u, half):
                pe.wait_ge(qk_kept, ONE + 2 * CT * n + 2 * CT - 1 + half)
                for c in range(CT):
                    x = xT[u][:, c, half * GROUP:(half + 1) * GROUP]
                    mm = nc.tensor.matmul(ps_q[0:GROUP, half, 0:C], x, w[:, c, 2 * C:3 * C],
                                          start=(c == 0), stop=(c == CT - 1))
                mm.then_inc(qkv_ready, 1)

            def scores(n, u, half):
                k = 2 * n + half
                pe.wait_ge(logit_ready, ONE + k)
                pe.wait_ge(qk_kept, ONE + 2 * CT * (n + 1))
                for c in range(CT):
                    for j in range(4):
                        rows = slice(32 * j, 32 * j + 32)
                        q = qk[u][rows, c, half * GROUP:(half + 1) * GROUP]
                        kk = qk[u][rows, CT + c, half * GROUP:(half + 1) * GROUP]
                        mm = nc.tensor.matmul(ps_s[:, j, c * GROUP:(c + 1) * GROUP], q, kk, start=True, stop=True)
                mm.then_inc(s_ready, 1)

            def turn(n, half):
                k = 2 * n + half
                pe.wait_ge(prob_ready, ONE + k + 1)
                pe.wait_ge(o_kept, ONE + k)
                for h in range(NH):
                    mm = nc.tensor.transpose(ps_t[0:GROUP, h // 4, (h % 4) * GROUP:(h % 4 + 1) * GROUP],
                                             prob[half][:, h, :], ident[0:GROUP, 0:GROUP])
                mm.then_inc(t_ready, 1)

            def weigh(n, u, half):
                k = 2 * n + half
                pe.wait_ge(t_kept, ONE + k + 1)
                pe.wait_ge(v_kept, ONE + 2 * (n + 1))
                for c in range(CT):
                    for j in range(4):
                        nc.tensor.matmul(ps_t[32 * j:32 * j + 32, 0, c * GROUP:(c + 1) * GROUP],
                                         v[u][:, half, (4 * c + j) * DH:(4 * c + j + 1) * DH],
                                         probT[half][:, 2 * j + c, :], start=True, stop=True)
                for c in range(CT):
                    for j in range(4):
                        mm = nc.tensor.matmul(ps_t[32 * j:32 * j + 32, 0, (CT + c) * GROUP:(CT + c + 1) * GROUP],
                                              ones[:, :], probT[half][:, 2 * j + c, :], start=True, stop=True)
                mm.then_inc(o_ready, 1)

            def unit(n, u, more):
                scores(n, u, 1)
                if more:
                    project_qk(n + 1, 1 - u, range(2 * CT - 1))
                turn(n, 0)
                if more:
                    project_qk(n + 1, 1 - u, [2 * CT - 1])
                    project_v(n + 1, 1 - u, 0)
                weigh(n, u, 0)
                if more:
                    project_v(n + 1, 1 - u, 1)
                turn(n, 1)
                if more:
                    scores(n + 1, 1 - u, 0)
                weigh(n, u, 1)

            project_qk(0, 0, range(2 * CT))
            project_v(0, 0, 0)
            project_v(0, 0, 1)
            scores(0, 0, 0)
            with pe.Fori(0, UNITS // 2 - 1) as m:
                unit(2 * m, 0, True)
                unit(2 * m + 1, 1, True)
            unit(UNITS - 2, 0, True)
            unit(UNITS - 1, 1, False)

        @block.vector
        def _(dve):
            dve.wait_ge(consts_in, ONE + 16 * (3 + 2 * CT))

            def logits(n, u, half):
                k = 2 * n + half
                dve.wait_ge(s_ready, ONE + k + 1)
                if u:
                    dve.wait_ge(odd_in, ONE + 16 * CT * (n + 1))
                table = (tab_odd if u else tab)[:, half, :, :].rearrange("p c k -> p (c k)")
                table = table.unsqueeze(1).broadcast_to([GROUP, 4, CT * GROUP])
                nc.vector.scalar_tensor_tensor(
                    out=logit[half][:, :, :].rearrange("p (j c) k -> p j (c k)", j=4),
                    in0=ps_s[:, :, 0:2 * GROUP], scalar=SCALE,
                    in1=table, op0=ALU.mult, op1=ALU.add).then_inc(logit_ready, 1)
                dve.wait_ge(logit_ready, ONE + k + 1)
                nc.vector.tensor_reduce(top[half][:, :], logit[half][:, :, :], AX.X, ALU.max).then_inc(top_ready, 1)

            def keep_v(n, u):
                for half in range(2):
                    dve.wait_ge(qkv_ready, ONE + JOBS * n + 2 * CT + 1 + half)
                    nc.vector.tensor_tensor(v[u][:, half, :], ps_q[0:GROUP, half, 0:C], bias_v[:, :],
                                            ALU.add).then_inc(v_kept, 1)

            def outputs(n, u, half):
                k = 2 * n + half
                dve.wait_ge(o_kept, ONE + k + 1)
                nc.vector.reciprocal(rden[half][:, :, :].rearrange("p c k -> p (c k)"),
                                     sums[half][:, CT * GROUP:2 * CT * GROUP]).then_inc(recip_ready, 1)
                dve.wait_ge(recip_ready, ONE + k + 1)
                if half == 0:
                    dve.wait_ge(o_out[u], ONE + 8 * (n - u))
                dst = oT[u][:, :, :].rearrange("p c (r h k) -> p c h r k", r=WS, h=2)[:, :, half]
                for c in range(CT):
                    ins = nc.vector.tensor_tensor(
                        dst[:, c], sums[half][:, c * GROUP:(c + 1) * GROUP].rearrange("p (r k) -> p r k", r=WS),
                        rden[half][:, c, :].rearrange("p (r k) -> p r k", r=WS), ALU.mult)
                ins.then_inc(normalized, 1)

            def unit(n, u, more):
                logits(n, u, 1)
                if more:
                    keep_v(n + 1, 1 - u)
                outputs(n, u, 0)
                if more:
                    logits(n + 1, 1 - u, 0)
                outputs(n, u, 1)

            keep_v(0, 0)
            logits(0, 0, 0)
            with dve.Fori(0, UNITS // 2 - 1) as m:
                unit(2 * m, 0, True)
                unit(2 * m + 1, 1, True)
            unit(UNITS - 2, 0, True)
            unit(UNITS - 1, 1, False)

        @block.scalar
        def _(act):
            act.wait_ge(consts_in, ONE + 16 * (3 + 2 * CT))

            def keep_qk(n, u, jobs):
                act.wait_ge(s_ready, ONE + 2 * (n - u))
                for job in jobs:
                    act.wait_ge(qkv_ready, ONE + JOBS * n + job + 1)
                    nc.scalar.activation(qk[u][:, job, :], ps_q[:, job % 2, 0:UNIT], ACT.Identity,
                                         bias=bias_col[:, job:job + 1]).then_inc(qk_kept, 1)

            def exps(n, half):
                k = 2 * n + half
                act.wait_ge(shifted, ONE + k + 1)
                nc.scalar.activation(prob[half][:, :, :], logit[half][:, :, :], ACT.Exp).then_inc(prob_ready, 1)

            def keep_t(n, half):
                k = 2 * n + half
                act.wait_ge(t_ready, ONE + k + 1)
                nc.scalar.activation(probT[half][:, :, :].rearrange("p (a h) k -> p a (h k)", a=2),
                                     ps_t[0:GROUP, :, 0:4 * GROUP], ACT.Copy).then_inc(t_kept, 1)

            def keep_sums(n, half):
                k = 2 * n + half
                act.wait_ge(o_ready, ONE + k + 1)
                act.wait_ge(normalized, ONE + k - half)
                nc.scalar.activation(sums[half][:, :], ps_t[:, 0, 0:2 * CT * GROUP], ACT.Copy).then_inc(o_kept, 1)

            def unit(n, u, more):
                if more:
                    keep_qk(n + 1, 1 - u, range(2 * CT - 1))
                keep_t(n, 0)
                if more:
                    keep_qk(n + 1, 1 - u, [2 * CT - 1])
                exps(n, 1)
                keep_sums(n, 0)
                keep_t(n, 1)
                keep_sums(n, 1)
                if more:
                    exps(n + 1, 0)

            keep_qk(0, 0, range(2 * CT))
            exps(0, 0)
            with act.Fori(0, UNITS // 2 - 1) as m:
                unit(2 * m, 0, True)
                unit(2 * m + 1, 1, True)
            unit(UNITS - 2, 0, True)
            unit(UNITS - 1, 1, False)


def project_qkv(nc, d):
    with ExitStack() as ctx:
        sb = lambda n, s, t=F32: ctx.enter_context(nc.sbuf_tensor(n, s, t))
        ps = lambda n, s: ctx.enter_context(nc.psum_tensor(n, s, F32))
        sems = []

        def sem(name):
            sems.append(ctx.enter_context(nc.semaphore(name)))
            return sems[-1]

        w_out = sb("w_out", [128, CT, C])
        w = sb("w_qkv2", [128, CT, 3 * C])
        bias_out = sb("bias_out", [QT, NQ, C])
        bias_v = sb("bias_v2", [QT, NQ, C])
        bias_col = sb("bias_col2", [128, 2 * CT])
        ident = sb("ident2", [128, 128])
        minus_half = sb("minus_half", [QT, NQ])
        aT = [sb(f"aT{i}", [128, 2, CT, UNIT]) for i in range(2)]
        h1 = sb("h1", [QT, NQ, C])
        stats = sb("stats", [QT, NQ, 6])
        both = sb("both", [QT, NQ, 2])
        apart, mean, within, between = (sb(n, [QT, NQ]) for n in ("apart", "mean", "within", "between"))
        veps = sb("veps", [QT, NQ])
        rstd = sb("rstd", [QT, NQ])
        xn = sb("xn", [QT, NQ, C])
        xnT = sb("xnT", [128, CT, CH])
        full = [sb(f"full{i}", [128, CH]) for i in range(2)]
        hi = [sb(f"hi{i}", [128, CH], F32R) for i in range(2)]
        lo = [sb(f"lo{i}", [128, CH], F32R) for i in range(2)]
        v = sb("v_rows", [QT, NQ, C])
        ps_h = ps("ps_h", [128, 2, 512])
        ps_x = ps("ps_x", [128, 2, 512])
        ps_q = ps("ps_q2", [128, 2, 512])
        ps_v = ps("ps_v", [128, 2, 512])
        consts_in, id_zero, id_set, half_set = sem("consts_in2"), sem("id_zero2"), sem("id_set2"), sem("half_set")
        a_in = [sem(f"a_in{i}") for i in range(2)]
        h_ready, h_kept, h_out = sem("h_ready"), sem("h_kept"), sem("h_out")
        stats_ready, mv_ready, veps_ready, rstd_ready, xn_ready = (
            sem("stats_ready"), sem("mv_ready"), sem("veps_ready"), sem("rstd_ready"), sem("xn_ready"))
        xT_ready, xT_kept, q_ready, full_ready, hi_ready, lo_ready, parts_out = (
            sem("xT_ready"), sem("xT_kept"), sem("q_ready"), sem("full_ready"), sem("hi_ready"), sem("lo_ready"),
            [sem(f"parts_out{i}") for i in range(2)])
        bias_set = sem("bias_set")
        v_ready, v_kept, v_out = sem("v_ready"), sem("v_kept2"), sem("v_out")
        start_counts(nc, sems)
        block = ctx.enter_context(nc.Block())
        QK = 2 * CT
        SCALE = float(DH) ** -0.5

        @block.sync
        def _(sp):
            sp.dma_start(w_out[:, :, :], d.w_tok_out.rearrange("(t p) n -> p t n", p=128)).then_inc(consts_in, 16)
            sp.dma_start(w[:, :, :], d.w_qkv.rearrange("(t p) n -> p t n", p=128)).then_inc(consts_in, 16)
            sp.dma_start(bias_col[:, :], d.b_qkv[0:2 * C].rearrange("(t p) -> p t", p=128),
                         allow_slow_non_contiguous=True).then_inc(consts_in, 16)
            sp.dma_start(bias_out[:, :, :], view(d.b_tok_out, 0, [[0, QT], [0, NQ], [1, C]])).then_inc(consts_in, 16)
            sp.dma_start(bias_v[:, :, :], view(d.b_qkv, 2 * C, [[0, QT], [0, NQ], [1, C]])).then_inc(consts_in, 16)

            def load(m, i):
                for u in range(2):
                    sp.dma_start(aT[i][:, u, :, :], d.a1[2 * m + u]).then_inc(a_in[i], 16)

            def stores(m):
                sp.wait_ge(h_kept, ONE + 2 * m + 2)
                sp.dma_start(d.h1[m], h1[:, :, :]).then_inc(h_out, 16)
                for job in range(QK):
                    sp.wait_ge(hi_ready, ONE + QK * m + job + 1)
                    sp.dma_start((d.q, d.k)[job // CT][m, job % CT, 0], hi[job % 2][:, :].bitcast(F32)).then_inc(parts_out[job % 2], 16)
                    sp.wait_ge(lo_ready, ONE + QK * m + job + 1)
                    sp.dma_start((d.q, d.k)[job // CT][m, job % CT, 1], lo[job % 2][:, :].bitcast(F32)).then_inc(parts_out[job % 2], 16)
                sp.wait_ge(v_kept, ONE + 2 * m + 2)
                sp.dma_start(d.v[m].rearrange("(i p) c -> p i c", p=QT), v[:, :, :]).then_inc(v_out, 16)

            load(0, 0)
            load(1, 1)
            with sp.Fori(0, CHUNKS // 2 - 1) as m2:
                for i in range(2):
                    m = 2 * m2 + i
                    sp.wait_ge(h_ready, ONE + 2 * m + 2)
                    load(m + 2, i)
                    stores(m)
            stores(CHUNKS - 2)
            stores(CHUNKS - 1)
            sp.wait_ge(h_out, ONE + 16 * CHUNKS)
            for i in range(2):
                sp.wait_ge(parts_out[i], ONE + 16 * QK * CHUNKS)
            sp.wait_ge(v_out, ONE + 16 * CHUNKS)

        @block.gpsimd
        def _(pool):
            nc.gpsimd.memset(ident[:, :], 0.0).then_inc(id_zero, 1)
            pool.wait_ge(id_zero, ONE + 1)
            nc.gpsimd.affine_select(out=ident[:, :], in_=ident[:, :], compare_op=ALU.not_equal, fill=1.0, base=0,
                                    pattern=[[-1, 128]], channel_multiplier=1).then_inc(id_set, 1)
            nc.gpsimd.memset(minus_half[:, :], -0.5).then_inc(half_set, 1)
            pool.wait_ge(half_set, ONE + 1)

            def root(m):
                pool.wait_ge(veps_ready, ONE + m + 1)
                nc.gpsimd.tensor_tensor(rstd[:, :], veps[:, :], minus_half[:, :], ALU.pow).then_inc(rstd_ready, 1)

            def low(m, job):
                pool.wait_ge(hi_ready, ONE + QK * m + job + 1)
                pool.wait_ge(parts_out[job % 2], ONE + 32 * (QK // 2 * m + job // 2))
                nc.gpsimd.tensor_tensor(lo[job % 2][:, :], full[job % 2][:, :], hi[job % 2][:, :].bitcast(F32),
                                        ALU.subtract).then_inc(lo_ready, 1)

            root(0)
            with pool.Fori(0, CHUNKS - 1) as m:
                root(m + 1)
                for job in range(QK):
                    low(m, job)
            for job in range(QK):
                low(CHUNKS - 1, job)

        @block.tensor
        def _(pe):
            pe.wait_ge(consts_in, ONE + 16 * 5)
            pe.wait_ge(id_set, ONE + 1)

            def hidden(m, i):
                pe.wait_ge(a_in[i], ONE + 16 * (m - i) + 32)
                pe.wait_ge(h_kept, ONE + 2 * m)
                for r in range(NQ):
                    for c in range(CT):
                        mm = nc.tensor.matmul(ps_h[0:QT, r // 2, (r % 2) * C:(r % 2 + 1) * C],
                                              aT[i][:, r // 2, c, (r % 2) * QT:(r % 2 + 1) * QT], w_out[:, c, :],
                                              start=(c == 0), stop=(c == CT - 1))
                    if r % 2:
                        mm.then_inc(h_ready, 1)

            def turn(m):
                pe.wait_ge(xn_ready, ONE + NQ * (m + 1))
                pe.wait_ge(xT_kept, ONE + CT * m)
                for c in range(CT):
                    for r in range(NQ):
                        mm = nc.tensor.transpose(ps_x[:, c, r * QT:(r + 1) * QT], xn[:, r, c * 128:(c + 1) * 128],
                                                 ident[0:QT, 0:QT])
                    mm.then_inc(xT_ready, 1)

            def project(m):
                pe.wait_ge(xT_kept, ONE + CT * (m + 1))
                for job in range(QK):
                    pe.wait_ge(full_ready, ONE + QK * m + job - job % 2)
                    for c in range(CT):
                        mm = nc.tensor.matmul(ps_q[:, job % 2, 0:CH], w[:, c, job * 128:(job + 1) * 128],
                                              xnT[:, c, :], start=(c == 0), stop=(c == CT - 1))
                    mm.then_inc(q_ready, 1)
                pe.wait_ge(v_kept, ONE + 2 * m)
                for r in range(NQ):
                    for c in range(CT):
                        mm = nc.tensor.matmul(ps_v[0:QT, r // 2, (r % 2) * C:(r % 2 + 1) * C],
                                              xnT[:, c, r * QT:(r + 1) * QT], w[:, c, 2 * C:3 * C],
                                              start=(c == 0), stop=(c == CT - 1))
                    if r % 2:
                        mm.then_inc(v_ready, 1)

            hidden(0, 0)
            turn(0)
            hidden(1, 1)
            project(0)
            turn(1)
            with pe.Fori(0, CHUNKS // 2 - 1) as m2:
                for i in range(2):
                    hidden(2 * m2 + i + 2, i)
                    project(2 * m2 + i + 1)
                    turn(2 * m2 + i + 2)
            project(CHUNKS - 1)

        @block.vector
        def _(dve):
            dve.wait_ge(consts_in, ONE + 16 * 5)

            def norm(m):
                dve.wait_ge(h_out, ONE + 16 * m)
                for a in range(2):
                    dve.wait_ge(h_ready, ONE + 2 * m + a + 1)
                    nc.vector.tensor_tensor(h1[:, 2 * a:2 * a + 2, :].rearrange("p r c -> p (r c)"), ps_h[0:QT, a, :],
                                            bias_out[:, 0:2, :].rearrange("p r c -> p (r c)"),
                                            ALU.add).then_inc(h_kept, 1)
                dve.wait_ge(h_kept, ONE + 2 * m + 2)
                for r in range(NQ):
                    nc.vector.bn_stats(stats[:, r, :], h1[:, r, :]).then_inc(stats_ready, 1)
                dve.wait_ge(stats_ready, ONE + NQ * (m + 1))
                nc.vector.tensor_tensor(both[:, :, :], stats[:, :, 1:3], stats[:, :, 4:6], ALU.add).then_inc(mv_ready, 1)
                nc.vector.tensor_tensor(apart[:, :], stats[:, :, 1], stats[:, :, 4], ALU.subtract).then_inc(mv_ready, 1)
                dve.wait_ge(mv_ready, ONE + 5 * m + 2)
                nc.vector.tensor_scalar(mean[:, :], both[:, :, 0], 0.5, None, ALU.mult).then_inc(mv_ready, 1)
                nc.vector.tensor_scalar(within[:, :], both[:, :, 1], 1.0 / C, EPS, ALU.mult,
                                        ALU.add).then_inc(mv_ready, 1)
                nc.vector.scalar_tensor_tensor(out=between[:, :], in0=apart[:, :], scalar=0.25, in1=apart[:, :],
                                               op0=ALU.mult, op1=ALU.mult).then_inc(mv_ready, 1)
                dve.wait_ge(mv_ready, ONE + 5 * (m + 1))
                nc.vector.tensor_tensor(veps[:, :], within[:, :], between[:, :], ALU.add).then_inc(veps_ready, 1)
                dve.wait_ge(rstd_ready, ONE + m + 1)
                dve.wait_ge(xT_ready, ONE + CT * m)
                for r in range(NQ):
                    nc.vector.tensor_scalar(xn[:, r, :], h1[:, r, :], mean[:, r:r + 1], rstd[:, r:r + 1],
                                            ALU.subtract, ALU.mult).then_inc(xn_ready, 1)

            def high(m):
                for job in range(QK):
                    dve.wait_ge(full_ready, ONE + QK * m + job + 1)
                    dve.wait_ge(lo_ready, ONE + QK * m + job - job % 2)
                    dve.wait_ge(parts_out[job % 2], ONE + 32 * (QK // 2 * m + job // 2))
                    nc.vector.tensor_copy(hi[job % 2][:, :], full[job % 2][:, :]).then_inc(hi_ready, 1)

            def keep_v(m):
                dve.wait_ge(v_out, ONE + 16 * m)
                for a in range(2):
                    dve.wait_ge(v_ready, ONE + 2 * m + a + 1)
                    nc.vector.tensor_tensor(v[:, 2 * a:2 * a + 2, :].rearrange("p r c -> p (r c)"), ps_v[0:QT, a, :],
                                            bias_v[:, 0:2, :].rearrange("p r c -> p (r c)"),
                                            ALU.add).then_inc(v_kept, 1)

            nc.vector.tensor_scalar(bias_col[:, 0:CT], bias_col[:, 0:CT], SCALE, None, ALU.mult).then_inc(bias_set, 1)
            norm(0)
            with dve.Fori(0, CHUNKS - 1) as m:
                norm(m + 1)
                high(m)
                keep_v(m)
            high(CHUNKS - 1)
            keep_v(CHUNKS - 1)

        @block.scalar
        def _(act):
            def keep_xT(m):
                act.wait_ge(v_ready, ONE + 2 * m)
                for c in range(CT):
                    act.wait_ge(xT_ready, ONE + CT * m + c + 1)
                    nc.scalar.activation(xnT[:, c, :], ps_x[:, c, 0:CH], ACT.Copy).then_inc(xT_kept, 1)

            def keep(m):
                for job in range(QK):
                    act.wait_ge(q_ready, ONE + QK * m + job + 1)
                    act.wait_ge(lo_ready, ONE + QK * m + job - job % 2)
                    nc.scalar.activation(full[job % 2][:, :], ps_q[:, job % 2, 0:CH], ACT.Identity,
                                         bias=bias_col[:, job:job + 1],
                                         scale=SCALE if job < CT else 1.0).then_inc(full_ready, 1)

            act.wait_ge(bias_set, ONE + 1)
            keep_xT(0)
            with act.Fori(0, CHUNKS - 1) as m:
                keep(m)
                keep_xT(m + 1)
            keep(CHUNKS - 1)


def full_attention(nc, d):
    with ExitStack() as ctx:
        sb = lambda n, s, t=F32: ctx.enter_context(nc.sbuf_tensor(n, s, t))
        ps = lambda n, s: ctx.enter_context(nc.psum_tensor(n, s, F32))
        sems = []

        def sem(name):
            sems.append(ctx.enter_context(nc.semaphore(name)))
            return sems[-1]

        keys = [sb(f"keys{g}", [STACK + 1, HG, N], F32R) for g in range(G)]
        queries = [sb(f"queries{g}", [STACK + 1, HG, CH], F32R) for g in range(G)]
        values = [sb(f"values{g}", [128, KT, HG * DH]) for g in range(G)]
        corner_hi = [sb(f"corner_hi3{g}", [128, HG, 2 * QT], F32R) for g in range(G)]
        corner_lo = [sb(f"corner_lo3{g}", [128, HG, 128], F32R) for g in range(G)]
        prob = sb("prob3", [128, SLOTS, HG, CH])
        pair_sum = [sb(f"pair_sum{i}", [128, HG, CH]) for i in range(2)]
        ident = sb("ident3", [128, 128])
        ident_r = sb("ident_r", [128, 128], F32R)
        ones = sb("ones3", [128, 2, DH])
        tops = sb("tops", [QT, HG * NQ, PER_IMAGE])
        shift = sb("shift", [QT, HG * NQ])
        shift_rows = [sb(f"shift_rows{p}", [HG * NQ // 2, QT], F32R) for p in range(2)]
        den = sb("den3", [128, CH])
        out = [sb(f"out{i}", [128, CH]) for i in range(G)]
        SB = 3
        MB = 3
        ps_s = ps("ps_s3", [128, SB, 512])
        ps_m = ps("ps_m", [128, MB, 512])
        ps_o = ps("ps_o", [128, 512])
        ps_d = ps("ps_d", [128, 512])
        s_ready, exp_done, tile_used, d_used, summed = (
            sem("s_ready3"), sem("exp_done"), sem("tile_used"), sem("d_used"), sem("summed"))
        m_ready, m_used, tops_ready = sem("m_ready"), sem("m_used"), sem("tops_ready")
        id_zero, id_set, idr_set, ones_set = sem("id_zero3"), sem("id_set3"), sem("idr_set"), sem("ones_set3")
        k_in, q_in = [sem(f"k_in{g}") for g in range(G)], [sem(f"q_in{g}") for g in range(G)]
        shift_ready, rows_ready, rows_kept = sem("shift_ready"), sem("rows_ready"), sem("rows_kept")
        shift_in = [sem(f"shift_in{p}") for p in range(2)]
        o_kept, den_kept, recip_done, out_ready = sem("o_kept3"), sem("den_kept"), sem("recip_done"), sem("out_ready")
        out_out = [sem(f"out_out{g}") for g in range(G)]
        HALVES = G * CHUNKS
        TILES = HG * KT
        MAXES = HG * NQ * PER_IMAGE
        PAIRED = (KT - 1) // 2
        D_ITEMS = PAIRED + 1
        BEHIND = SLOTS - 1
        RECIPS = 4
        TURNS = (MAXES // 2 + 4, MAXES)
        start_counts(nc, sems, {tile_used: BEHIND})

        block = ctx.enter_context(nc.Block())

        def keys_of(t):
            return (0, FIRST) if t == 0 else (FIRST + 128 * (t - 1), 128)

        @block.sync
        def _(sp):
            def scored(n, g):
                sp.wait_ge(s_ready, ONE + TILES * (2 * n + g - 1))

            def load_keys(b, g):
                if b is not FIRST_IMAGE:
                    scored(b * PER_IMAGE, g)
                for c in range(PER_IMAGE):
                    for row, part in ((0, 0), (DH, 1), (2 * DH, 0)):
                        src = d.k[b * PER_IMAGE + c, g, part].rearrange("(j d) n -> d j n", j=HG)
                        sp.dma_start(keys[g][row:row + DH, :, c * CH:(c + 1) * CH].bitcast(F32), src
                                     ).then_inc(k_in[g], 16)

            def load_values(b, g):
                if b is not FIRST_IMAGE:
                    sp.wait_ge(tile_used, ONE + BEHIND + KT * (2 * PER_IMAGE * b - 1 + g))
                cols = slice(g * HG * DH, (g + 1) * HG * DH)
                sp.dma_start(values[g][0:FIRST, 0, :], d.v_rows[b, 0:FIRST, cols]).then_inc(k_in[g], 16)
                sp.dma_start(values[g][:, 1:KT, :],
                             d.v_rows[b, FIRST:N, cols].rearrange("(t p) c -> p t c", p=128)).then_inc(k_in[g], 16)
                sp.wait_ge(k_in[g], ONE + 16 * (3 * PER_IMAGE + 2) * (b + 1))

            def load_queries(n, g, corner_or_zero):
                if n is not FIRST_IMAGE:
                    scored(n, g)
                for row, part in ((0, 0), (DH, 0), (2 * DH, 1)):
                    sp.dma_start(queries[g][row:row + DH, :, :].bitcast(F32),
                                 d.q[n, g, part].rearrange("(j d) n -> d j n", j=HG)).then_inc(q_in[g], 16)
                sp.dma_start(corner_hi[g][:, :, 0:128].bitcast(F32), corner_or_zero[g, :, 0]).then_inc(q_in[g], 16)
                sp.dma_start(corner_lo[g][:, :, :].bitcast(F32), corner_or_zero[g, :, 1]).then_inc(q_in[g], 16)

            def shifts(h, g):
                for p in range(2):
                    sp.wait_ge(rows_kept, ONE + 2 * h + p + 1)
                    sp.dma_start(queries[g][STACK:STACK + 1, 2 * p:2 * p + 2, :].rearrange("p j n -> p (j n)"
                                                                                            ).bitcast(F32),
                                 shift_rows[p][:, :].bitcast(F32)).then_inc(shift_in[p], 16)

            def store(h, g):
                sp.wait_ge(out_ready, ONE + h + 1)
                sp.dma_start(d.a2[h], out[g][:, :]).then_inc(out_out[g], 16)

            def chunk(b, n, first_of_image, corner_or_zero):
                for g in range(G):
                    if first_of_image:
                        load_keys(b, g)
                        load_values(b, g)
                    load_queries(n, g, corner_or_zero)
                    if n is not FIRST_IMAGE:
                        store(2 * n - 2 + g, g)
                    shifts(2 * n + g, g)

            FIRST_IMAGE = 0
            chunk(FIRST_IMAGE, FIRST_IMAGE, True, d.corner)
            with sp.Fori(1, PER_IMAGE) as c:
                chunk(FIRST_IMAGE, c, False, d.no_corner)
            with sp.Fori(1, B) as b:
                chunk(b, b * PER_IMAGE, True, d.corner)
                with sp.Fori(1, PER_IMAGE) as c:
                    chunk(b, b * PER_IMAGE + c, False, d.no_corner)
            for g in range(G):
                store(HALVES - G + g, g)
            for g in range(G):
                sp.wait_ge(out_out[g], ONE + 16 * CHUNKS)

        @block.gpsimd
        def _(pool):
            nc.gpsimd.memset(ident[:, :], 0.0).then_inc(id_zero, 1)
            pool.wait_ge(id_zero, ONE + 1)
            nc.gpsimd.affine_select(out=ident[:, :], in_=ident[:, :], compare_op=ALU.not_equal, fill=1.0, base=0,
                                    pattern=[[-1, 128]], channel_multiplier=1).then_inc(id_set, 1)
            pool.wait_ge(id_set, ONE + 1)
            nc.gpsimd.tensor_copy(ident_r[:, :], ident[:, :]).then_inc(idr_set, 1)
            nc.gpsimd.memset(ones[:, 1, :], 1.0).then_inc(ones_set, 1)
            for g in range(G):
                nc.gpsimd.memset(corner_hi[g][:, :, 128:2 * QT].bitcast(F32), 0.0).then_inc(ones_set, 1)

            def add(h, k):
                pool.wait_ge(exp_done, ONE + h * TILES + HG * (2 * k + 1))
                pool.wait_ge(d_used, ONE + h * D_ITEMS + (k - 1 if k > 2 else 0))
                nc.gpsimd.tensor_tensor(pair_sum[k % 2][:, :, :], prob[:, (2 * k - 1) % SLOTS, :, :],
                                        prob[:, 2 * k % SLOTS, :, :], ALU.add).then_inc(summed, 1)

            with pool.Fori(0, HALVES) as h:
                for k in range(1, PAIRED + 1):
                    add(h, k)

        @block.tensor
        def _(pe):
            pe.wait_ge(idr_set, ONE + 1)
            pe.wait_ge(ones_set, ONE + 4 + 3 * G)

            def score(h, g, t, j):
                at, k = keys_of(t)
                i = HG * t + j
                if t == 0 and j % 2 == 0:
                    pe.wait_ge(shift_in[j // 2], ONE + 16 * (h + 1))
                pe.wait_ge(exp_done, ONE + h * TILES + max(0, i - SB + 1))
                o = ps_s[0:k, i % SB, :]
                last = t == KT - 1
                mm = nc.tensor.matmul(o[:, 0:CH], keys[g][:, j, at:at + k], queries[g][:, j, :],
                                      start=True, stop=not last, skip_group_check=last)
                if last:
                    for part in (corner_hi, corner_lo):
                        mm = nc.tensor.matmul(o[:, 0:128], ident_r[:, :], part[g][:, j, 0:128],
                                              start=False, stop=part is corner_lo, skip_group_check=True)
                mm.then_inc(s_ready, 1)

            def weigh(h, g, t):
                pe.wait_ge(exp_done, ONE + h * TILES + HG * (t + 1))
                if t == 0:
                    pe.wait_ge(o_kept, ONE + h)
                for j in range(HG):
                    mm = nc.tensor.matmul(ps_o[j * DH:(j + 1) * DH, 0:CH], values[g][:, t, j * DH:(j + 1) * DH],
                                          prob[:, t % SLOTS, j, :], start=(t == 0), stop=(t == KT - 1))
                mm.then_inc(tile_used, 1)

            def total(h, k):
                if k == 0:
                    pe.wait_ge(den_kept, ONE + h)
                else:
                    pe.wait_ge(summed, ONE + h * PAIRED + k)
                for j in range(HG):
                    moving = prob[:, 0, j, :] if k == 0 else pair_sum[k % 2][:, j, :]
                    mm = nc.tensor.matmul(ps_d[j * DH:(j + 1) * DH, 0:CH], ones[:, int(k > 0), :], moving,
                                          start=(k == 0), stop=(k == PAIRED))
                mm.then_inc(d_used, 1)

            def maximum(h, g, chunk, i):
                if i == 0:
                    pe.wait_ge(q_in[g], ONE + 80 * (chunk + 1))
                j, r, c = i // (NQ * PER_IMAGE), i // PER_IMAGE % NQ, i % PER_IMAGE
                if i in (0, TURNS[0] + MB - 1):
                    pe.wait_ge(rows_kept, ONE + 2 * h + int(i > 0))
                pe.wait_ge(m_used, ONE + h * MAXES + max(0, i - MB + 1))
                o = ps_m[0:QT, i % MB, :]
                last = c == PER_IMAGE - 1 and r < 2
                mm = nc.tensor.matmul(o[:, 0:CH], queries[g][0:STACK, j, r * QT:(r + 1) * QT],
                                      keys[g][0:STACK, j, c * CH:(c + 1) * CH],
                                      start=True, stop=not last, skip_group_check=last)
                if last:
                    mm = nc.tensor.matmul(o[:, CH - 128:CH], corner_hi[g][:, j, r * QT:(r + 1) * QT],
                                          ident_r[:, :], start=False, stop=True, skip_group_check=True)
                mm.then_inc(m_ready, 1)

            def turn(h, p):
                pe.wait_ge(shift_ready, ONE + 2 * h + p + 1)
                pe.wait_ge(m_used, ONE + h * MAXES + TURNS[p])
                nc.tensor.transpose(ps_m[0:HG * NQ // 2, (TURNS[p] - 1) % MB, 0:QT],
                                    shift[:, p * HG * NQ // 2:(p + 1) * HG * NQ // 2],
                                    ident[0:QT, 0:QT]).then_inc(rows_ready, 1)

            SPREAD = 6
            LEAD, TAIL = 2, 2

            def half(h, g, chunk_next, has_next, has_before):
                done, turned = 0, 0
                slots = 0
                total_slots = SPREAD * (KT - LEAD - TAIL)

                def spread():
                    nonlocal done, turned, slots
                    if not has_next or t < LEAD:
                        return
                    slots += 1
                    while done < min(MAXES, -(-MAXES * slots // total_slots)):
                        if turned == 0 and done == TURNS[0]:
                            turn(h + 1, 0)
                            turned = 1
                        maximum(h + 1, 1 - g, chunk_next, done)
                        done += 1

                for t in range(KT):
                    score(h, g, t, 0)
                    spread()
                    score(h, g, t, 1)
                    spread()
                    score(h, g, t, 2)
                    spread()
                    if t > 0:
                        weigh(h, g, t - 1)
                    elif has_before:
                        weigh(h - 1, 1 - g, KT - 1)
                    spread()
                    score(h, g, t, 3)
                    spread()
                    if has_next and t == KT - TAIL:
                        turn(h + 1, 1)
                    if t in (0, 2) and has_before:
                        total(h - 1, PAIRED - 1 + t // 2)
                    if t == 4:
                        total(h, 0)
                    if t >= 5 and t % 2:
                        total(h, (t - 3) // 2)
                    spread()

            for i in range(MAXES):
                if i == TURNS[0]:
                    turn(0, 0)
                maximum(0, 0, 0, i)
            turn(0, 1)
            half(0, 0, 0, True, False)
            with pe.Fori(0, CHUNKS - 1) as n:
                half(2 * n + 1, 1, n + 1, True, True)
                half(2 * n + 2, 0, n + 1, True, True)
            half(HALVES - 1, 1, 0, False, True)
            weigh(HALVES - 1, 1, KT - 1)
            total(HALVES - 1, PAIRED - 1)
            total(HALVES - 1, PAIRED)

        @block.scalar
        def _(act):
            def keep_den(h):
                act.wait_ge(d_used, ONE + D_ITEMS * (h + 1))
                act.wait_ge(out_ready, ONE + h)
                nc.scalar.activation(den[:, :], ps_d[:, 0:CH], ACT.Copy).then_inc(den_kept, 1)

            def half(h, has_before):
                for t in range(KT):
                    at, k = keys_of(t)
                    act.wait_ge(tile_used, ONE + h * KT + t)
                    if t > SLOTS:
                        act.wait_ge(summed, ONE + h * PAIRED + (t - SLOTS + 1) // 2)
                    elif t == SLOTS:
                        act.wait_ge(d_used, ONE + h * D_ITEMS + 1)
                    elif has_before:
                        act.wait_ge(summed, ONE + (h - 1) * PAIRED + (t + KT - SLOTS + 1) // 2)
                    for j in range(HG):
                        i = HG * t + j
                        act.wait_ge(s_ready, ONE + h * TILES + i + 1)
                        nc.scalar.activation(prob[0:k, t % SLOTS, j, :], ps_s[0:k, i % SB, 0:CH],
                                             ACT.Exp).then_inc(exp_done, 1)
                    if t == 3 and has_before:
                        keep_den(h - 1)

            half(0, False)
            with act.Fori(1, HALVES) as h:
                half(h, True)
            keep_den(HALVES - 1)

        @block.vector
        def _(dve):
            half_max = MAXES // 2

            def maximum(h, i):
                dve.wait_ge(m_ready, ONE + h * MAXES + i + 1)
                nc.vector.tensor_reduce(tops[:, i // PER_IMAGE, i % PER_IMAGE:i % PER_IMAGE + 1],
                                        ps_m[0:QT, i % MB, 0:CH], AX.X, ALU.max).then_inc(m_used, 1)
                if i % half_max == half_max - 1:
                    p = i // half_max
                    rows = slice(p * HG * NQ // 2, (p + 1) * HG * NQ // 2)
                    dve.wait_ge(m_used, ONE + h * MAXES + i + 1)
                    nc.vector.tensor_reduce(shift[:, rows], tops[:, rows, :], AX.X, ALU.max,
                                            negate=True).then_inc(shift_ready, 1)
                if i + 1 in TURNS:
                    p = TURNS.index(i + 1)
                    dve.wait_ge(rows_ready, ONE + 2 * h + p + 1)
                    dve.wait_ge(shift_in[p], ONE + 16 * h)
                    nc.vector.tensor_copy(shift_rows[p][:, :], ps_m[0:HG * NQ // 2, i % MB, 0:QT]
                                          ).then_inc(rows_kept, 1)

            def keep_out(h, g):
                dve.wait_ge(tile_used, ONE + BEHIND + KT * (h + 1))
                dve.wait_ge(out_out[g], ONE + 8 * (h - g))
                nc.vector.tensor_copy(out[g][:, :], ps_o[:, 0:CH]).then_inc(o_kept, 1)

            def recip(h, piece):
                w = CH // RECIPS
                if piece == 0:
                    dve.wait_ge(den_kept, ONE + h + 1)
                nc.vector.reciprocal(den[:, piece * w:(piece + 1) * w],
                                     den[:, piece * w:(piece + 1) * w]).then_inc(recip_done, 1)

            def normalize(h, g):
                dve.wait_ge(recip_done, ONE + RECIPS * (h + 1))
                nc.vector.tensor_tensor(out[g][:, :], out[g][:, :], den[:, :], ALU.mult).then_inc(out_ready, 1)

            def half(h, g):
                keep_out(h, g)
                for i in range(MAXES):
                    maximum(h + 2, i)
                    if i in (22, 24, 26, 28):
                        recip(h, (i - 22) // 2)
                    if i == 30:
                        normalize(h, g)

            nc.vector.memset(ones[0:FIRST, 0, :], 1.0).then_inc(ones_set, 1)
            nc.vector.memset(ones[FIRST:128, 0, :], 0.0).then_inc(ones_set, 1)
            nc.vector.memset(prob[FIRST:128, 0, :, :], 0.0).then_inc(ones_set, 1)
            for g in range(G):
                nc.vector.memset(values[g][FIRST:128, 0, :], 0.0).then_inc(ones_set, 1)
                nc.vector.memset(keys[g][STACK:STACK + 1, :, :].bitcast(F32), 1.0).then_inc(ones_set, 1)
            for h in range(2):
                for i in range(MAXES):
                    maximum(h, i)
            with dve.Fori(0, CHUNKS - 1) as n:
                half(2 * n, 0)
                half(2 * n + 1, 1)
            for h, g in ((HALVES - 2, 0), (HALVES - 1, 1)):
                keep_out(h, g)
                for piece in range(RECIPS):
                    recip(h, piece)
                normalize(h, g)


def gated_ffn(nc, d):
    with ExitStack() as outer:
        osb = lambda n, s, t=F32: outer.enter_context(nc.sbuf_tensor(n, s, t))
        xnT = osb("xnT4", [128, CHUNKS, CT, CH])
        gate = osb("gate", [QT, B, PER_IMAGE * NQ])
        coef = osb("coef", [QT, B, PER_IMAGE * NQ])
        project_out(nc, d, xnT, gate)
        rank_gates(nc, d, gate, coef)
        ffn(nc, d, xnT, coef)


def project_out(nc, d, xnT, gate):
    with ExitStack() as ctx:
        sb = lambda n, s, t=F32: ctx.enter_context(nc.sbuf_tensor(n, s, t))
        ps = lambda n, s: ctx.enter_context(nc.psum_tensor(n, s, F32))
        sems = []

        def sem(name):
            sems.append(ctx.enter_context(nc.semaphore(name)))
            return sems[-1]

        w = sb("w_proj", [128, CT, C])
        bias = sb("bias_proj", [QT, NQ, C])
        w_gate = sb("w_gate", [QT, C])
        b_gate = sb("b_gate", [QT, 1])
        ident = sb("ident4", [128, 128])
        minus_half = sb("minus_half4", [QT, NQ])
        aT = [sb(f"aT4{i}", [128, G, CH]) for i in range(2)]
        h1 = [sb(f"h1b{i}", [QT, NQ, C]) for i in range(2)]
        h1b = sb("h1_biased", [QT, NQ, C])
        h2 = sb("h2", [QT, NQ, C])
        stats = sb("stats4", [QT, NQ, 6])
        both = sb("both4", [QT, NQ, 2])
        apart, mean, within, between = (sb(n, [QT, NQ]) for n in ("apart4", "mean4", "within4", "between4"))
        veps = sb("veps4", [QT, NQ])
        rstd = sb("rstd4", [QT, NQ])
        xn = sb("xn4", [QT, NQ, C])
        base = sb("base", [QT, NQ, C])
        product = sb("product", [QT, NQ, C])
        dots = sb("dots", [QT, NQ])
        ps_h = ps("ps_h4", [128, 2, 512])
        ps_x = ps("ps_x4", [128, 2, 512])
        consts_in, id_zero, id_set, half_set = sem("consts_in4"), sem("id_zero4"), sem("id_set4"), sem("half_set4")
        a_in = [sem(f"a_in4{i}") for i in range(2)]
        biased, h_ready, h_kept = sem("biased"), sem("h_ready4"), sem("h_kept4")
        stats_ready, mv_ready, veps_ready, rstd_ready, xn_ready = (
            sem("stats_ready4"), sem("mv_ready4"), sem("veps_ready4"), sem("rstd_ready4"), sem("xn_ready4"))
        xT_ready, xT_kept, base_ready, base_out = (
            sem("xT_ready4"), sem("xT_kept4"), sem("base_ready"), sem("base_out"))
        dots_ready, gate_ready, gate_out = sem("dots_ready"), sem("gate_ready"), sem("gate_out")
        start_counts(nc, sems)
        block = ctx.enter_context(nc.Block())

        @block.sync
        def _(sp):
            sp.dma_start(w[:, :, :], d.w_proj.rearrange("(t p) n -> p t n", p=128)).then_inc(consts_in, 16)
            sp.dma_start(bias[:, :, :], view(d.b_proj, 0, [[0, QT], [0, NQ], [1, C]])).then_inc(consts_in, 16)
            sp.dma_start(w_gate[:, :], view(d.w_gate, 0, [[0, QT], [1, C]])).then_inc(consts_in, 16)
            sp.dma_start(b_gate[:, :], view(d.b_gate, 0, [[0, QT], [1, 1]])).then_inc(consts_in, 16)

            def load(m, i):
                for g in range(G):
                    sp.dma_start(aT[i][:, g, :], d.a2[2 * m + g]).then_inc(a_in[i], 16)
                sp.dma_start(h1[i][:, :, :], d.h1[m]).then_inc(a_in[i], 16)

            def store(m):
                sp.wait_ge(base_ready, ONE + m + 1)
                sp.dma_start(d.base[m], base[:, :, :]).then_inc(base_out, 16)

            load(0, 0)
            load(1, 1)
            with sp.Fori(0, CHUNKS // 2 - 1) as m2:
                for i in range(2):
                    m = 2 * m2 + i
                    sp.wait_ge(biased, ONE + m + 1)
                    sp.wait_ge(h_ready, ONE + 2 * m + 2)
                    load(m + 2, i)
                    store(m)
            store(CHUNKS - 2)
            store(CHUNKS - 1)
            sp.wait_ge(base_out, ONE + 16 * CHUNKS)
            sp.wait_ge(gate_ready, ONE + CHUNKS)
            for b in range(B):
                sp.dma_start(d.gate[b].rearrange("(i p) -> p i", p=QT), gate[:, b, :],
                             allow_slow_non_contiguous=True).then_inc(gate_out, 16)
            sp.wait_ge(gate_out, ONE + 16 * B)

        @block.gpsimd
        def _(pool):
            nc.gpsimd.memset(ident[:, :], 0.0).then_inc(id_zero, 1)
            pool.wait_ge(id_zero, ONE + 1)
            nc.gpsimd.affine_select(out=ident[:, :], in_=ident[:, :], compare_op=ALU.not_equal, fill=1.0, base=0,
                                    pattern=[[-1, 128]], channel_multiplier=1).then_inc(id_set, 1)
            nc.gpsimd.memset(minus_half[:, :], -0.5).then_inc(half_set, 1)
            pool.wait_ge(half_set, ONE + 1)
            pool.wait_ge(consts_in, ONE + 64)

            def add_bias(m, i):
                pool.wait_ge(a_in[i], ONE + 24 * (m - i) + 48)
                pool.wait_ge(h_kept, ONE + 2 * m)
                nc.gpsimd.tensor_tensor(h1b[:, :, :], h1[i][:, :, :], bias[:, :, :], ALU.add).then_inc(biased, 1)

            def root(m):
                pool.wait_ge(veps_ready, ONE + m + 1)
                nc.gpsimd.tensor_tensor(rstd[:, :], veps[:, :], minus_half[:, :], ALU.pow).then_inc(rstd_ready, 1)

            def add_base(m):
                pool.wait_ge(xn_ready, ONE + NQ * (m + 1))
                pool.wait_ge(base_out, ONE + 16 * m)
                nc.gpsimd.tensor_tensor(base[:, :, :], h2[:, :, :], xn[:, :, :], ALU.add).then_inc(base_ready, 1)

            add_bias(0, 0)
            with pool.Fori(0, CHUNKS // 2 - 1) as m2:
                for i in range(2):
                    m = 2 * m2 + i
                    root(m)
                    add_bias(m + 1, 1 - i)
                    add_base(m)
            root(CHUNKS - 2)
            add_bias(CHUNKS - 1, 1)
            add_base(CHUNKS - 2)
            root(CHUNKS - 1)
            add_base(CHUNKS - 1)

        @block.tensor
        def _(pe):
            pe.wait_ge(consts_in, ONE + 64)
            pe.wait_ge(id_set, ONE + 1)

            def hidden(m, i):
                pe.wait_ge(a_in[i], ONE + 24 * (m - i) + 48)
                pe.wait_ge(h_kept, ONE + 2 * m)
                for r in range(NQ):
                    for c in range(CT):
                        mm = nc.tensor.matmul(ps_h[0:QT, r // 2, (r % 2) * C:(r % 2 + 1) * C],
                                              aT[i][:, c, r * QT:(r + 1) * QT], w[:, c, :],
                                              start=(c == 0), stop=(c == CT - 1))
                    if r % 2:
                        mm.then_inc(h_ready, 1)

            def turn(m):
                pe.wait_ge(xn_ready, ONE + NQ * (m + 1))
                pe.wait_ge(xT_kept, ONE + CT * m)
                for c in range(CT):
                    for r in range(NQ):
                        mm = nc.tensor.transpose(ps_x[:, c, r * QT:(r + 1) * QT], xn[:, r, c * 128:(c + 1) * 128],
                                                 ident[0:QT, 0:QT])
                    mm.then_inc(xT_ready, 1)

            hidden(0, 0)
            with pe.Fori(0, CHUNKS // 2 - 1) as m2:
                hidden(2 * m2 + 1, 1)
                turn(2 * m2)
                hidden(2 * m2 + 2, 0)
                turn(2 * m2 + 1)
            hidden(CHUNKS - 1, 1)
            turn(CHUNKS - 2)
            turn(CHUNKS - 1)

        @block.scalar
        def _(act):
            with act.Fori(0, CHUNKS) as m:
                for c in range(CT):
                    act.wait_ge(xT_ready, ONE + CT * m + c + 1)
                    nc.scalar.activation(xnT[:, m, c, :], ps_x[:, c, 0:CH], ACT.Copy).then_inc(xT_kept, 1)

        @block.vector
        def _(dve):
            dve.wait_ge(consts_in, ONE + 64)

            def norm(m, gates):
                dve.wait_ge(biased, ONE + m + 1)
                dve.wait_ge(base_ready, ONE + m)
                for a in range(2):
                    dve.wait_ge(h_ready, ONE + 2 * m + a + 1)
                    nc.vector.tensor_tensor(h2[:, 2 * a:2 * a + 2, :].rearrange("p r c -> p (r c)"), ps_h[0:QT, a, :],
                                            h1b[:, 2 * a:2 * a + 2, :].rearrange("p r c -> p (r c)"),
                                            ALU.add).then_inc(h_kept, 1)
                dve.wait_ge(h_kept, ONE + 2 * m + 2)
                for r in range(NQ):
                    nc.vector.bn_stats(stats[:, r, :], h2[:, r, :]).then_inc(stats_ready, 1)
                dve.wait_ge(stats_ready, ONE + NQ * (m + 1))
                nc.vector.tensor_tensor(both[:, :, :], stats[:, :, 1:3], stats[:, :, 4:6], ALU.add).then_inc(mv_ready, 1)
                nc.vector.tensor_tensor(apart[:, :], stats[:, :, 1], stats[:, :, 4], ALU.subtract).then_inc(mv_ready, 1)
                dve.wait_ge(mv_ready, ONE + 5 * m + 2)
                nc.vector.tensor_scalar(mean[:, :], both[:, :, 0], 0.5, None, ALU.mult).then_inc(mv_ready, 1)
                nc.vector.tensor_scalar(within[:, :], both[:, :, 1], 1.0 / C, EPS, ALU.mult,
                                        ALU.add).then_inc(mv_ready, 1)
                nc.vector.scalar_tensor_tensor(out=between[:, :], in0=apart[:, :], scalar=0.25, in1=apart[:, :],
                                               op0=ALU.mult, op1=ALU.mult).then_inc(mv_ready, 1)
                dve.wait_ge(mv_ready, ONE + 5 * (m + 1))
                nc.vector.tensor_tensor(veps[:, :], within[:, :], between[:, :], ALU.add).then_inc(veps_ready, 1)
                dve.wait_ge(rstd_ready, ONE + m + 1)
                dve.wait_ge(xT_ready, ONE + CT * m)
                for r in range(NQ):
                    nc.vector.tensor_scalar(xn[:, r, :], h2[:, r, :], mean[:, r:r + 1], rstd[:, r:r + 1],
                                            ALU.subtract, ALU.mult).then_inc(xn_ready, 1)
                for r in range(NQ):
                    dve.wait_ge(xn_ready, ONE + NQ * m + r + 1)
                    nc.vector.tensor_tensor_reduce(product[:, r, :], xn[:, r, :], w_gate[:, :], 1.0, 0.0, ALU.mult,
                                                   ALU.add, dots[:, r:r + 1]).then_inc(dots_ready, 1)
                dve.wait_ge(dots_ready, ONE + NQ * (m + 1))
                nc.vector.tensor_scalar(gates, dots[:, :], b_gate[:, 0:1], None, ALU.add).then_inc(gate_ready, 1)

            flat = gate[:, :, :].rearrange("p b i -> p (b i)")
            with dve.Fori(0, CHUNKS) as m:
                norm(m, flat[:, bass.ds(m * NQ, NQ)])


def rank_gates(nc, d, gate, coef):
    with ExitStack() as ctx:
        sb = lambda n, s, t=F32: ctx.enter_context(nc.sbuf_tensor(n, s, t))
        sem = lambda n: ctx.enter_context(nc.semaphore(n))
        TILES = N // QT
        row = [sb(f"gate_row{i}", [QT, N]) for i in range(B)]
        own = sb("own", [QT, TILES])
        hits = sb("hits", [QT, 4, N], mybir.dt.bfloat16)
        count = sb("count", [QT, TILES, 4])
        rank = sb("rank", [QT, TILES])
        kept = sb("kept", [QT, TILES])
        earlier = sb("earlier", [QT, QT])
        row_in = [sem(f"row_in{b}") for b in range(B)]
        tri_one, tri_set, zero_set = sem("tri_one"), sem("tri_set"), sem("zero_set5")
        own_ready, counted, ranked, kept_ready, coef_ready = (
            sem("own_ready"), sem("counted"), sem("ranked"), sem("kept_ready"), sem("coef_ready"))
        block = ctx.enter_context(nc.Block())
        OPS = 4 * TILES - 2

        @block.sync
        def _(sp):
            for b in range(B):
                sp.dma_start(row[b][:, :], view(d.gate, b * N, [[0, QT], [1, N]])).then_inc(row_in[b], 16)

        @block.gpsimd
        def _(pool):
            nc.gpsimd.memset(earlier[:, :], 1.0).then_inc(tri_one, 1)
            pool.wait_ge(tri_one, 1)
            nc.gpsimd.affine_select(out=earlier[:, :], in_=earlier[:, :], compare_op=ALU.is_gt, fill=0.0, base=0,
                                    pattern=[[-1, QT]], channel_multiplier=1).then_inc(tri_set, 1)

        @block.vector
        def _(dve):
            nc.vector.memset(count[:, :, :], 0.0).then_inc(zero_set, 1)
            dve.wait_ge(zero_set, 1)
            dve.wait_ge(tri_set, 1)
            for b in range(B):
                nc.vector.tensor_copy(own[:, :], gate[:, b, :]).then_inc(own_ready, 1)
                dve.wait_ge(own_ready, b + 1)
                dve.wait_ge(row_in[b], 16)
                dve.wait_ge(ranked, b)
                for i in range(TILES):
                    a, z = i * QT, (i + 1) * QT
                    mine = own[:, i:i + 1]

                    def tally(lo, hi, op, slot):
                        nc.vector.tensor_scalar(hits[:, slot, lo:hi], row[b][:, lo:hi], mine, 0.0, op, ALU.add,
                                                accum_out=count[:, i, slot:slot + 1]).then_inc(counted, 1)

                    if i > 0:
                        dve.wait_ge(counted, OPS * b + 4 * i - 1)
                        tally(0, a, ALU.is_ge, 0)
                    elif b > 0:
                        dve.wait_ge(counted, OPS * b)
                    if i < TILES - 1:
                        tally(z, N, ALU.is_gt, 1)
                    tally(a, z, ALU.is_gt, 2)
                    nc.vector.scalar_tensor_tensor(out=hits[:, 3, a:z], in0=row[b][:, a:z], scalar=mine,
                                                   in1=earlier[:, :], op0=ALU.is_equal, op1=ALU.mult,
                                                   accum_out=count[:, i, 3:4]).then_inc(counted, 1)
                dve.wait_ge(counted, OPS * (b + 1))
                nc.vector.tensor_reduce(rank[:, :], count[:, :, :], AX.X, ALU.add).then_inc(ranked, 1)
                dve.wait_ge(ranked, b + 1)
                nc.vector.tensor_scalar(kept[:, :], rank[:, :], float(KEEP), None, ALU.is_lt).then_inc(kept_ready, 1)
                dve.wait_ge(kept_ready, b + 1)
                nc.vector.tensor_tensor(coef[:, b, :], own[:, :], kept[:, :], ALU.mult).then_inc(coef_ready, 1)
                dve.wait_ge(coef_ready, b + 1)


def ffn(nc, d, xnT, coef):
    with ExitStack() as ctx:
        sb = lambda n, s, t=F32: ctx.enter_context(nc.sbuf_tensor(n, s, t))
        ps = lambda n, s: ctx.enter_context(nc.psum_tensor(n, s, F32))
        sems = []

        def sem(name):
            sems.append(ctx.enter_context(nc.semaphore(name)))
            return sems[-1]

        w_up = sb("w_up", [128, CT, HID])
        w_down = sb("w_down", [128, HT, C])
        b_up = sb("b_up", [128, HT])
        b_down = sb("b_down", [QT, 2, C])
        base = [sb(f"base5{i}", [QT, NQ, C]) for i in range(2)]
        coefs = sb("coefs", [QT, NQ])
        hT = sb("hT", [128, HT, CH])
        y = sb("y", [QT, NQ, C])
        out = sb("out5", [QT, NQ, C])
        ps_h = ps("ps_h5", [128, 4, 512])
        ps_y = ps("ps_y", [128, 4, 512])
        base_in = [sem(f"base_in{i}") for i in range(2)]
        consts_in, h_ready, h_kept = sem("consts_in5"), sem("h_ready5"), sem("h_kept5")
        y_ready, y_kept, coefs_set, out_ready, out_out = (
            sem("y_ready"), sem("y_kept"), sem("coefs_set"), sem("out_ready5"), sem("out_out5"))
        start_counts(nc, sems)
        block = ctx.enter_context(nc.Block())

        @block.sync
        def _(sp):
            sp.dma_start(w_up[:, :, :], d.w_up.rearrange("(t p) n -> p t n", p=128)).then_inc(consts_in, 16)
            sp.dma_start(w_down[:, :, :], d.w_down.rearrange("(t p) n -> p t n", p=128)).then_inc(consts_in, 16)
            sp.dma_start(b_up[:, :], d.b_up.rearrange("(t p) -> p t", p=128),
                         allow_slow_non_contiguous=True).then_inc(consts_in, 16)
            sp.dma_start(b_down[:, :, :], view(d.b_down, 0, [[0, QT], [0, 2], [1, C]])).then_inc(consts_in, 16)

            def load(m, i):
                sp.dma_start(base[i][:, :, :], d.base[m]).then_inc(base_in[i], 16)

            def store(m):
                sp.wait_ge(out_ready, ONE + NQ * (m + 1))
                sp.dma_start(d.out[m].rearrange("(i p) c -> p i c", p=QT), out[:, :, :]).then_inc(out_out, 16)

            load(0, 0)
            load(1, 1)
            with sp.Fori(0, CHUNKS // 2 - 1) as m2:
                for i in range(2):
                    store(2 * m2 + i)
                    load(2 * m2 + i + 2, i)
            store(CHUNKS - 2)
            store(CHUNKS - 1)
            sp.wait_ge(out_out, ONE + 16 * CHUNKS)

        @block.tensor
        def _(pe):
            pe.wait_ge(consts_in, ONE + 64)

            def up(m, t):
                if t < 4:
                    pe.wait_ge(h_kept, ONE + HT * m)
                else:
                    pe.wait_ge(h_kept, ONE + HT * m + t - 3)
                for c in range(CT):
                    mm = nc.tensor.matmul(ps_h[:, t % 4, 0:CH], w_up[:, c, t * 128:(t + 1) * 128], xnT[:, m, c, :],
                                          start=(c == 0), stop=(c == CT - 1))
                mm.then_inc(h_ready, 1)

            def down(m, r):
                pe.wait_ge(h_kept, ONE + HT * (m + 1))
                pe.wait_ge(y_kept, ONE + NQ * m)
                for t in range(HT):
                    mm = nc.tensor.matmul(ps_y[0:QT, r, 0:C], hT[:, t, r * QT:(r + 1) * QT], w_down[:, t, :],
                                          start=(t == 0), stop=(t == HT - 1))
                mm.then_inc(y_ready, 1)

            with pe.Fori(0, CHUNKS) as m:
                for t in range(HT):
                    up(m, t)
                for r in range(NQ):
                    down(m, r)

        @block.scalar
        def _(act):
            act.wait_ge(consts_in, ONE + 64)
            with act.Fori(0, CHUNKS) as m:
                act.wait_ge(y_ready, ONE + NQ * m)
                for t in range(HT):
                    act.wait_ge(h_ready, ONE + HT * m + t + 1)
                    nc.scalar.activation(hT[:, t, :], ps_h[:, t % 4, 0:CH], ACT.Gelu_apprx_tanh,
                                         bias=b_up[:, t:t + 1]).then_inc(h_kept, 1)

        @block.vector
        def _(dve):
            dve.wait_ge(consts_in, ONE + 64)
            flat = coef[:, :, :].rearrange("p b i -> p (b i)")

            def chunk(m, i):
                dve.wait_ge(out_ready, ONE + NQ * m)
                nc.vector.tensor_copy(coefs[:, :], flat[:, bass.ds(m * NQ, NQ)]).then_inc(coefs_set, 1)
                dve.wait_ge(coefs_set, ONE + m + 1)
                dve.wait_ge(base_in[i], ONE + 8 * (m - i) + 16)
                dve.wait_ge(out_out, ONE + 16 * m)
                for r in range(NQ):
                    dve.wait_ge(y_ready, ONE + NQ * m + r + 1)
                    nc.vector.tensor_tensor(y[:, r, :], ps_y[0:QT, r, 0:C], b_down[:, 0, :], ALU.add).then_inc(y_kept, 1)
                for r in range(NQ):
                    dve.wait_ge(y_kept, ONE + NQ * m + r + 1)
                    nc.vector.scalar_tensor_tensor(out=out[:, r, :], in0=y[:, r, :], scalar=coefs[:, r:r + 1],
                                                   in1=base[i][:, r, :], op0=ALU.mult, op1=ALU.add
                                                   ).then_inc(out_ready, 1)

            with dve.Fori(0, CHUNKS // 2) as m2:
                chunk(2 * m2, 0)
                chunk(2 * m2 + 1, 1)


class Dram:
    pass


def vit_tower(nc, d):
    def scratch(name, shape, dt=F32):
        return nc.dram_tensor(name, shape, dt, kind="Internal").ap()

    d.win_bias = scratch("win_bias", [4, GROUP, GROUP])
    d.negs = scratch("negs", [28, 28])
    d.skew = scratch("skew", [NH * 128 * 257])
    d.corner = scratch("corner_parts", [G, 128, 2, HG, 128])
    d.no_corner = scratch("no_corner", [G, 128, 2, HG, 128])
    d.a1 = scratch("window_out", [UNITS, 128, CT, UNIT])
    d.h1 = scratch("hidden1", [CHUNKS, QT, NQ, C])
    d.q = scratch("q_parts", [CHUNKS, G, 2, 128, CH])
    d.k = scratch("k_parts", [CHUNKS, G, 2, 128, CH])
    d.v = scratch("v_rows_dram", [CHUNKS, CH, C])
    d.v_rows = d.v.rearrange("(b k) n c -> b (k n) c", b=B)
    d.a2 = scratch("attention_out", [G * CHUNKS, 128, CH])
    d.base = scratch("base_rows", [CHUNKS, QT, NQ, C])
    d.gate = scratch("gate_rows", [B, N])
    setup_tables(nc, d)
    window_attention(nc, d)
    project_qkv(nc, d)
    full_attention(nc, d)
    gated_ffn(nc, d)


def kernel(**inputs):
    import numpy as np
    import concourse.bacc as bacc
    from concourse import mybir as mb
    from concourse.bass_utils import run_bass_kernel_spmd as run

    def rolled(x, axis):
        k = WS // 2
        head, tail = np.split(x, [k], axis=axis)
        return np.concatenate([tail, head], axis=axis)

    x = rolled(rolled(np.asarray(inputs["x"]), 2), 3)
    w1 = np.asarray(inputs["L0_tok_w1"]).reshape(DH, NH, 3, C)
    arrays = {
        "x": x.reshape(B, CT, 128, SIDE // WS, WS, 2, HALFROW).transpose(0, 3, 2, 1, 5, 4, 6).reshape(
            UNITS, 128, CT, UNIT),
        "w_tok": w1.transpose(3, 2, 1, 0).reshape(C, 3 * C),
        "b_tok": np.asarray(inputs["L0_tok_b1"]).reshape(DH, NH, 3).transpose(2, 1, 0).reshape(3 * C),
        "w_tok_out": np.asarray(inputs["L0_tok_w2"]).T,
        "b_tok_out": inputs["L0_tok_b2"],
        "pos_emb": inputs["L0_tok_pos_emb"],
        "w_qkv": inputs["L0_attn_qkv_w"],
        "b_qkv": inputs["L0_attn_qkv_b"],
        "w_proj": inputs["L0_attn_proj_w"],
        "b_proj": inputs["L0_attn_proj_b"],
        "rpb": np.asarray(inputs["L0_attn_rpb_table"]).T,
        "w_gate": np.asarray(inputs["L0_ffn_wr"]).reshape(C),
        "b_gate": inputs["L0_ffn_br"],
        "w_up": inputs["L0_ffn_w1"],
        "b_up": inputs["L0_ffn_b1"],
        "w_down": inputs["L0_ffn_w2"],
        "b_down": inputs["L0_ffn_b2"],
    }
    nc = bacc.Bacc("TRN2", target_bir_lowering=False, num_devices=1)
    d = Dram()
    launch = {}
    for name, a in arrays.items():
        a = np.ascontiguousarray(a)
        launch[f"in_{name}"] = a
        ap = nc.dram_tensor(f"in_{name}", a.shape, mb.dt.from_np(a.dtype), kind="ExternalInput").ap()
        d.__dict__[name] = ap
    d.out = nc.dram_tensor("out", (CHUNKS, CH, C), F32, kind="ExternalOutput").ap()
    vit_tower(nc, d)
    r = run(nc, [launch], core_ids=[0])
    return r.results[0]["out"].reshape(B, N, C)
```

```python
from contextlib import ExitStack

import concourse.bass as bass
from concourse import mybir

ALU = mybir.AluOpType
ACT = mybir.ActivationFunctionType
AX = mybir.AxisListType
F32 = mybir.dt.float32
F32R = mybir.dt.float32r

B = 4
C = 256
CT = C // 128
SIDE = 56
N = SIDE * SIDE
NH = 8
DH = C // NH
WS = 4
GROUP = SIDE // 2 * WS
UNIT = 2 * GROUP
UNITS = B * N // UNIT
HALFROW = SIDE // 2
CH = 448
CHUNKS = B * N // CH
PER_IMAGE = N // CH
QT = 112
NQ = CH // QT
G = 2
HG = NH // G
FIRST = 64
KT = 1 + (N - FIRST) // 128
SLOTS = 5
STACK = 3 * DH
HID = 4 * C
HT = HID // 128
KEEP = max(1, N // 2) - 1
REL = 127
NEG = -1.0e30
EPS = 1e-5


def view(dram, offset, dims):
    return bass.AP(dram.tensor, offset, dims)


ONE = 1


def start_counts(nc, sems, more=None):
    with nc.Block() as block:
        @block.vector
        def _(dve):
            for s in sems:
                dve.sem_inc(s, ONE)
            for s, uses in (more or {}).items():
                dve.sem_inc(s, uses)


def setup_tables(nc, d):
    with ExitStack() as ctx:
        sb = lambda n, s, t=F32: ctx.enter_context(nc.sbuf_tensor(n, s, t))
        sem = lambda n: ctx.enter_context(nc.semaphore(n))
        neg = sb("neg", [GROUP, 4, GROUP])
        rel = sb("rel", [NH, REL])
        edge = sb("edge", [NH, 255])
        corner = sb("corner", [128, NH, 128])
        corner_hi = sb("corner_hi", [128, NH, 128], F32R)
        corner_lo = sb("corner_lo", [128, NH, 128], F32R)
        zero = sb("zero", [128, 2, HG, 128])
        zero_set, zero_out = sem("zero_set"), sem("zero_out")
        neg_set, filled, placed, masked = sem("neg_set"), sem("filled"), sem("placed"), sem("masked")
        rel_in, edge_zero, edge_set, skewed, corner_in = (
            sem("rel_in"), sem("edge_zero"), sem("edge_set"), sem("skewed"), sem("corner_in"))
        hi_set, lo_set, corner_out = sem("hi_set"), sem("lo_set"), sem("corner_out")
        block = ctx.enter_context(nc.Block())

        def table(v, offset, dims):
            return view(d.win_bias, v * GROUP * GROUP + offset, dims)

        @block.sync
        def _(sp):
            sp.wait_ge(neg_set, 1)
            sp.dma_start(d.win_bias.rearrange("v p k -> p v k"), neg[:, :, :]).then_inc(filled, 16)
            sp.dma_start(d.negs, neg[0:28, 0, 0:28]).then_inc(filled, 16)
            sp.wait_ge(filled, 32)
            n = 0
            for v in range(4):
                for r in range(WS):
                    for p in range(WS):
                        src = view(d.pos_emb, (WS - 1 - r) * 7 + WS - 1 - p, [[0, 7], [7, WS], [1, WS]])
                        dst = table(v, (r * HALFROW + p) * GROUP,
                                    [[WS * GROUP + WS, 7], [HALFROW, WS], [1, WS]])
                        sp.dma_start(dst, src).then_inc(placed, 16)
                        n += 16
            sp.wait_ge(placed, n)
            half, m = GROUP // 2, 0
            for v in (1, 3):
                for off in (half * GROUP, half):
                    for part in (0, 28):
                        sp.dma_start(table(v, off + part * GROUP, [[GROUP, 28], [1, 28]]), d.negs).then_inc(masked, 16)
                        sp.dma_start(table(v, off + part * GROUP + 28, [[GROUP, 28], [1, 28]]),
                                     d.negs).then_inc(masked, 16)
                        m += 32
            sp.wait_ge(masked, m)
            for v in (2, 3):
                for r in range(WS):
                    for a, b in ((26, 24), (24, 26)):
                        dst = table(v, (r * HALFROW + a) * GROUP + b, [[GROUP, 2], [HALFROW, WS], [1, 2]])
                        sp.dma_start(dst, view(d.negs, 0, [[28, 2], [2, WS], [1, 2]])).then_inc(masked, 16)
                        m += 16
            sp.wait_ge(masked, m)

        @block.scalar
        def _(act):
            act.dma_start(rel[:, :], d.rpb).then_inc(rel_in, 16)
            act.wait_ge(edge_set, 1)
            act.dma_start(view(d.skew, 0, [[128 * 257, NH], [257, 128], [1, 255]]),
                          edge[:, :].unsqueeze(1).broadcast_to([NH, 128, 255])).then_inc(skewed, 16)
            act.wait_ge(skewed, 16)
            act.dma_start(corner[:, :, :], view(d.skew, 127, [[256, 128], [128 * 257, NH], [1, 128]])
                          ).then_inc(corner_in, 16)
            act.wait_ge(zero_set, 1)
            for g in range(G):
                act.dma_start(d.no_corner[g], zero[:, :, :, :]).then_inc(zero_out, 16)
            act.wait_ge(hi_set, 1)
            act.wait_ge(lo_set, 1)
            for g in range(G):
                act.dma_start(d.corner[g, :, 0], corner_hi[:, g * HG:(g + 1) * HG, :].bitcast(F32)).then_inc(corner_out, 16)
                act.dma_start(d.corner[g, :, 1], corner_lo[:, g * HG:(g + 1) * HG, :].bitcast(F32)).then_inc(corner_out, 16)
            act.wait_ge(corner_out, 16 * 2 * G)
            act.wait_ge(zero_out, 16 * G)

        @block.vector
        def _(dve):
            nc.vector.memset(neg[:, :, :], NEG).then_inc(neg_set, 1)
            nc.vector.memset(edge[:, :], 0.0).then_inc(edge_zero, 1)
            nc.vector.memset(zero[:, :, :, :], 0.0).then_inc(zero_set, 1)
            dve.wait_ge(rel_in, 16)
            dve.wait_ge(edge_zero, 1)
            nc.vector.tensor_scalar(edge[:, 0:REL], rel[:, :], rel[:, REL - 1:REL], None,
                                    ALU.subtract).then_inc(edge_set, 1)
            dve.wait_ge(corner_in, 16)
            nc.vector.tensor_copy(corner_hi[:, :, :], corner[:, :, :]).then_inc(hi_set, 1)
            dve.wait_ge(hi_set, 1)
            nc.vector.tensor_tensor(corner_lo[:, :, :], corner[:, :, :], corner_hi[:, :, :].bitcast(F32),
                                    ALU.subtract).then_inc(lo_set, 1)


def window_attention(nc, d):
    with ExitStack() as ctx:
        sb = lambda n, s, t=F32: ctx.enter_context(nc.sbuf_tensor(n, s, t))
        ps = lambda n, s: ctx.enter_context(nc.psum_tensor(n, s, F32))
        sems = []

        def sem(name):
            sems.append(ctx.enter_context(nc.semaphore(name)))
            return sems[-1]

        w = sb("w_qkv", [128, CT, 3 * C])
        bias_col = sb("bias_col", [128, 2 * CT])
        bias_v = sb("bias_v", [GROUP, C])
        ident = sb("ident", [128, 128])
        ones = sb("ones", [GROUP, DH])
        tab = sb("tab", [GROUP, 2, CT, GROUP])
        tab_odd = sb("tab_odd", [GROUP, 2, CT, GROUP])
        xT = [sb(f"xT{i}", [128, CT, UNIT]) for i in range(2)]
        qk = [sb(f"qk{i}", [128, 2 * CT, UNIT]) for i in range(2)]
        v = [sb(f"v{i}", [GROUP, 2, C]) for i in range(2)]
        logit = [sb(f"logit{i}", [GROUP, NH, GROUP]) for i in range(2)]
        prob = [sb(f"prob{i}", [GROUP, NH, GROUP]) for i in range(2)]
        probT = [sb(f"probT{i}", [GROUP, NH, GROUP]) for i in range(2)]
        top = [sb(f"top{i}", [GROUP, NH]) for i in range(2)]
        sums = [sb(f"sums{i}", [128, 2 * CT * GROUP]) for i in range(2)]
        rden = [sb(f"rden{i}", [128, CT, GROUP]) for i in range(2)]
        oT = [sb(f"oT{i}", [128, CT, UNIT]) for i in range(2)]
        ps_s = ps("ps_s", [GROUP, 4, 512])
        ps_t = ps("ps_t", [128, 2, 512])
        ps_q = ps("ps_q", [128, 2, 512])

        consts_in, id_zero, id_set, ones_set, odd_in = (
            sem("consts_in"), sem("id_zero"), sem("id_set"), sem("ones_set"), sem("odd_in"))
        x_in, qkv_ready = [sem(f"x_in{u}") for u in range(2)], sem("qkv_ready")
        qk_kept, v_kept = sem("qk_kept"), sem("v_kept")
        s_ready, logit_ready, top_ready, shifted, prob_ready = (
            sem("s_ready"), sem("logit_ready"), sem("top_ready"), sem("shifted"), sem("prob_ready"))
        t_ready, t_kept, o_ready, recip_ready, o_kept, o_out = (
            sem("t_ready"), sem("t_kept"), sem("o_ready"), sem("recip_ready"), sem("o_kept"),
            [sem(f"o_out{u}") for u in range(2)])
        normalized = sem("normalized")
        start_counts(nc, sems)
        block = ctx.enter_context(nc.Block())
        JOBS = 2 * CT + 2
        SCALE = 1.0 / float(DH) ** 0.5

        @block.sync
        def _(sp):
            sp.dma_start(w[:, :, :], d.w_tok.rearrange("(t p) n -> p t n", p=128)).then_inc(consts_in, 16)
            sp.dma_start(bias_col[:, :], d.b_tok[0:2 * C].rearrange("(t p) -> p t", p=128),
                         allow_slow_non_contiguous=True).then_inc(consts_in, 16)
            sp.dma_start(bias_v[:, :], view(d.b_tok, 2 * C, [[0, GROUP], [1, C]])).then_inc(consts_in, 16)
            for half in range(2):
                for c in range(CT):
                    sp.dma_start(tab[:, half, c, :], d.win_bias[2 * half]).then_inc(consts_in, 16)
            for u in range(2):
                sp.dma_start(xT[u][:, :, :], d.x[u]).then_inc(x_in[u], 16)

            def pair(m, last_row):
                sp.wait_ge(logit_ready, ONE + 4 * m)
                for half in range(2):
                    for c in range(CT):
                        sp.dma_start(tab_odd[:, half, c, :], d.win_bias[2 * half + last_row]).then_inc(odd_in, 16)

            def store(m, u):
                sp.wait_ge(normalized, ONE + 4 * m + 2 * u + 2)
                sp.dma_start(d.a1[2 * m + u], oT[u][:, :, :]).then_inc(o_out[u], 16)

            def load(m, u):
                sp.wait_ge(qkv_ready, ONE + JOBS * (2 * m + u + 1))
                sp.dma_start(xT[u][:, :, :], d.x[2 * m + u + 2]).then_inc(x_in[u], 16)

            def body(m, last_row, more):
                pair(m, last_row)
                if more:
                    load(m, 0)
                    load(m, 1)
                store(m, 0)
                store(m, 1)

            rows = UNITS // B // 2
            with sp.Fori(0, B - 1) as b:
                with sp.Fori(0, rows - 1) as r:
                    body(b * rows + r, 0, True)
                body(b * rows + rows - 1, 1, True)
            with sp.Fori(0, rows - 1) as r:
                body((B - 1) * rows + r, 0, True)
            body(B * rows - 1, 1, False)
            for u in range(2):
                sp.wait_ge(o_out[u], ONE + 8 * UNITS)

        @block.gpsimd
        def _(pool):
            nc.gpsimd.memset(ident[:, :], 0.0).then_inc(id_zero, 1)
            pool.wait_ge(id_zero, ONE + 1)
            nc.gpsimd.affine_select(out=ident[:, :], in_=ident[:, :], compare_op=ALU.not_equal, fill=1.0, base=0,
                                    pattern=[[-1, 128]], channel_multiplier=1).then_inc(id_set, 1)
            nc.gpsimd.memset(ones[:, :], 1.0).then_inc(ones_set, 1)

            def shift(k, p):
                pool.wait_ge(top_ready, ONE + k + 1)
                nc.gpsimd.tensor_tensor(logit[p][:, :, :], logit[p][:, :, :],
                                        top[p][:, :].unsqueeze(2).broadcast_to([GROUP, NH, GROUP]),
                                        ALU.subtract).then_inc(shifted, 1)

            with pool.Fori(0, UNITS // 2) as m:
                for k in range(4):
                    shift(4 * m + k, k % 2)

        @block.tensor
        def _(pe):
            pe.wait_ge(consts_in, ONE + 16 * (3 + 2 * CT))
            pe.wait_ge(id_set, ONE + 1)
            pe.wait_ge(ones_set, ONE + 1)

            def project_qk(n, u, jobs):
                pe.wait_ge(x_in[u], ONE + 8 * (n - u) + 16)
                for job in jobs:
                    if job < 2:
                        pe.wait_ge(v_kept, ONE + 2 * n)
                    else:
                        pe.wait_ge(qk_kept, ONE + 2 * CT * n + job - 1)
                    for c in range(CT):
                        mm = nc.tensor.matmul(ps_q[:, job % 2, 0:UNIT], w[:, c, job * 128:(job + 1) * 128],
                                              xT[u][:, c, :], start=(c == 0), stop=(c == CT - 1))
                    mm.then_inc(qkv_ready, 1)

            def project_v(n, u, half):
                pe.wait_ge(qk_kept, ONE + 2 * CT * n + 2 * CT - 1 + half)
                for c in range(CT):
                    x = xT[u][:, c, half * GROUP:(half + 1) * GROUP]
                    mm = nc.tensor.matmul(ps_q[0:GROUP, half, 0:C], x, w[:, c, 2 * C:3 * C],
                                          start=(c == 0), stop=(c == CT - 1))
                mm.then_inc(qkv_ready, 1)

            def scores(n, u, half):
                k = 2 * n + half
                pe.wait_ge(logit_ready, ONE + k)
                pe.wait_ge(qk_kept, ONE + 2 * CT * (n + 1))
                for c in range(CT):
                    for j in range(4):
                        rows = slice(32 * j, 32 * j + 32)
                        q = qk[u][rows, c, half * GROUP:(half + 1) * GROUP]
                        kk = qk[u][rows, CT + c, half * GROUP:(half + 1) * GROUP]
                        mm = nc.tensor.matmul(ps_s[:, j, c * GROUP:(c + 1) * GROUP], q, kk, start=True, stop=True)
                mm.then_inc(s_ready, 1)

            def turn(n, half):
                k = 2 * n + half
                pe.wait_ge(prob_ready, ONE + k + 1)
                pe.wait_ge(o_kept, ONE + k)
                for h in range(NH):
                    mm = nc.tensor.transpose(ps_t[0:GROUP, h // 4, (h % 4) * GROUP:(h % 4 + 1) * GROUP],
                                             prob[half][:, h, :], ident[0:GROUP, 0:GROUP])
                mm.then_inc(t_ready, 1)

            def weigh(n, u, half):
                k = 2 * n + half
                pe.wait_ge(t_kept, ONE + k + 1)
                pe.wait_ge(v_kept, ONE + 2 * (n + 1))
                for c in range(CT):
                    for j in range(4):
                        nc.tensor.matmul(ps_t[32 * j:32 * j + 32, 0, c * GROUP:(c + 1) * GROUP],
                                         v[u][:, half, (4 * c + j) * DH:(4 * c + j + 1) * DH],
                                         probT[half][:, 2 * j + c, :], start=True, stop=True)
                for c in range(CT):
                    for j in range(4):
                        mm = nc.tensor.matmul(ps_t[32 * j:32 * j + 32, 0, (CT + c) * GROUP:(CT + c + 1) * GROUP],
                                              ones[:, :], probT[half][:, 2 * j + c, :], start=True, stop=True)
                mm.then_inc(o_ready, 1)

            def unit(n, u, more):
                scores(n, u, 1)
                if more:
                    project_qk(n + 1, 1 - u, range(2 * CT - 1))
                turn(n, 0)
                if more:
                    project_qk(n + 1, 1 - u, [2 * CT - 1])
                    project_v(n + 1, 1 - u, 0)
                weigh(n, u, 0)
                if more:
                    project_v(n + 1, 1 - u, 1)
                turn(n, 1)
                if more:
                    scores(n + 1, 1 - u, 0)
                weigh(n, u, 1)

            project_qk(0, 0, range(2 * CT))
            project_v(0, 0, 0)
            project_v(0, 0, 1)
            scores(0, 0, 0)
            with pe.Fori(0, UNITS // 2 - 1) as m:
                unit(2 * m, 0, True)
                unit(2 * m + 1, 1, True)
            unit(UNITS - 2, 0, True)
            unit(UNITS - 1, 1, False)

        @block.vector
        def _(dve):
            dve.wait_ge(consts_in, ONE + 16 * (3 + 2 * CT))

            def logits(n, u, half):
                k = 2 * n + half
                dve.wait_ge(s_ready, ONE + k + 1)
                if u:
                    dve.wait_ge(odd_in, ONE + 16 * CT * (n + 1))
                table = (tab_odd if u else tab)[:, half, :, :].rearrange("p c k -> p (c k)")
                table = table.unsqueeze(1).broadcast_to([GROUP, 4, CT * GROUP])
                nc.vector.scalar_tensor_tensor(
                    out=logit[half][:, :, :].rearrange("p (j c) k -> p j (c k)", j=4),
                    in0=ps_s[:, :, 0:2 * GROUP], scalar=SCALE,
                    in1=table, op0=ALU.mult, op1=ALU.add).then_inc(logit_ready, 1)
                dve.wait_ge(logit_ready, ONE + k + 1)
                nc.vector.tensor_reduce(top[half][:, :], logit[half][:, :, :], AX.X, ALU.max).then_inc(top_ready, 1)

            def keep_v(n, u):
                for half in range(2):
                    dve.wait_ge(qkv_ready, ONE + JOBS * n + 2 * CT + 1 + half)
                    nc.vector.tensor_tensor(v[u][:, half, :], ps_q[0:GROUP, half, 0:C], bias_v[:, :],
                                            ALU.add).then_inc(v_kept, 1)

            def outputs(n, u, half):
                k = 2 * n + half
                dve.wait_ge(o_kept, ONE + k + 1)
                nc.vector.reciprocal(rden[half][:, :, :].rearrange("p c k -> p (c k)"),
                                     sums[half][:, CT * GROUP:2 * CT * GROUP]).then_inc(recip_ready, 1)
                dve.wait_ge(recip_ready, ONE + k + 1)
                if half == 0:
                    dve.wait_ge(o_out[u], ONE + 8 * (n - u))
                dst = oT[u][:, :, :].rearrange("p c (r h k) -> p c h r k", r=WS, h=2)[:, :, half]
                for c in range(CT):
                    ins = nc.vector.tensor_tensor(
                        dst[:, c], sums[half][:, c * GROUP:(c + 1) * GROUP].rearrange("p (r k) -> p r k", r=WS),
                        rden[half][:, c, :].rearrange("p (r k) -> p r k", r=WS), ALU.mult)
                ins.then_inc(normalized, 1)

            def unit(n, u, more):
                logits(n, u, 1)
                if more:
                    keep_v(n + 1, 1 - u)
                outputs(n, u, 0)
                if more:
                    logits(n + 1, 1 - u, 0)
                outputs(n, u, 1)

            keep_v(0, 0)
            logits(0, 0, 0)
            with dve.Fori(0, UNITS // 2 - 1) as m:
                unit(2 * m, 0, True)
                unit(2 * m + 1, 1, True)
            unit(UNITS - 2, 0, True)
            unit(UNITS - 1, 1, False)

        @block.scalar
        def _(act):
            act.wait_ge(consts_in, ONE + 16 * (3 + 2 * CT))

            def keep_qk(n, u, jobs):
                act.wait_ge(s_ready, ONE + 2 * (n - u))
                for job in jobs:
                    act.wait_ge(qkv_ready, ONE + JOBS * n + job + 1)
                    nc.scalar.activation(qk[u][:, job, :], ps_q[:, job % 2, 0:UNIT], ACT.Identity,
                                         bias=bias_col[:, job:job + 1]).then_inc(qk_kept, 1)

            def exps(n, half):
                k = 2 * n + half
                act.wait_ge(shifted, ONE + k + 1)
                nc.scalar.activation(prob[half][:, :, :], logit[half][:, :, :], ACT.Exp).then_inc(prob_ready, 1)

            def keep_t(n, half):
                k = 2 * n + half
                act.wait_ge(t_ready, ONE + k + 1)
                nc.scalar.activation(probT[half][:, :, :].rearrange("p (a h) k -> p a (h k)", a=2),
                                     ps_t[0:GROUP, :, 0:4 * GROUP], ACT.Copy).then_inc(t_kept, 1)

            def keep_sums(n, half):
                k = 2 * n + half
                act.wait_ge(o_ready, ONE + k + 1)
                act.wait_ge(normalized, ONE + k - half)
                nc.scalar.activation(sums[half][:, :], ps_t[:, 0, 0:2 * CT * GROUP], ACT.Copy).then_inc(o_kept, 1)

            def unit(n, u, more):
                if more:
                    keep_qk(n + 1, 1 - u, range(2 * CT - 1))
                keep_t(n, 0)
                if more:
                    keep_qk(n + 1, 1 - u, [2 * CT - 1])
                exps(n, 1)
                keep_sums(n, 0)
                keep_t(n, 1)
                keep_sums(n, 1)
                if more:
                    exps(n + 1, 0)

            keep_qk(0, 0, range(2 * CT))
            exps(0, 0)
            with act.Fori(0, UNITS // 2 - 1) as m:
                unit(2 * m, 0, True)
                unit(2 * m + 1, 1, True)
            unit(UNITS - 2, 0, True)
            unit(UNITS - 1, 1, False)


def project_qkv(nc, d):
    with ExitStack() as ctx:
        sb = lambda n, s, t=F32: ctx.enter_context(nc.sbuf_tensor(n, s, t))
        ps = lambda n, s: ctx.enter_context(nc.psum_tensor(n, s, F32))
        sems = []

        def sem(name):
            sems.append(ctx.enter_context(nc.semaphore(name)))
            return sems[-1]

        w_out = sb("w_out", [128, CT, C])
        w = sb("w_qkv2", [128, CT, 3 * C])
        bias_out = sb("bias_out", [QT, NQ, C])
        bias_v = sb("bias_v2", [QT, NQ, C])
        bias_col = sb("bias_col2", [128, 2 * CT])
        ident = sb("ident2", [128, 128])
        minus_half = sb("minus_half", [QT, NQ])
        aT = [sb(f"aT{i}", [128, 2, CT, UNIT]) for i in range(2)]
        h1 = sb("h1", [QT, NQ, C])
        stats = sb("stats", [QT, NQ, 6])
        both = sb("both", [QT, NQ, 2])
        apart, mean, within, between = (sb(n, [QT, NQ]) for n in ("apart", "mean", "within", "between"))
        veps = sb("veps", [QT, NQ])
        rstd = sb("rstd", [QT, NQ])
        xn = sb("xn", [QT, NQ, C])
        xnT = sb("xnT", [128, CT, CH])
        full = [sb(f"full{i}", [128, CH]) for i in range(2)]
        hi = [sb(f"hi{i}", [128, CH], F32R) for i in range(2)]
        lo = [sb(f"lo{i}", [128, CH], F32R) for i in range(2)]
        v = sb("v_rows", [QT, NQ, C])
        ps_h = ps("ps_h", [128, 2, 512])
        ps_x = ps("ps_x", [128, 2, 512])
        ps_q = ps("ps_q2", [128, 2, 512])
        ps_v = ps("ps_v", [128, 2, 512])
        consts_in, id_zero, id_set, half_set = sem("consts_in2"), sem("id_zero2"), sem("id_set2"), sem("half_set")
        a_in = [sem(f"a_in{i}") for i in range(2)]
        h_ready, h_kept, h_out = sem("h_ready"), sem("h_kept"), sem("h_out")
        stats_ready, mv_ready, veps_ready, rstd_ready, xn_ready = (
            sem("stats_ready"), sem("mv_ready"), sem("veps_ready"), sem("rstd_ready"), sem("xn_ready"))
        xT_ready, xT_kept, q_ready, full_ready, hi_ready, lo_ready, parts_out = (
            sem("xT_ready"), sem("xT_kept"), sem("q_ready"), sem("full_ready"), sem("hi_ready"), sem("lo_ready"),
            [sem(f"parts_out{i}") for i in range(2)])
        bias_set = sem("bias_set")
        v_ready, v_kept, v_out = sem("v_ready"), sem("v_kept2"), sem("v_out")
        start_counts(nc, sems)
        block = ctx.enter_context(nc.Block())
        QK = 2 * CT
        SCALE = float(DH) ** -0.5

        @block.sync
        def _(sp):
            sp.dma_start(w_out[:, :, :], d.w_tok_out.rearrange("(t p) n -> p t n", p=128)).then_inc(consts_in, 16)
            sp.dma_start(w[:, :, :], d.w_qkv.rearrange("(t p) n -> p t n", p=128)).then_inc(consts_in, 16)
            sp.dma_start(bias_col[:, :], d.b_qkv[0:2 * C].rearrange("(t p) -> p t", p=128),
                         allow_slow_non_contiguous=True).then_inc(consts_in, 16)
            sp.dma_start(bias_out[:, :, :], view(d.b_tok_out, 0, [[0, QT], [0, NQ], [1, C]])).then_inc(consts_in, 16)
            sp.dma_start(bias_v[:, :, :], view(d.b_qkv, 2 * C, [[0, QT], [0, NQ], [1, C]])).then_inc(consts_in, 16)

            def load(m, i):
                for u in range(2):
                    sp.dma_start(aT[i][:, u, :, :], d.a1[2 * m + u]).then_inc(a_in[i], 16)

            def stores(m):
                sp.wait_ge(h_kept, ONE + 2 * m + 2)
                sp.dma_start(d.h1[m], h1[:, :, :]).then_inc(h_out, 16)
                for job in range(QK):
                    sp.wait_ge(hi_ready, ONE + QK * m + job + 1)
                    sp.dma_start((d.q, d.k)[job // CT][m, job % CT, 0], hi[job % 2][:, :].bitcast(F32)).then_inc(parts_out[job % 2], 16)
                    sp.wait_ge(lo_ready, ONE + QK * m + job + 1)
                    sp.dma_start((d.q, d.k)[job // CT][m, job % CT, 1], lo[job % 2][:, :].bitcast(F32)).then_inc(parts_out[job % 2], 16)
                sp.wait_ge(v_kept, ONE + 2 * m + 2)
                sp.dma_start(d.v[m].rearrange("(i p) c -> p i c", p=QT), v[:, :, :]).then_inc(v_out, 16)

            load(0, 0)
            load(1, 1)
            with sp.Fori(0, CHUNKS // 2 - 1) as m2:
                for i in range(2):
                    m = 2 * m2 + i
                    sp.wait_ge(h_ready, ONE + 2 * m + 2)
                    load(m + 2, i)
                    stores(m)
            stores(CHUNKS - 2)
            stores(CHUNKS - 1)
            sp.wait_ge(h_out, ONE + 16 * CHUNKS)
            for i in range(2):
                sp.wait_ge(parts_out[i], ONE + 16 * QK * CHUNKS)
            sp.wait_ge(v_out, ONE + 16 * CHUNKS)

        @block.gpsimd
        def _(pool):
            nc.gpsimd.memset(ident[:, :], 0.0).then_inc(id_zero, 1)
            pool.wait_ge(id_zero, ONE + 1)
            nc.gpsimd.affine_select(out=ident[:, :], in_=ident[:, :], compare_op=ALU.not_equal, fill=1.0, base=0,
                                    pattern=[[-1, 128]], channel_multiplier=1).then_inc(id_set, 1)
            nc.gpsimd.memset(minus_half[:, :], -0.5).then_inc(half_set, 1)
            pool.wait_ge(half_set, ONE + 1)

            def root(m):
                pool.wait_ge(veps_ready, ONE + m + 1)
                nc.gpsimd.tensor_tensor(rstd[:, :], veps[:, :], minus_half[:, :], ALU.pow).then_inc(rstd_ready, 1)

            def low(m, job):
                pool.wait_ge(hi_ready, ONE + QK * m + job + 1)
                pool.wait_ge(parts_out[job % 2], ONE + 32 * (QK // 2 * m + job // 2))
                nc.gpsimd.tensor_tensor(lo[job % 2][:, :], full[job % 2][:, :], hi[job % 2][:, :].bitcast(F32),
                                        ALU.subtract).then_inc(lo_ready, 1)

            root(0)
            with pool.Fori(0, CHUNKS - 1) as m:
                root(m + 1)
                for job in range(QK):
                    low(m, job)
            for job in range(QK):
                low(CHUNKS - 1, job)

        @block.tensor
        def _(pe):
            pe.wait_ge(consts_in, ONE + 16 * 5)
            pe.wait_ge(id_set, ONE + 1)

            def hidden(m, i):
                pe.wait_ge(a_in[i], ONE + 16 * (m - i) + 32)
                pe.wait_ge(h_kept, ONE + 2 * m)
                for r in range(NQ):
                    for c in range(CT):
                        mm = nc.tensor.matmul(ps_h[0:QT, r // 2, (r % 2) * C:(r % 2 + 1) * C],
                                              aT[i][:, r // 2, c, (r % 2) * QT:(r % 2 + 1) * QT], w_out[:, c, :],
                                              start=(c == 0), stop=(c == CT - 1))
                    if r % 2:
                        mm.then_inc(h_ready, 1)

            def turn(m):
                pe.wait_ge(xn_ready, ONE + NQ * (m + 1))
                pe.wait_ge(xT_kept, ONE + CT * m)
                for c in range(CT):
                    for r in range(NQ):
                        mm = nc.tensor.transpose(ps_x[:, c, r * QT:(r + 1) * QT], xn[:, r, c * 128:(c + 1) * 128],
                                                 ident[0:QT, 0:QT])
                    mm.then_inc(xT_ready, 1)

            def project(m):
                pe.wait_ge(xT_kept, ONE + CT * (m + 1))
                for job in range(QK):
                    pe.wait_ge(full_ready, ONE + QK * m + job - job % 2)
                    for c in range(CT):
                        mm = nc.tensor.matmul(ps_q[:, job % 2, 0:CH], w[:, c, job * 128:(job + 1) * 128],
                                              xnT[:, c, :], start=(c == 0), stop=(c == CT - 1))
                    mm.then_inc(q_ready, 1)
                pe.wait_ge(v_kept, ONE + 2 * m)
                for r in range(NQ):
                    for c in range(CT):
                        mm = nc.tensor.matmul(ps_v[0:QT, r // 2, (r % 2) * C:(r % 2 + 1) * C],
                                              xnT[:, c, r * QT:(r + 1) * QT], w[:, c, 2 * C:3 * C],
                                              start=(c == 0), stop=(c == CT - 1))
                    if r % 2:
                        mm.then_inc(v_ready, 1)

            hidden(0, 0)
            turn(0)
            hidden(1, 1)
            project(0)
            turn(1)
            with pe.Fori(0, CHUNKS // 2 - 1) as m2:
                for i in range(2):
                    hidden(2 * m2 + i + 2, i)
                    project(2 * m2 + i + 1)
                    turn(2 * m2 + i + 2)
            project(CHUNKS - 1)

        @block.vector
        def _(dve):
            dve.wait_ge(consts_in, ONE + 16 * 5)

            def norm(m):
                dve.wait_ge(h_out, ONE + 16 * m)
                for a in range(2):
                    dve.wait_ge(h_ready, ONE + 2 * m + a + 1)
                    nc.vector.tensor_tensor(h1[:, 2 * a:2 * a + 2, :].rearrange("p r c -> p (r c)"), ps_h[0:QT, a, :],
                                            bias_out[:, 0:2, :].rearrange("p r c -> p (r c)"),
                                            ALU.add).then_inc(h_kept, 1)
                dve.wait_ge(h_kept, ONE + 2 * m + 2)
                for r in range(NQ):
                    nc.vector.bn_stats(stats[:, r, :], h1[:, r, :]).then_inc(stats_ready, 1)
                dve.wait_ge(stats_ready, ONE + NQ * (m + 1))
                nc.vector.tensor_tensor(both[:, :, :], stats[:, :, 1:3], stats[:, :, 4:6], ALU.add).then_inc(mv_ready, 1)
                nc.vector.tensor_tensor(apart[:, :], stats[:, :, 1], stats[:, :, 4], ALU.subtract).then_inc(mv_ready, 1)
                dve.wait_ge(mv_ready, ONE + 5 * m + 2)
                nc.vector.tensor_scalar(mean[:, :], both[:, :, 0], 0.5, None, ALU.mult).then_inc(mv_ready, 1)
                nc.vector.tensor_scalar(within[:, :], both[:, :, 1], 1.0 / C, EPS, ALU.mult,
                                        ALU.add).then_inc(mv_ready, 1)
                nc.vector.scalar_tensor_tensor(out=between[:, :], in0=apart[:, :], scalar=0.25, in1=apart[:, :],
                                               op0=ALU.mult, op1=ALU.mult).then_inc(mv_ready, 1)
                dve.wait_ge(mv_ready, ONE + 5 * (m + 1))
                nc.vector.tensor_tensor(veps[:, :], within[:, :], between[:, :], ALU.add).then_inc(veps_ready, 1)
                dve.wait_ge(rstd_ready, ONE + m + 1)
                dve.wait_ge(xT_ready, ONE + CT * m)
                for r in range(NQ):
                    nc.vector.tensor_scalar(xn[:, r, :], h1[:, r, :], mean[:, r:r + 1], rstd[:, r:r + 1],
                                            ALU.subtract, ALU.mult).then_inc(xn_ready, 1)

            def high(m):
                for job in range(QK):
                    dve.wait_ge(full_ready, ONE + QK * m + job + 1)
                    dve.wait_ge(lo_ready, ONE + QK * m + job - job % 2)
                    dve.wait_ge(parts_out[job % 2], ONE + 32 * (QK // 2 * m + job // 2))
                    nc.vector.tensor_copy(hi[job % 2][:, :], full[job % 2][:, :]).then_inc(hi_ready, 1)

            def keep_v(m):
                dve.wait_ge(v_out, ONE + 16 * m)
                for a in range(2):
                    dve.wait_ge(v_ready, ONE + 2 * m + a + 1)
                    nc.vector.tensor_tensor(v[:, 2 * a:2 * a + 2, :].rearrange("p r c -> p (r c)"), ps_v[0:QT, a, :],
                                            bias_v[:, 0:2, :].rearrange("p r c -> p (r c)"),
                                            ALU.add).then_inc(v_kept, 1)

            nc.vector.tensor_scalar(bias_col[:, 0:CT], bias_col[:, 0:CT], SCALE, None, ALU.mult).then_inc(bias_set, 1)
            norm(0)
            with dve.Fori(0, CHUNKS - 1) as m:
                norm(m + 1)
                high(m)
                keep_v(m)
            high(CHUNKS - 1)
            keep_v(CHUNKS - 1)

        @block.scalar
        def _(act):
            def keep_xT(m):
                act.wait_ge(v_ready, ONE + 2 * m)
                for c in range(CT):
                    act.wait_ge(xT_ready, ONE + CT * m + c + 1)
                    nc.scalar.activation(xnT[:, c, :], ps_x[:, c, 0:CH], ACT.Copy).then_inc(xT_kept, 1)

            def keep(m):
                for job in range(QK):
                    act.wait_ge(q_ready, ONE + QK * m + job + 1)
                    act.wait_ge(lo_ready, ONE + QK * m + job - job % 2)
                    nc.scalar.activation(full[job % 2][:, :], ps_q[:, job % 2, 0:CH], ACT.Identity,
                                         bias=bias_col[:, job:job + 1],
                                         scale=SCALE if job < CT else 1.0).then_inc(full_ready, 1)

            act.wait_ge(bias_set, ONE + 1)
            keep_xT(0)
            with act.Fori(0, CHUNKS - 1) as m:
                keep(m)
                keep_xT(m + 1)
            keep(CHUNKS - 1)


def full_attention(nc, d):
    with ExitStack() as ctx:
        sb = lambda n, s, t=F32: ctx.enter_context(nc.sbuf_tensor(n, s, t))
        ps = lambda n, s: ctx.enter_context(nc.psum_tensor(n, s, F32))
        sems = []

        def sem(name):
            sems.append(ctx.enter_context(nc.semaphore(name)))
            return sems[-1]

        keys = [sb(f"keys{g}", [STACK + 1, HG, N], F32R) for g in range(G)]
        queries = [sb(f"queries{g}", [STACK + 1, HG, CH], F32R) for g in range(G)]
        values = [sb(f"values{g}", [128, KT, HG * DH]) for g in range(G)]
        corner_hi = [sb(f"corner_hi3{g}", [128, HG, 2 * QT], F32R) for g in range(G)]
        corner_lo = [sb(f"corner_lo3{g}", [128, HG, 128], F32R) for g in range(G)]
        prob = sb("prob3", [128, SLOTS, HG, CH])
        pair_sum = [sb(f"pair_sum{i}", [128, HG, CH]) for i in range(2)]
        ident = sb("ident3", [128, 128])
        ident_r = sb("ident_r", [128, 128], F32R)
        ones = sb("ones3", [128, 2, DH])
        tops = sb("tops", [QT, HG * NQ, PER_IMAGE])
        shift = sb("shift", [QT, HG * NQ])
        shift_rows = [sb(f"shift_rows{p}", [HG * NQ // 2, QT], F32R) for p in range(2)]
        den = sb("den3", [128, CH])
        out = [sb(f"out{i}", [128, CH]) for i in range(G)]
        SB = 3
        MB = 3
        ps_s = ps("ps_s3", [128, SB, 512])
        ps_m = ps("ps_m", [128, MB, 512])
        ps_o = ps("ps_o", [128, 512])
        ps_d = ps("ps_d", [128, 512])
        s_ready, exp_done, tile_used, d_used, summed = (
            sem("s_ready3"), sem("exp_done"), sem("tile_used"), sem("d_used"), sem("summed"))
        m_ready, m_used, tops_ready = sem("m_ready"), sem("m_used"), sem("tops_ready")
        id_zero, id_set, idr_set, ones_set = sem("id_zero3"), sem("id_set3"), sem("idr_set"), sem("ones_set3")
        k_in = [[sem(f"k_in{g}_{j}") for j in range(HG)] for g in range(G)]
        keys_ready = [sem(f"keys_ready{j}") for j in range(HG)]
        v_in, q_in = [sem(f"v_in{g}") for g in range(G)], [sem(f"q_in{g}") for g in range(G)]
        corner_in = [sem(f"corner_in{g}") for g in range(G)]
        shift_ready, rows_ready, rows_kept = sem("shift_ready"), sem("rows_ready"), sem("rows_kept")
        shift_in = [sem(f"shift_in{p}") for p in range(2)]
        o_kept, den_kept, recip_done, out_ready = sem("o_kept3"), sem("den_kept"), sem("recip_done"), sem("out_ready")
        out_out = [sem(f"out_out{g}") for g in range(G)]
        HALVES = G * CHUNKS
        TILES = HG * KT
        MAXES = HG * NQ * PER_IMAGE
        PAIRED = (KT - 1) // 2
        D_ITEMS = PAIRED + 1
        BEHIND = SLOTS - 1
        RECIPS = 8
        TURNS = (MAXES // 2 + 4, MAXES)
        start_counts(nc, sems, {tile_used: BEHIND})

        block = ctx.enter_context(nc.Block())

        def score_bank(g, i):
            return (i + g) % SB

        def bank_before(g, i):
            if i >= SB:
                return i - SB + 1
            return max(k for k in range(TILES) if score_bank(1 - g, k) == score_bank(g, i)) + 1 - TILES

        def keys_of(t):
            return (0, FIRST) if t == 0 else (FIRST + 128 * (t - 1), 128)

        @block.sync
        def _(sp):
            def scored(n, g):
                sp.wait_ge(s_ready, ONE + TILES * (2 * n + g - 1))

            def load_keys(b, g):
                if b is not FIRST_IMAGE:
                    scored(b * PER_IMAGE, g)
                for j in range(HG):
                    for row, part in ((0, 0), (DH, 1), (2 * DH, 0)):
                        src = d.k[bass.ds(b * PER_IMAGE, PER_IMAGE), g, part, j * DH:(j + 1) * DH]
                        sp.dma_start(keys[g][row:row + DH, j, :].rearrange("p (c n) -> p c n", c=PER_IMAGE).bitcast(F32),
                                     src.rearrange("c d n -> d c n")).then_inc(k_in[g][j], 16)

            def load_values(b, g):
                if b is not FIRST_IMAGE:
                    sp.wait_ge(tile_used, ONE + BEHIND + KT * (2 * PER_IMAGE * b - 1 + g))
                cols = slice(g * HG * DH, (g + 1) * HG * DH)
                sp.dma_start(values[g][0:FIRST, 0, :], d.v_rows[b, 0:FIRST, cols]).then_inc(v_in[g], 16)
                sp.dma_start(values[g][:, 1:KT, :],
                             d.v_rows[b, FIRST:N, cols].rearrange("(t p) c -> p t c", p=128)).then_inc(v_in[g], 16)

            def tell_keys(b, g, first_of_image):
                for j in range(HG):
                    if first_of_image:
                        sp.wait_ge(k_in[g][j], ONE + 48 * (b + 1))
                        if j == HG - 1:
                            sp.wait_ge(v_in[g], ONE + 32 * (b + 1))
                    sp.sem_inc(keys_ready[j], 1)

            def load_queries(n, g, corner_or_zero):
                if n is not FIRST_IMAGE:
                    scored(n, g)
                for row, part in ((0, 0), (DH, 0), (2 * DH, 1)):
                    sp.dma_start(queries[g][row:row + DH, :, :].bitcast(F32),
                                 d.q[n, g, part].rearrange("(j d) n -> d j n", j=HG)).then_inc(q_in[g], 16)
                sp.dma_start(corner_hi[g][:, :, 0:128].bitcast(F32), corner_or_zero[g, :, 0]).then_inc(corner_in[g], 16)
                sp.dma_start(corner_lo[g][:, :, :].bitcast(F32), corner_or_zero[g, :, 1]).then_inc(corner_in[g], 16)

            def shifts(h, g):
                for p in range(2):
                    sp.wait_ge(rows_kept, ONE + 2 * h + p + 1)
                    sp.dma_start(queries[g][STACK:STACK + 1, 2 * p:2 * p + 2, :].rearrange("p j n -> p (j n)"
                                                                                            ).bitcast(F32),
                                 shift_rows[p][:, :].bitcast(F32)).then_inc(shift_in[p], 16)

            def store(h, g):
                sp.wait_ge(out_ready, ONE + h + 1)
                sp.dma_start(d.a2[h], out[g][:, :]).then_inc(out_out[g], 16)

            def chunk(b, n, first_of_image, corner_or_zero):
                for g in range(G):
                    load_queries(n, g, corner_or_zero)
                    if first_of_image:
                        load_keys(b, g)
                        load_values(b, g)
                    tell_keys(b, g, first_of_image)
                    if n is not FIRST_IMAGE:
                        store(2 * n - 2 + g, g)
                    shifts(2 * n + g, g)

            FIRST_IMAGE = 0
            chunk(FIRST_IMAGE, FIRST_IMAGE, True, d.corner)
            with sp.Fori(1, PER_IMAGE) as c:
                chunk(FIRST_IMAGE, c, False, d.no_corner)
            with sp.Fori(1, B) as b:
                chunk(b, b * PER_IMAGE, True, d.corner)
                with sp.Fori(1, PER_IMAGE) as c:
                    chunk(b, b * PER_IMAGE + c, False, d.no_corner)
            for g in range(G):
                store(HALVES - G + g, g)
            for g in range(G):
                sp.wait_ge(out_out[g], ONE + 16 * CHUNKS)

        @block.gpsimd
        def _(pool):
            nc.gpsimd.memset(ident[:, :], 0.0).then_inc(id_zero, 1)
            pool.wait_ge(id_zero, ONE + 1)
            nc.gpsimd.affine_select(out=ident[:, :], in_=ident[:, :], compare_op=ALU.not_equal, fill=1.0, base=0,
                                    pattern=[[-1, 128]], channel_multiplier=1).then_inc(id_set, 1)
            pool.wait_ge(id_set, ONE + 1)
            nc.gpsimd.tensor_copy(ident_r[:, :], ident[:, :]).then_inc(idr_set, 1)
            nc.gpsimd.memset(ones[:, 1, :], 1.0).then_inc(ones_set, 1)
            for g in range(G):
                nc.gpsimd.memset(corner_hi[g][:, :, 128:2 * QT].bitcast(F32), 0.0).then_inc(ones_set, 1)

            def add(h, k, has_before):
                pool.wait_ge(exp_done, ONE + h * TILES + HG * (2 * k + 1))
                if has_before or k > 2:
                    pool.wait_ge(d_used, ONE + h * D_ITEMS + (k - 1 if k > 2 else k - 2))
                nc.gpsimd.tensor_tensor(pair_sum[k % 2][:, :, :], prob[:, (2 * k - 1) % SLOTS, :, :],
                                        prob[:, 2 * k % SLOTS, :, :], ALU.add).then_inc(summed, 1)

            for k in range(1, PAIRED + 1):
                add(0, k, False)
            with pool.Fori(1, HALVES) as h:
                for k in range(1, PAIRED + 1):
                    add(h, k, True)

        @block.tensor
        def _(pe):
            pe.wait_ge(idr_set, ONE + 1)
            pe.wait_ge(ones_set, ONE + 4 + 3 * G)

            def score(h, g, t, j, has_before):
                at, k = keys_of(t)
                i = HG * t + j
                if t == 0 and j % 2 == 0:
                    pe.wait_ge(shift_in[j // 2], ONE + 16 * (h + 1))
                if has_before or i >= SB:
                    pe.wait_ge(exp_done, ONE + h * TILES + bank_before(g, i))
                o = ps_s[0:k, score_bank(g, i), :]
                last = t == KT - 1
                mm = nc.tensor.matmul(o[:, 0:CH], keys[g][:, j, at:at + k], queries[g][:, j, :],
                                      start=True, stop=not last, skip_group_check=last)
                if last:
                    for part in (corner_hi, corner_lo):
                        mm = nc.tensor.matmul(o[:, 0:128], ident_r[:, :], part[g][:, j, 0:128],
                                              start=False, stop=part is corner_lo, skip_group_check=True)
                mm.then_inc(s_ready, 1)

            def weigh(h, g, t):
                pe.wait_ge(exp_done, ONE + h * TILES + HG * (t + 1))
                if t == 0:
                    pe.wait_ge(o_kept, ONE + h)
                for j in range(HG):
                    mm = nc.tensor.matmul(ps_o[j * DH:(j + 1) * DH, 0:CH], values[g][:, t, j * DH:(j + 1) * DH],
                                          prob[:, t % SLOTS, j, :], start=(t == 0), stop=(t == KT - 1))
                mm.then_inc(tile_used, 1)

            def total(h, k):
                if k == 0:
                    pe.wait_ge(den_kept, ONE + h)
                else:
                    pe.wait_ge(summed, ONE + h * PAIRED + k)
                for j in range(HG):
                    moving = prob[:, 0, j, :] if k == 0 else pair_sum[k % 2][:, j, :]
                    mm = nc.tensor.matmul(ps_d[j * DH:(j + 1) * DH, 0:CH], ones[:, int(k > 0), :], moving,
                                          start=(k == 0), stop=(k == PAIRED))
                mm.then_inc(d_used, 1)

            def maximum(h, g, chunk, i):
                if i == 0:
                    pe.wait_ge(q_in[g], ONE + 48 * (chunk + 1))
                j, r, c = i // (NQ * PER_IMAGE), i // PER_IMAGE % NQ, i % PER_IMAGE
                if i % (NQ * PER_IMAGE) == 0:
                    pe.wait_ge(keys_ready[j], ONE + h + 1)
                if i in (0, TURNS[0] + MB - 1):
                    pe.wait_ge(rows_kept, ONE + 2 * h + int(i > 0))
                pe.wait_ge(m_used, ONE + h * MAXES + max(0, i - MB + 1))
                o = ps_m[0:QT, i % MB, :]
                last = c == PER_IMAGE - 1 and r < 2
                if i == PER_IMAGE - 1:
                    pe.wait_ge(corner_in[g], ONE + 32 * (chunk + 1))
                mm = nc.tensor.matmul(o[:, 0:CH], queries[g][0:STACK, j, r * QT:(r + 1) * QT],
                                      keys[g][0:STACK, j, c * CH:(c + 1) * CH],
                                      start=True, stop=not last, skip_group_check=last)
                if last:
                    mm = nc.tensor.matmul(o[:, CH - 128:CH], corner_hi[g][:, j, r * QT:(r + 1) * QT],
                                          ident_r[:, :], start=False, stop=True, skip_group_check=True)
                mm.then_inc(m_ready, 1)

            def turn(h, p):
                pe.wait_ge(shift_ready, ONE + 2 * h + p + 1)
                pe.wait_ge(m_used, ONE + h * MAXES + TURNS[p])
                nc.tensor.transpose(ps_m[0:HG * NQ // 2, (TURNS[p] - 1) % MB, 0:QT],
                                    shift[:, p * HG * NQ // 2:(p + 1) * HG * NQ // 2],
                                    ident[0:QT, 0:QT]).then_inc(rows_ready, 1)

            SPREAD = 6
            LEAD, TAIL = 1, 2

            def half(h, g, chunk_next, has_next, has_before):
                done, turned = 0, 0
                slots = 0
                total_slots = SPREAD * (KT - LEAD - TAIL)

                def spread():
                    nonlocal done, turned, slots
                    if not has_next or t < LEAD:
                        return
                    slots += 1
                    while done < min(MAXES, -(-MAXES * slots // total_slots)):
                        if turned == 0 and done == TURNS[0]:
                            turn(h + 1, 0)
                            turned = 1
                        maximum(h + 1, 1 - g, chunk_next, done)
                        done += 1

                for t in range(KT):
                    score(h, g, t, 0, has_before)
                    spread()
                    score(h, g, t, 1, has_before)
                    spread()
                    score(h, g, t, 2, has_before)
                    spread()
                    if t > 0:
                        weigh(h, g, t - 1)
                    elif has_before:
                        weigh(h - 1, 1 - g, KT - 1)
                    spread()
                    score(h, g, t, 3, has_before)
                    spread()
                    if has_next and t == KT - TAIL:
                        turn(h + 1, 1)
                    if t in (0, 2) and has_before:
                        total(h - 1, PAIRED - 1 + int(t == 2))
                    if t == 4:
                        total(h, 0)
                    if t >= 5 and t % 2:
                        total(h, (t - 3) // 2)
                    spread()

            for i in range(MAXES):
                if i == TURNS[0]:
                    turn(0, 0)
                maximum(0, 0, 0, i)
            turn(0, 1)
            half(0, 0, 0, True, False)
            with pe.Fori(0, CHUNKS - 1) as n:
                half(2 * n + 1, 1, n + 1, True, True)
                half(2 * n + 2, 0, n + 1, True, True)
            half(HALVES - 1, 1, 0, False, True)
            weigh(HALVES - 1, 1, KT - 1)
            total(HALVES - 1, PAIRED - 1)
            total(HALVES - 1, PAIRED)

        @block.scalar
        def _(act):
            def keep_den(h):
                act.wait_ge(d_used, ONE + D_ITEMS * (h + 1))
                act.wait_ge(out_ready, ONE + h)
                nc.scalar.activation(den[:, :], ps_d[:, 0:CH], ACT.Copy).then_inc(den_kept, 1)

            def half(h, g, has_before):
                for t in range(KT):
                    at, k = keys_of(t)
                    act.wait_ge(tile_used, ONE + h * KT + t)
                    if t > SLOTS:
                        act.wait_ge(summed, ONE + h * PAIRED + (t - SLOTS + 1) // 2)
                    elif t == SLOTS:
                        act.wait_ge(d_used, ONE + h * D_ITEMS + 1)
                    elif has_before:
                        act.wait_ge(summed, ONE + (h - 1) * PAIRED + (t + KT - SLOTS + 1) // 2)
                    for j in range(HG):
                        i = HG * t + j
                        act.wait_ge(s_ready, ONE + h * TILES + i + 1)
                        nc.scalar.activation(prob[0:k, t % SLOTS, j, :], ps_s[0:k, score_bank(g, i), 0:CH],
                                             ACT.Exp).then_inc(exp_done, 1)
                    if t == 3 and has_before:
                        keep_den(h - 1)

            half(0, 0, False)
            with act.Fori(0, CHUNKS - 1) as n:
                half(2 * n + 1, 1, True)
                half(2 * n + 2, 0, True)
            half(HALVES - 1, 1, True)
            keep_den(HALVES - 1)

        @block.vector
        def _(dve):
            half_max = MAXES // 2

            def maximum(h, i):
                dve.wait_ge(m_ready, ONE + h * MAXES + i + 1)
                nc.vector.tensor_reduce(tops[:, i // PER_IMAGE, i % PER_IMAGE:i % PER_IMAGE + 1],
                                        ps_m[0:QT, i % MB, 0:CH], AX.X, ALU.max).then_inc(m_used, 1)
                if i % half_max == half_max - 1:
                    p = i // half_max
                    rows = slice(p * HG * NQ // 2, (p + 1) * HG * NQ // 2)
                    dve.wait_ge(m_used, ONE + h * MAXES + i + 1)
                    nc.vector.tensor_reduce(shift[:, rows], tops[:, rows, :], AX.X, ALU.max,
                                            negate=True).then_inc(shift_ready, 1)
                if i + 1 in TURNS:
                    p = TURNS.index(i + 1)
                    dve.wait_ge(rows_ready, ONE + 2 * h + p + 1)
                    dve.wait_ge(shift_in[p], ONE + 16 * h)
                    nc.vector.tensor_copy(shift_rows[p][:, :], ps_m[0:HG * NQ // 2, i % MB, 0:QT]
                                          ).then_inc(rows_kept, 1)

            def keep_out(h, g):
                dve.wait_ge(tile_used, ONE + BEHIND + KT * (h + 1))
                dve.wait_ge(out_out[g], ONE + 8 * (h - g))
                nc.vector.tensor_copy(out[g][:, :], ps_o[:, 0:CH]).then_inc(o_kept, 1)

            def recip(h, piece):
                w = CH // RECIPS
                if piece == 0:
                    dve.wait_ge(den_kept, ONE + h + 1)
                nc.vector.reciprocal(den[:, piece * w:(piece + 1) * w],
                                     den[:, piece * w:(piece + 1) * w]).then_inc(recip_done, 1)

            def normalize(h, g):
                dve.wait_ge(recip_done, ONE + RECIPS * (h + 1))
                nc.vector.tensor_tensor(out[g][:, :], out[g][:, :], den[:, :], ALU.mult).then_inc(out_ready, 1)

            FIRST_RECIP, RECIP_STEP = 16, 8

            def half(h, g):
                keep_out(h, g)
                for i in range(MAXES):
                    maximum(h + 2, i)
                    piece, off = divmod(i - FIRST_RECIP, RECIP_STEP)
                    if off == 0 and 0 <= piece < RECIPS:
                        recip(h, piece)
                    if off == 0 and piece == RECIPS:
                        normalize(h, g)

            nc.vector.memset(ones[0:FIRST, 0, :], 1.0).then_inc(ones_set, 1)
            nc.vector.memset(ones[FIRST:128, 0, :], 0.0).then_inc(ones_set, 1)
            nc.vector.memset(prob[FIRST:128, 0, :, :], 0.0).then_inc(ones_set, 1)
            for g in range(G):
                nc.vector.memset(values[g][FIRST:128, 0, :], 0.0).then_inc(ones_set, 1)
                nc.vector.memset(keys[g][STACK:STACK + 1, :, :].bitcast(F32), 1.0).then_inc(ones_set, 1)
            for h in range(2):
                for i in range(MAXES):
                    maximum(h, i)
            with dve.Fori(0, CHUNKS - 1) as n:
                half(2 * n, 0)
                half(2 * n + 1, 1)
            for h, g in ((HALVES - 2, 0), (HALVES - 1, 1)):
                keep_out(h, g)
                for piece in range(RECIPS):
                    recip(h, piece)
                normalize(h, g)


def gated_ffn(nc, d):
    with ExitStack() as outer:
        osb = lambda n, s, t=F32: outer.enter_context(nc.sbuf_tensor(n, s, t))
        xnT = osb("xnT4", [128, CHUNKS, CT, CH])
        gate = osb("gate", [QT, B, PER_IMAGE * NQ])
        project_out(nc, d, xnT, gate)
        ffn(nc, d, xnT, gate)


def project_out(nc, d, xnT, gate):
    with ExitStack() as ctx:
        sb = lambda n, s, t=F32: ctx.enter_context(nc.sbuf_tensor(n, s, t))
        ps = lambda n, s: ctx.enter_context(nc.psum_tensor(n, s, F32))
        sems = []

        def sem(name):
            sems.append(ctx.enter_context(nc.semaphore(name)))
            return sems[-1]

        w = sb("w_proj", [128, CT, C])
        bias = sb("bias_proj", [QT, NQ, C])
        w_gate = sb("w_gate", [QT, C])
        b_gate = sb("b_gate", [QT, 1])
        ident = sb("ident4", [128, 128])
        minus_half = sb("minus_half4", [QT, NQ])
        aT = [sb(f"aT4{i}", [128, G, CH]) for i in range(2)]
        h1 = [sb(f"h1b{i}", [QT, NQ, C]) for i in range(2)]
        h1b = sb("h1_biased", [QT, NQ, C])
        h2 = [sb(f"h2{i}", [QT, NQ, C]) for i in range(2)]
        stats = sb("stats4", [QT, NQ, 6])
        both = sb("both4", [QT, NQ, 2])
        apart, mean, within, between = (sb(n, [QT, NQ]) for n in ("apart4", "mean4", "within4", "between4"))
        veps = sb("veps4", [QT, NQ])
        rstd = sb("rstd4", [QT, NQ])
        xn = [sb(f"xn4{i}", [QT, NQ, C]) for i in range(2)]
        base = [sb(f"base{i}", [QT, NQ, C]) for i in range(2)]
        product = sb("product", [QT, NQ, C])
        dots = sb("dots", [QT, NQ])
        ps_h = ps("ps_h4", [128, 2, 512])
        ps_x = ps("ps_x4", [128, 2, 512])
        consts_in, id_zero, id_set, half_set = sem("consts_in4"), sem("id_zero4"), sem("id_set4"), sem("half_set4")
        a_in = [sem(f"a_in4{i}") for i in range(2)]
        biased, h_ready, h_kept = sem("biased"), sem("h_ready4"), sem("h_kept4")
        stats_ready, mv_ready, veps_ready, rstd_ready, xn_ready = (
            sem("stats_ready4"), sem("mv_ready4"), sem("veps_ready4"), sem("rstd_ready4"), sem("xn_ready4"))
        xT_ready, xT_kept, base_ready = sem("xT_ready4"), sem("xT_kept4"), sem("base_ready")
        base_out = [sem(f"base_out{i}") for i in range(2)]
        dots_ready, gate_ready, gate_out = sem("dots_ready"), sem("gate_ready"), sem("gate_out")
        start_counts(nc, sems, {base_ready: 1, xT_ready: CT})
        block = ctx.enter_context(nc.Block())

        @block.sync
        def _(sp):
            sp.dma_start(w[:, :, :], d.w_proj.rearrange("(t p) n -> p t n", p=128)).then_inc(consts_in, 16)
            sp.dma_start(bias[:, :, :], view(d.b_proj, 0, [[0, QT], [0, NQ], [1, C]])).then_inc(consts_in, 16)
            sp.dma_start(w_gate[:, :], view(d.w_gate, 0, [[0, QT], [1, C]])).then_inc(consts_in, 16)
            sp.dma_start(b_gate[:, :], view(d.b_gate, 0, [[0, QT], [1, 1]])).then_inc(consts_in, 16)

            def load(m, i):
                for g in range(G):
                    sp.dma_start(aT[i][:, g, :], d.a2[2 * m + g]).then_inc(a_in[i], 16)
                sp.dma_start(h1[i][:, :, :], d.h1[m]).then_inc(a_in[i], 16)

            def store(m, i):
                sp.wait_ge(base_ready, ONE + m + 2)
                sp.dma_start(d.base[m], base[i][:, :, :]).then_inc(base_out[i], 16)

            load(0, 0)
            load(1, 1)
            with sp.Fori(0, CHUNKS // 2 - 1) as m2:
                for i in range(2):
                    m = 2 * m2 + i
                    sp.wait_ge(biased, ONE + m + 1)
                    sp.wait_ge(h_ready, ONE + 2 * m + 2)
                    load(m + 2, i)
                    store(m, i)
            store(CHUNKS - 2, 0)
            store(CHUNKS - 1, 1)
            for i in range(2):
                sp.wait_ge(base_out[i], ONE + 8 * CHUNKS)
            sp.wait_ge(gate_ready, ONE + CHUNKS)
            for b in range(B):
                sp.dma_start(d.gate[b].rearrange("(i p) -> p i", p=QT), gate[:, b, :],
                             allow_slow_non_contiguous=True).then_inc(gate_out, 16)
            sp.wait_ge(gate_out, ONE + 16 * B)

        @block.gpsimd
        def _(pool):
            nc.gpsimd.memset(ident[:, :], 0.0).then_inc(id_zero, 1)
            pool.wait_ge(id_zero, ONE + 1)
            nc.gpsimd.affine_select(out=ident[:, :], in_=ident[:, :], compare_op=ALU.not_equal, fill=1.0, base=0,
                                    pattern=[[-1, 128]], channel_multiplier=1).then_inc(id_set, 1)
            nc.gpsimd.memset(minus_half[:, :], -0.5).then_inc(half_set, 1)
            pool.wait_ge(half_set, ONE + 1)
            pool.wait_ge(consts_in, ONE + 64)

            def add_bias(m, i):
                pool.wait_ge(a_in[i], ONE + 24 * (m - i) + 48)
                pool.wait_ge(h_kept, ONE + 2 * m)
                nc.gpsimd.tensor_tensor(h1b[:, :, :], h1[i][:, :, :], bias[:, :, :], ALU.add).then_inc(biased, 1)

            def root(m):
                pool.wait_ge(veps_ready, ONE + m + 1)
                nc.gpsimd.tensor_tensor(rstd[:, :], veps[:, :], minus_half[:, :], ALU.pow).then_inc(rstd_ready, 1)

            def add_base(m, i):
                pool.wait_ge(xn_ready, ONE + NQ * (m + 1))
                pool.wait_ge(base_out[i], ONE + 8 * (m - i))
                nc.gpsimd.tensor_tensor(base[i][:, :, :], h2[i][:, :, :], xn[i][:, :, :], ALU.add).then_inc(base_ready, 1)

            add_bias(0, 0)
            with pool.Fori(0, CHUNKS // 2 - 1) as m2:
                for i in range(2):
                    m = 2 * m2 + i
                    root(m)
                    add_bias(m + 1, 1 - i)
                    add_base(m, i)
            root(CHUNKS - 2)
            add_bias(CHUNKS - 1, 1)
            add_base(CHUNKS - 2, 0)
            root(CHUNKS - 1)
            add_base(CHUNKS - 1, 1)

        @block.tensor
        def _(pe):
            pe.wait_ge(consts_in, ONE + 64)
            pe.wait_ge(id_set, ONE + 1)

            def hidden(m, i):
                pe.wait_ge(a_in[i], ONE + 24 * (m - i) + 48)
                pe.wait_ge(h_kept, ONE + 2 * m)
                for r in range(NQ):
                    for c in range(CT):
                        mm = nc.tensor.matmul(ps_h[0:QT, r // 2, (r % 2) * C:(r % 2 + 1) * C],
                                              aT[i][:, c, r * QT:(r + 1) * QT], w[:, c, :],
                                              start=(c == 0), stop=(c == CT - 1))
                    if r % 2:
                        mm.then_inc(h_ready, 1)

            def turn(m, i):
                pe.wait_ge(xn_ready, ONE + NQ * (m + 1))
                pe.wait_ge(xT_kept, ONE + CT * m)
                for c in range(CT):
                    for r in range(NQ):
                        mm = nc.tensor.transpose(ps_x[:, c, r * QT:(r + 1) * QT], xn[i][:, r, c * 128:(c + 1) * 128],
                                                 ident[0:QT, 0:QT])
                    mm.then_inc(xT_ready, 1)

            hidden(0, 0)
            with pe.Fori(0, CHUNKS // 2 - 1) as m2:
                hidden(2 * m2 + 1, 1)
                turn(2 * m2, 0)
                hidden(2 * m2 + 2, 0)
                turn(2 * m2 + 1, 1)
            hidden(CHUNKS - 1, 1)
            turn(CHUNKS - 2, 0)
            turn(CHUNKS - 1, 1)

        @block.scalar
        def _(act):
            with act.Fori(0, CHUNKS) as m:
                for c in range(CT):
                    act.wait_ge(xT_ready, ONE + CT * (m + 1) + c + 1)
                    nc.scalar.activation(xnT[:, m, c, :], ps_x[:, c, 0:CH], ACT.Copy).then_inc(xT_kept, 1)

        @block.vector
        def _(dve):
            dve.wait_ge(consts_in, ONE + 64)

            def norm(m, i, gates):
                dve.wait_ge(biased, ONE + m + 1)
                dve.wait_ge(base_ready, ONE + m)
                for a in range(2):
                    dve.wait_ge(h_ready, ONE + 2 * m + a + 1)
                    nc.vector.tensor_tensor(h2[i][:, 2 * a:2 * a + 2, :].rearrange("p r c -> p (r c)"), ps_h[0:QT, a, :],
                                            h1b[:, 2 * a:2 * a + 2, :].rearrange("p r c -> p (r c)"),
                                            ALU.add).then_inc(h_kept, 1)
                dve.wait_ge(h_kept, ONE + 2 * m + 2)
                for r in range(NQ):
                    nc.vector.bn_stats(stats[:, r, :], h2[i][:, r, :]).then_inc(stats_ready, 1)
                dve.wait_ge(stats_ready, ONE + NQ * (m + 1))
                nc.vector.tensor_tensor(both[:, :, :], stats[:, :, 1:3], stats[:, :, 4:6], ALU.add).then_inc(mv_ready, 1)
                nc.vector.tensor_tensor(apart[:, :], stats[:, :, 1], stats[:, :, 4], ALU.subtract).then_inc(mv_ready, 1)
                dve.wait_ge(mv_ready, ONE + 5 * m + 2)
                nc.vector.tensor_scalar(mean[:, :], both[:, :, 0], 0.5, None, ALU.mult).then_inc(mv_ready, 1)
                nc.vector.tensor_scalar(within[:, :], both[:, :, 1], 1.0 / C, EPS, ALU.mult,
                                        ALU.add).then_inc(mv_ready, 1)
                nc.vector.scalar_tensor_tensor(out=between[:, :], in0=apart[:, :], scalar=0.25, in1=apart[:, :],
                                               op0=ALU.mult, op1=ALU.mult).then_inc(mv_ready, 1)
                dve.wait_ge(mv_ready, ONE + 5 * (m + 1))
                nc.vector.tensor_tensor(veps[:, :], within[:, :], between[:, :], ALU.add).then_inc(veps_ready, 1)
                dve.wait_ge(rstd_ready, ONE + m + 1)
                dve.wait_ge(xT_ready, ONE + CT * m)
                for r in range(NQ):
                    nc.vector.tensor_scalar(xn[i][:, r, :], h2[i][:, r, :], mean[:, r:r + 1], rstd[:, r:r + 1],
                                            ALU.subtract, ALU.mult).then_inc(xn_ready, 1)
                for r in range(NQ):
                    dve.wait_ge(xn_ready, ONE + NQ * m + r + 1)
                    nc.vector.tensor_tensor_reduce(product[:, r, :], xn[i][:, r, :], w_gate[:, :], 1.0, 0.0, ALU.mult,
                                                   ALU.add, dots[:, r:r + 1]).then_inc(dots_ready, 1)
                dve.wait_ge(dots_ready, ONE + NQ * (m + 1))
                nc.vector.tensor_scalar(gates, dots[:, :], b_gate[:, 0:1], None, ALU.add).then_inc(gate_ready, 1)

            flat = gate[:, :, :].rearrange("p b i -> p (b i)")
            with dve.Fori(0, CHUNKS // 2) as m2:
                for i in range(2):
                    m = 2 * m2 + i
                    norm(m, i, flat[:, bass.ds(m * NQ, NQ)])


def ffn(nc, d, xnT, gate):
    with ExitStack() as ctx:
        sb = lambda n, s, t=F32: ctx.enter_context(nc.sbuf_tensor(n, s, t))
        ps = lambda n, s: ctx.enter_context(nc.psum_tensor(n, s, F32))
        sems = []

        def sem(name):
            sems.append(ctx.enter_context(nc.semaphore(name)))
            return sems[-1]

        TILES = N // QT
        w_up = sb("w_up", [128, CT, HID])
        w_down = sb("w_down", [128, HT, C])
        b_up = sb("b_up", [128, HT])
        b_down = sb("b_down", [QT, C])
        row = [sb(f"gate_row{i}", [QT, N]) for i in range(2)]
        own = sb("own", [QT, TILES])
        hits = sb("hits", [QT, 2, N], mybir.dt.bfloat16)
        ties = sb("ties", [QT, 2, QT], mybir.dt.bfloat16)
        count = sb("count", [QT, TILES, 4])
        rank = sb("rank", [QT, TILES])
        kept = sb("kept", [QT, TILES])
        earlier = sb("earlier", [QT, QT])
        base = [sb(f"base5{i}", [QT, NQ, C]) for i in range(3)]
        coefs = [sb(f"coefs{i}", [QT, TILES]) for i in range(2)]
        hT = sb("hT", [128, HT, CH])
        y = sb("y", [QT, NQ, C])
        out = sb("out5", [QT, NQ, C])
        ps_h = ps("ps_h5", [128, 4, 512])
        ps_y = ps("ps_y", [128, 4, 512])
        base_in = [sem(f"base_in{i}") for i in range(3)]
        row_in = [sem(f"row_in{i}") for i in range(2)]
        consts_in, h_ready, h_kept = sem("consts_in5"), sem("h_ready5"), sem("h_kept5")
        y_ready, y_kept, out_ready, out_out = sem("y_ready"), sem("y_kept"), sem("out_ready5"), sem("out_out5")
        tri_one, tri_set, zero_set = sem("tri_one"), sem("tri_set"), sem("zero_set5")
        own_ready, counted, ranked, kept_ready, coefs_ready = (
            sem("own_ready"), sem("counted"), sem("ranked"), sem("kept_ready"), sem("coefs_ready"))
        start_counts(nc, sems)
        block = ctx.enter_context(nc.Block())
        OPS = 4 * TILES - 2
        BUFFER = [j % 2 for j in range(PER_IMAGE - 1)] + [2]
        USES = [BUFFER.count(i) for i in range(3)]

        @block.sync
        def _(sp):
            sp.dma_start(row[0][:, :], view(d.gate, 0, [[0, QT], [1, N]])).then_inc(row_in[0], 16)
            sp.dma_start(w_up[:, :, :], d.w_up.rearrange("(t p) n -> p t n", p=128)).then_inc(consts_in, 16)
            sp.dma_start(w_down[:, :, :], d.w_down.rearrange("(t p) n -> p t n", p=128)).then_inc(consts_in, 16)
            sp.dma_start(b_up[:, :], d.b_up.rearrange("(t p) -> p t", p=128),
                         allow_slow_non_contiguous=True).then_inc(consts_in, 16)
            sp.dma_start(b_down[:, :], view(d.b_down, 0, [[0, QT], [1, C]])).then_inc(consts_in, 16)
            sp.dma_start(row[1][:, :], view(d.gate, N, [[0, QT], [1, N]])).then_inc(row_in[1], 16)

            def load(m, i):
                sp.dma_start(base[i][:, :, :], d.base[m]).then_inc(base_in[i], 16)

            def store(m):
                sp.wait_ge(out_ready, ONE + NQ * (m + 1))
                sp.dma_start(d.out[m].rearrange("(i p) c -> p i c", p=QT), out[:, :, :]).then_inc(out_out, 16)

            def image(b, last=False):
                for j in range(PER_IMAGE):
                    after = [k for k in range(j + 1, j + 1 + PER_IMAGE) if BUFFER[k % PER_IMAGE] == BUFFER[j]][0]
                    store(PER_IMAGE * b + j)
                    if after < PER_IMAGE or not last:
                        load(PER_IMAGE * b + after, BUFFER[j])

            for j, i in [(0, 0), (1, 1), (PER_IMAGE - 1, 2)]:
                load(j, i)
            for b in range(B):
                if 2 <= b + 1 < B:
                    sp.wait_ge(counted, ONE + OPS * b)
                    sp.dma_start(row[(b + 1) % 2][:, :], view(d.gate, (b + 1) * N, [[0, QT], [1, N]])
                                 ).then_inc(row_in[(b + 1) % 2], 16)
                image(b, b == B - 1)
            sp.wait_ge(out_out, ONE + 16 * CHUNKS)

        @block.gpsimd
        def _(pool):
            nc.gpsimd.memset(earlier[:, :], 1.0).then_inc(tri_one, 1)
            pool.wait_ge(tri_one, ONE + 1)
            nc.gpsimd.affine_select(out=earlier[:, :], in_=earlier[:, :], compare_op=ALU.is_gt, fill=0.0, base=0,
                                    pattern=[[-1, QT]], channel_multiplier=1).then_inc(tri_set, 1)

        @block.tensor
        def _(pe):
            pe.wait_ge(consts_in, ONE + 64)

            def up(m, t):
                if t < 4:
                    pe.wait_ge(h_kept, ONE + HT * m)
                else:
                    pe.wait_ge(h_kept, ONE + HT * m + t - 3)
                for c in range(CT):
                    mm = nc.tensor.matmul(ps_h[:, t % 4, 0:CH], w_up[:, c, t * 128:(t + 1) * 128], xnT[:, m, c, :],
                                          start=(c == 0), stop=(c == CT - 1))
                mm.then_inc(h_ready, 1)

            def down(m, r):
                pe.wait_ge(h_kept, ONE + HT * (m + 1))
                pe.wait_ge(y_kept, ONE + NQ * m)
                for t in range(HT):
                    mm = nc.tensor.matmul(ps_y[0:QT, r, 0:C], hT[:, t, r * QT:(r + 1) * QT], w_down[:, t, :],
                                          start=(t == 0), stop=(t == HT - 1))
                mm.then_inc(y_ready, 1)

            with pe.Fori(0, CHUNKS) as m:
                for t in range(HT):
                    up(m, t)
                for r in range(NQ):
                    down(m, r)

        @block.scalar
        def _(act):
            act.wait_ge(consts_in, ONE + 64)
            with act.Fori(0, CHUNKS) as m:
                act.wait_ge(y_ready, ONE + NQ * m)
                for t in range(HT):
                    act.wait_ge(h_ready, ONE + HT * m + t + 1)
                    nc.scalar.activation(hT[:, t, :], ps_h[:, t % 4, 0:CH], ACT.Gelu_apprx_tanh,
                                         bias=b_up[:, t:t + 1]).then_inc(h_kept, 1)

        @block.vector
        def _(dve):
            def take_own(b):
                nc.vector.tensor_copy(own[:, :], gate[:, b, :]).then_inc(own_ready, 1)
                dve.wait_ge(own_ready, ONE + b + 1)
                dve.wait_ge(row_in[b % 2], ONE + 16 * (b // 2 + 1))

            def compare(b, i):
                a, z = i * QT, (i + 1) * QT
                mine = own[:, i:i + 1]
                gates = row[b % 2]

                def tally(lo, hi, op, slot):
                    nc.vector.tensor_scalar(hits[:, i % 2, lo:hi], gates[:, lo:hi], mine, 0.0, op, ALU.add,
                                            accum_out=count[:, i, slot:slot + 1]).then_inc(counted, 1)

                if i > 1:
                    dve.wait_ge(counted, ONE + OPS * b + 4 * (i - 1) - 1)
                elif b > 0:
                    dve.wait_ge(ranked, ONE + b)
                if i > 0:
                    tally(0, a, ALU.is_ge, 0)
                if i < TILES - 1:
                    tally(z, N, ALU.is_gt, 1)
                tally(a, z, ALU.is_gt, 2)
                nc.vector.scalar_tensor_tensor(out=ties[:, i % 2, :], in0=gates[:, a:z], scalar=mine,
                                               in1=earlier[:, :], op0=ALU.is_equal, op1=ALU.mult,
                                               accum_out=count[:, i, 3:4]).then_inc(counted, 1)

            def settle(b):
                dve.wait_ge(counted, ONE + OPS * (b + 1))
                nc.vector.tensor_reduce(rank[:, :], count[:, :, :], AX.X, ALU.add).then_inc(ranked, 1)
                dve.wait_ge(ranked, ONE + b + 1)
                nc.vector.tensor_scalar(kept[:, :], rank[:, :], float(KEEP), None, ALU.is_lt).then_inc(kept_ready, 1)
                dve.wait_ge(kept_ready, ONE + b + 1)
                nc.vector.tensor_tensor(coefs[b % 2][:, :], own[:, :], kept[:, :], ALU.mult).then_inc(coefs_ready, 1)
                dve.wait_ge(coefs_ready, ONE + b + 1)

            def finish(b, j):
                m, i = PER_IMAGE * b + j, BUFFER[j]
                dve.wait_ge(base_in[i], ONE + 16 * (USES[i] * b + BUFFER[:j + 1].count(i)))
                dve.wait_ge(out_out, ONE + 16 * m)
                for r in range(NQ):
                    dve.wait_ge(y_ready, ONE + NQ * m + r + 1)
                    nc.vector.tensor_tensor(y[:, r, :], ps_y[0:QT, r, 0:C], b_down[:, :], ALU.add).then_inc(y_kept, 1)
                for r in range(NQ):
                    dve.wait_ge(y_kept, ONE + NQ * m + r + 1)
                    nc.vector.scalar_tensor_tensor(out=out[:, r, :], in0=y[:, r, :],
                                                   scalar=coefs[b % 2][:, j * NQ + r:j * NQ + r + 1],
                                                   in1=base[i][:, r, :], op0=ALU.mult, op1=ALU.add
                                                   ).then_inc(out_ready, 1)

            nc.vector.memset(count[:, :, :], 0.0).then_inc(zero_set, 1)
            dve.wait_ge(zero_set, ONE + 1)
            dve.wait_ge(tri_set, ONE + 1)
            dve.wait_ge(consts_in, ONE + 64)
            take_own(0)
            for i in range(TILES):
                compare(0, i)
            settle(0)
            for b in range(B):
                if b + 1 < B:
                    take_own(b + 1)
                for j in range(PER_IMAGE):
                    if b + 1 < B:
                        for i in range(j * NQ, (j + 1) * NQ):
                            compare(b + 1, i)
                    finish(b, j)
                if b + 1 < B:
                    settle(b + 1)


class Dram:
    pass


def vit_tower(nc, d):
    def scratch(name, shape, dt=F32):
        return nc.dram_tensor(name, shape, dt, kind="Internal").ap()

    d.win_bias = scratch("win_bias", [4, GROUP, GROUP])
    d.negs = scratch("negs", [28, 28])
    d.skew = scratch("skew", [NH * 128 * 257])
    d.corner = scratch("corner_parts", [G, 128, 2, HG, 128])
    d.no_corner = scratch("no_corner", [G, 128, 2, HG, 128])
    d.a1 = scratch("window_out", [UNITS, 128, CT, UNIT])
    d.h1 = scratch("hidden1", [CHUNKS, QT, NQ, C])
    d.q = scratch("q_parts", [CHUNKS, G, 2, 128, CH])
    d.k = scratch("k_parts", [CHUNKS, G, 2, 128, CH])
    d.v = scratch("v_rows_dram", [CHUNKS, CH, C])
    d.v_rows = d.v.rearrange("(b k) n c -> b (k n) c", b=B)
    d.a2 = scratch("attention_out", [G * CHUNKS, 128, CH])
    d.base = scratch("base_rows", [CHUNKS, QT, NQ, C])
    d.gate = scratch("gate_rows", [B, N])
    setup_tables(nc, d)
    window_attention(nc, d)
    project_qkv(nc, d)
    full_attention(nc, d)
    gated_ffn(nc, d)


def kernel(**inputs):
    import numpy as np
    import concourse.bacc as bacc
    from concourse import mybir as mb
    from concourse.bass_utils import run_bass_kernel_spmd as run

    def rolled(x, axis):
        k = WS // 2
        head, tail = np.split(x, [k], axis=axis)
        return np.concatenate([tail, head], axis=axis)

    x = rolled(rolled(np.asarray(inputs["x"]), 2), 3)
    w1 = np.asarray(inputs["L0_tok_w1"]).reshape(DH, NH, 3, C)
    arrays = {
        "x": x.reshape(B, CT, 128, SIDE // WS, WS, 2, HALFROW).transpose(0, 3, 2, 1, 5, 4, 6).reshape(
            UNITS, 128, CT, UNIT),
        "w_tok": w1.transpose(3, 2, 1, 0).reshape(C, 3 * C),
        "b_tok": np.asarray(inputs["L0_tok_b1"]).reshape(DH, NH, 3).transpose(2, 1, 0).reshape(3 * C),
        "w_tok_out": np.asarray(inputs["L0_tok_w2"]).T,
        "b_tok_out": inputs["L0_tok_b2"],
        "pos_emb": inputs["L0_tok_pos_emb"],
        "w_qkv": inputs["L0_attn_qkv_w"],
        "b_qkv": inputs["L0_attn_qkv_b"],
        "w_proj": inputs["L0_attn_proj_w"],
        "b_proj": inputs["L0_attn_proj_b"],
        "rpb": np.asarray(inputs["L0_attn_rpb_table"]).T,
        "w_gate": np.asarray(inputs["L0_ffn_wr"]).reshape(C),
        "b_gate": inputs["L0_ffn_br"],
        "w_up": inputs["L0_ffn_w1"],
        "b_up": inputs["L0_ffn_b1"],
        "w_down": inputs["L0_ffn_w2"],
        "b_down": inputs["L0_ffn_b2"],
    }
    nc = bacc.Bacc("TRN2", target_bir_lowering=False, num_devices=1)
    d = Dram()
    launch = {}
    for name, a in arrays.items():
        a = np.ascontiguousarray(a)
        launch[f"in_{name}"] = a
        ap = nc.dram_tensor(f"in_{name}", a.shape, mb.dt.from_np(a.dtype), kind="ExternalInput").ap()
        d.__dict__[name] = ap
    d.out = nc.dram_tensor("out", (CHUNKS, CH, C), F32, kind="ExternalOutput").ap()
    vit_tower(nc, d)
    r = run(nc, [launch], core_ids=[0])
    return r.results[0]["out"].reshape(B, N, C)
```
